# Optimizing a Trainium2 kernel written in Bass

```python
import numpy as np
import jax
import jax.numpy as jnp

def _softmax(x, axis=-1):
    return jax.nn.softmax(x, axis=axis)

def _gelu(x):
    return jax.nn.gelu(x, approximate=True)

def _silu(x):
    return jax.nn.silu(x)

def _sigmoid(x):
    return jax.nn.sigmoid(x)

def _layernorm(x, axis=-1, eps=1e-05):
    m = jnp.mean(x, axis=axis, keepdims=True)
    v = jnp.var(x, axis=axis, keepdims=True)
    return (x - m) / jnp.sqrt(v + eps)

def _scatter_add(tgt, idx, src, axis=0):
    return tgt.at[idx].add(src)

def _segment_sum(src, seg, n):
    return jax.ops.segment_sum(src, seg, n)
kernel_name = 'mk_recurrent_d1_jaxref_r4_d7a39b'

def setup_inputs(seed: int=0):
    np.random.seed(seed)
    _w = jnp.asarray

    def _L0_attn_setup():
        import jax, jax.numpy as jnp
        import numpy as np
        HIDDEN = 512
        NUM_V = 16
        NUM_K = 8
        HK = 128
        HV = 128
        KCONV = 4
        KEY_DIM = NUM_K * HK
        VALUE_DIM = NUM_V * HV
        CONV_DIM = 2 * KEY_DIM + VALUE_DIM
        R = NUM_V // NUM_K
        L2_EPS = 1e-06
        NORM_EPS = 1e-06
        key = jax.random.key(seed)
        ks = jax.random.split(key, 8)
        s = 0.02
        return {'hidden_states': jax.random.normal(ks[0], (1, 256, HIDDEN), jnp.float32), 'w_qkvz': jax.random.normal(ks[1], (2 * KEY_DIM + 2 * VALUE_DIM, HIDDEN), jnp.float32) * s, 'w_ba': jax.random.normal(ks[2], (2 * NUM_V, HIDDEN), jnp.float32) * s, 'conv_w': jax.random.normal(ks[3], (CONV_DIM, KCONV), jnp.float32) * s, 'dt_bias': jnp.ones((NUM_V,), jnp.float32), 'A_log': jnp.log(jax.random.uniform(ks[4], (NUM_V,), jnp.float32, 0.001, 16.0)), 'norm_weight': jnp.ones((HV,), jnp.float32), 'w_out': jax.random.normal(ks[5], (HIDDEN, VALUE_DIM), jnp.float32) * s}
    _L0_attn_in = _L0_attn_setup()

    def _L0_ffn_setup():
        import jax, jax.numpy as jnp
        import numpy as np
        B, T, D, FF = (4, 512, 512, 1408)
        EPS = 1e-06

        def rmsnorm(x, w):
            var = jnp.mean(jnp.square(x), axis=-1, keepdims=True)
            return x * jax.lax.rsqrt(var + EPS) * w
        key = jax.random.key(seed)
        ks = jax.random.split(key, 9)
        s = 0.02
        return {'hidden_states': jax.random.normal(ks[0], (B, T, D), jnp.float32), 'w_router': jax.random.normal(ks[1], (D,), jnp.float32) * s, 'b_router': jnp.zeros((), jnp.float32), 'norm1_w': jnp.ones((D,), jnp.float32), 'wv': jax.random.normal(ks[2], (D, D), jnp.float32) * s, 'bv': jnp.zeros((D,), jnp.float32), 'wo': jax.random.normal(ks[3], (D, D), jnp.float32) * s, 'norm2_w': jnp.ones((D,), jnp.float32), 'w_gate': jax.random.normal(ks[4], (D, FF), jnp.float32) * s, 'w_up': jax.random.normal(ks[5], (D, FF), jnp.float32) * s, 'w_down': jax.random.normal(ks[6], (FF, D), jnp.float32) * s}
    _L0_ffn_in = _L0_ffn_setup()
    _d = {'L0_attn_hidden_states': _L0_attn_in['hidden_states'], 'L0_attn_w_qkvz': _L0_attn_in['w_qkvz'], 'L0_attn_w_ba': _L0_attn_in['w_ba'], 'L0_attn_conv_w': _L0_attn_in['conv_w'], 'L0_attn_dt_bias': _L0_attn_in['dt_bias'], 'L0_attn_A_log': _L0_attn_in['A_log'], 'L0_attn_norm_weight': _L0_attn_in['norm_weight'], 'L0_attn_w_out': _L0_attn_in['w_out'], 'L0_ffn_w_router': _L0_ffn_in['w_router'], 'L0_ffn_b_router': _L0_ffn_in['b_router'], 'L0_ffn_norm1_w': _L0_ffn_in['norm1_w'], 'L0_ffn_wv': _L0_ffn_in['wv'], 'L0_ffn_bv': _L0_ffn_in['bv'], 'L0_ffn_wo': _L0_ffn_in['wo'], 'L0_ffn_norm2_w': _L0_ffn_in['norm2_w'], 'L0_ffn_w_gate': _L0_ffn_in['w_gate'], 'L0_ffn_w_up': _L0_ffn_in['w_up'], 'L0_ffn_w_down': _L0_ffn_in['w_down']}
    _x0 = _d['L0_attn_hidden_states']
    _d['L0_attn_hidden_states'] = jax.random.normal(jax.random.fold_in(jax.random.key(seed), 1), (4, 1024, 512), dtype=_x0.dtype)
    del _x0
    return _d

def reference(L0_attn_hidden_states, L0_attn_w_qkvz, L0_attn_w_ba, L0_attn_conv_w, L0_attn_dt_bias, L0_attn_A_log, L0_attn_norm_weight, L0_attn_w_out, L0_ffn_w_router, L0_ffn_b_router, L0_ffn_norm1_w, L0_ffn_wv, L0_ffn_bv, L0_ffn_wo, L0_ffn_norm2_w, L0_ffn_w_gate, L0_ffn_w_up, L0_ffn_w_down):

    def _L0_attn_ref(hidden_states, w_qkvz, w_ba, conv_w, dt_bias, A_log, norm_weight, w_out):
        import jax, jax.numpy as jnp
        import numpy as np
        HIDDEN = 512
        NUM_V = 16
        NUM_K = 8
        HK = 128
        HV = 128
        KCONV = 4
        KEY_DIM = NUM_K * HK
        VALUE_DIM = NUM_V * HV
        CONV_DIM = 2 * KEY_DIM + VALUE_DIM
        R = NUM_V // NUM_K
        L2_EPS = 1e-06
        NORM_EPS = 1e-06
        B, T, _ = hidden_states.shape
        qkvz = hidden_states @ w_qkvz.T
        ba = hidden_states @ w_ba.T
        qkvz = qkvz.reshape(B, T, NUM_K, 2 * HK + 2 * R * HV)
        q, k, v, z = jnp.split(qkvz, [HK, 2 * HK, 2 * HK + R * HV], axis=3)
        v = v.reshape(B, T, NUM_V, HV)
        z = z.reshape(B, T, NUM_V, HV)
        ba = ba.reshape(B, T, NUM_K, 2 * R)
        b = ba[..., :R].reshape(B, T, NUM_V)
        a = ba[..., R:].reshape(B, T, NUM_V)
        mixed = jnp.concatenate([q.reshape(B, T, KEY_DIM), k.reshape(B, T, KEY_DIM), v.reshape(B, T, VALUE_DIM)], axis=-1)
        xc = mixed.transpose(0, 2, 1)
        yc = jax.lax.conv_general_dilated(xc, conv_w[:, None, :], (1,), [(KCONV - 1, 0)], feature_group_count=CONV_DIM, dimension_numbers=('NCH', 'OIH', 'NCH'))
        yc = jax.nn.silu(yc).transpose(0, 2, 1)
        q, k, v = jnp.split(yc, [KEY_DIM, 2 * KEY_DIM], axis=-1)
        q = q.reshape(B, T, NUM_K, HK)
        k = k.reshape(B, T, NUM_K, HK)
        v = v.reshape(B, T, NUM_V, HV)
        beta = jax.nn.sigmoid(b)
        g = -jnp.exp(A_log) * jax.nn.softplus(a + dt_bias)
        q = jnp.repeat(q, R, axis=2)
        k = jnp.repeat(k, R, axis=2)
        q = q * jax.lax.rsqrt(jnp.sum(q * q, -1, keepdims=True) + L2_EPS)
        k = k * jax.lax.rsqrt(jnp.sum(k * k, -1, keepdims=True) + L2_EPS)
        scale = HK ** (-0.5)

        def step(S, xs):
            qt, kt, vt, gt, bt = xs
            S = S * jnp.exp(gt)[..., None, None]
            kv = jnp.einsum('bhk,bhkv->bhv', kt, S)
            delta = (vt - kv) * bt[..., None]
            S = S + jnp.einsum('bhk,bhv->bhkv', kt, delta)
            o = jnp.einsum('bhk,bhkv->bhv', qt * scale, S)
            return (S, o)
        S0 = jnp.zeros((B, NUM_V, HK, HV), hidden_states.dtype)
        xs = (q.transpose(1, 0, 2, 3), k.transpose(1, 0, 2, 3), v.transpose(1, 0, 2, 3), g.transpose(1, 0, 2), beta.transpose(1, 0, 2))
        _, o = jax.lax.scan(step, S0, xs)
        o = o.transpose(1, 0, 2, 3)
        xf = o.astype(jnp.float32) * jax.nn.silu(z.astype(jnp.float32))
        var = jnp.mean(xf * xf, -1, keepdims=True)
        xn = xf * jax.lax.rsqrt(var + NORM_EPS) * norm_weight
        return xn.reshape(B, T, VALUE_DIM) @ w_out.T

    def _L0_ffn_ref(hidden_states, w_router, b_router, norm1_w, wv, bv, wo, norm2_w, w_gate, w_up, w_down):
        import jax, jax.numpy as jnp
        import numpy as np
        B, T, D, FF = (4, 512, 512, 1408)
        EPS = 1e-06

        def rmsnorm(x, w):
            var = jnp.mean(jnp.square(x), axis=-1, keepdims=True)
            return x * jax.lax.rsqrt(var + EPS) * w
        x = hidden_states
        scores = jnp.einsum('btd,d->bt', x, w_router) + b_router
        routed = jax.nn.sigmoid(scores) > 0.5
        h1 = rmsnorm(x, norm1_w)
        v = jnp.einsum('btd,de->bte', h1, wv) + bv
        attn = jnp.einsum('bte,ed->btd', v, wo)
        h = x + attn
        h2 = rmsnorm(h, norm2_w)
        mlp = jnp.einsum('btf,fd->btd', jax.nn.silu(h2 @ w_gate) * (h2 @ w_up), w_down)
        processed = h + mlp
        return jnp.where(routed[..., None], processed, x)
    x = L0_attn_hidden_states
    xn = _layernorm(x, axis=-1)
    s = _L0_attn_ref(xn, L0_attn_w_qkvz, L0_attn_w_ba, L0_attn_conv_w, L0_attn_dt_bias, L0_attn_A_log, L0_attn_norm_weight, L0_attn_w_out)
    g = _silu(_L0_ffn_ref(xn, L0_ffn_w_router, L0_ffn_b_router, L0_ffn_norm1_w, L0_ffn_wv, L0_ffn_bv, L0_ffn_wo, L0_ffn_norm2_w, L0_ffn_w_gate, L0_ffn_w_up, L0_ffn_w_down))
    x = x + s * g
    return x

_drawn_inputs = setup_inputs


def setup_inputs(seed=0):
    import zlib

    import numpy as np

    out = dict(_drawn_inputs(seed))
    spreads = {'L0_attn_dt_bias': (1.0, 0.6),
     'L0_attn_norm_weight': (1.0, 0.6),
     'L0_ffn_norm1_w': (1.0, 0.6),
     'L0_ffn_bv': (0.0, 0.8),
     'L0_ffn_norm2_w': (1.0, 0.6)}
    factors = {'L0_attn_w_qkvz': 8.0,
     'L0_attn_w_ba': 8.0,
     'L0_attn_conv_w': 8.0,
     'L0_attn_A_log': 8.0,
     'L0_attn_w_out': 8.0,
     'L0_ffn_w_router': 8.0,
     'L0_ffn_wv': 8.0,
     'L0_ffn_wo': 8.0,
     'L0_ffn_w_gate': 8.0,
     'L0_ffn_w_up': 8.0,
     'L0_ffn_w_down': 8.0}
    for name, (base, spread) in spreads.items():
        noise = np.random.default_rng([zlib.crc32(name.encode()), seed]).standard_normal(out[name].shape)
        drawn = base * np.exp(spread * noise) if base else spread * noise
        out[name] = jnp.asarray(drawn.astype(out[name].dtype))
    for name, factor in factors.items():
        out[name] = (out[name] * factor).astype(out[name].dtype)
    return out
```

```python
from contextlib import ExitStack

import numpy as np

import concourse.bass as bass
from concourse import mybir

ALU = mybir.AluOpType
ACT = mybir.ActivationFunctionType
F32 = mybir.dt.float32

P = 128
BATCH, T, D = 4, 1024, 512
KT = D // P
FF = 1408
FT = FF // P
NUM_K, NUM_V, TAPS = 8, 16, 4
REP = NUM_V // NUM_K
GROUPS = 2
GK, GV = NUM_K // GROUPS, NUM_V // GROUPS
ROWS_K = 2 * P + 2 * REP * P
GROWS = GK * ROWS_K
HALO = TAPS - 1
PADT = T + HALO
TILE = 256
CPT = TILE // P
WIN = TILE + HALO
FTILE = 512
HEADS = 4
KPB = HEADS // REP
NB = GV // HEADS
BODY_TILES = 2
BODY_CHUNKS = BODY_TILES * CPT
UNITS = BODY_CHUNKS * NB
LEVELS = 7
LN_EPS = 1e-5
RMS_EPS = 1e-6
L2_EPS = 1e-6
SCALE = float(P) ** -0.5

C_ID, C_GT, C_ONE, C_LT, C_LE, C_M0T, C_M = 0, 1, 2, 3, 5, 7, 8
N_CONST = C_M + LEVELS


def constants():
    r = np.arange(P)
    c = np.zeros((P, N_CONST, P), np.float32)
    c[:, C_ID] = np.eye(P)
    c[:, C_GT] = r[:, None] > r[None, :]
    for i in range(KPB):
        c[:, C_LT + i] = r[:, None] < r[None, :]
        c[:, C_LE + i] = r[:, None] <= r[None, :]
    c[:, C_ONE] = 1.0
    for lv in range(LEVELS):
        s = 1 << lv
        a, b = r[:, None] // s, r[None, :] // s
        off = (a // 2 == b // 2) & (a % 2 == 1) & (b % 2 == 0)
        c[:, C_M + lv] = np.eye(P) - off
    c[:, C_M0T] = c[:, C_M].T
    return c


def feed_forward(nc, bank, x, cst, w_router, b_router, norm1_w, wv, bv, wo, norm2_w, w_gate, w_up, w_down, xt_d, g_d, part_d):
    with ExitStack() as ctx:
        def sb(name, shape):
            return ctx.enter_context(nc.sbuf_tensor(name, shape, F32))

        def sem(name):
            return ctx.enter_context(nc.semaphore(name))

        NJ = FTILE // P
        ident = sb("f_ident", [P, P])
        ones = sb("f_ones", [P, P])
        wv_sb, wo_sb = sb("wv_sb", [P, KT, D]), sb("wo_sb", [P, KT, D])
        wg_sb, wu_sb = sb("wg_sb", [P, KT, FF]), sb("wu_sb", [P, KT, FF])
        wd_sb = sb("wd_sb", [P, FT, D])
        wr_sb, br_sb = sb("wr_sb", [P, D]), sb("br_sb", [P, 1])
        n1_sb, n2_sb, bv_sb = sb("n1_sb", [P, KT]), sb("n2_sb", [P, KT]), sb("bv_sb", [P, KT])
        eps_sb, mhalf = sb("eps_sb", [P, 1]), sb("mhalf", [P, FTILE])
        zero = sb("zero", [P, FTILE])
        xn = sb("xn", [P, NJ, D])
        junk, junk2 = sb("junk", [P, D]), sb("junk2", [P, D])
        stats, mv = sb("stats", [P, NJ, 6]), sb("mv", [P, NJ, 2])
        rstd, ssq, r1 = sb("rstd", [P, NJ]), sb("ssq", [P, NJ]), sb("r1", [P, NJ])
        score, routed, kept = sb("score", [P, NJ]), sb("routed", [P, NJ]), sb("kept", [P, NJ])
        h1 = sb("h1", [P, NJ, D])
        xt, h1t = sb("xt", [P, KT, FTILE]), sb("h1t", [P, KT, FTILE])
        vt, ht = sb("vt", [P, KT, FTILE]), sb("ht", [P, KT, FTILE])
        hsq = sb("hsq", [P, KT, FTILE])
        r2 = sb("r2", [P, FTILE])
        h2t = h1t
        gate = sb("gate", [P, 2, FTILE])
        hid = sb("hid", [P, FT, FTILE])
        sel, g_sb = sb("sel", [P, 2, D]), sb("g_sb", [P, 2, D])

        w_in, z_set, z_out = sem("w_in"), sem("z_set"), sem("z_out")
        names = ["x_in", "stat", "mvs", "var", "rst", "xnd", "sqd", "r1a", "r1d", "msk", "h1d", "tr", "xtd", "h1td",
                 "xt_out", "v_ps", "v_sb", "a_ps", "h_sb", "sq_sb", "ss_ps", "ms_sb", "r2_sb", "h2_sb", "g_ps", "u_ps", "g_act",
                 "hid_sb", "d_ps", "xk", "selw", "g_done", "g_out0", "g_out1"]
        s = {n: sem("f_" + n) for n in names}
        first, last = s[names[0]].num, s[names[-1]].num

        with nc.Block() as block:
            @block.sync
            def _(sp):
                kp = lambda a: a.rearrange("(k p) n -> p k n", p=P)
                loads = [(ident[:], cst[:, C_ID, :]), (ones[:], cst[:, C_ONE, :]), (wv_sb[:], kp(wv)), (wo_sb[:], kp(wo)), (wg_sb[:], kp(w_gate)), (wu_sb[:], kp(w_up)),
                         (wd_sb[:], kp(w_down)), (wr_sb[:], w_router.partition_broadcast(P)), (br_sb[:], b_router.partition_broadcast(P)),
                         (n1_sb[:], norm1_w), (n2_sb[:], norm2_w), (bv_sb[:], bv)]
                for dst, src in loads:
                    sp.dma_start(dst, src).then_inc(w_in, 16)
                sp.wait_ge(z_set, 1)
                n = 0
                for b in range(BATCH):
                    sp.dma_start(xt_d[:, :, b * PADT:b * PADT + HALO], zero[:, 0:KT * HALO].rearrange("p (k c) -> p k c", k=KT)).then_inc(z_out, 16)
                    n += 1
                for k in range(KT):
                    sp.dma_start(xt_d[:, k, BATCH * PADT:BATCH * PADT + WIN], zero[:, 0:WIN]).then_inc(z_out, 16)
                    n += 1
                for r in range(BATCH * T // P):
                    sp.dma_start(part_d[r * P:(r + 1) * P, :], zero[:]).then_inc(z_out, 16)
                    n += 1
                sp.wait_ge(z_out, 16 * n)
                sp.wait_ge(w_in, 16 * len(loads))

            @block.gpsimd
            def _(pool):
                pool.memset(zero[:], 0.0).then_inc(z_set, 1)
                pool.memset(eps_sb[:], RMS_EPS)
                pool.memset(mhalf[:], -0.5)

        with nc.Fori(0, BATCH) as b, nc.Fori(0, T // FTILE) as half:
            row = b * T + half * FTILE
            with nc.Block() as block:
                @block.sync
                def _(sp):
                    sp.dma_start(xn[:], x[bass.ds(row, FTILE), :].rearrange("(j p) d -> p j d", p=P)).then_inc(s["x_in"], 16)
                    sp.wait_ge(s["xtd"], NJ)
                    sp.dma_start(xt_d[:, :, bass.ds(b * PADT + HALO + half * FTILE, FTILE)], xt[:]).then_inc(s["xt_out"], 16)
                    for j in range(NJ):
                        sp.wait_ge(s["g_done"], j + 1)
                        sp.dma_start(g_d[bass.ds(row + j * P, P), :], g_sb[:, j % 2, :]).then_inc(s[f"g_out{j % 2}"], 16)
                    sp.wait_ge(s["xt_out"], 16)
                    for p in range(2):
                        sp.wait_ge(s[f"g_out{p}"], 8 * NJ)

                @block.gpsimd
                def _(pool):
                    pool.wait_ge(s["mvs"], NJ)
                    pool.tensor_scalar(rstd[:], mv[:, :, 1], LN_EPS, None, ALU.add).then_inc(s["var"], 1)
                    pool.wait_ge(s["var"], 1)
                    pool.tensor_tensor(rstd[:], rstd[:], mhalf[:, 0:NJ], ALU.pow).then_inc(s["rst"], 1)
                    pool.wait_ge(s["sqd"], NJ)
                    pool.tensor_scalar(r1[:], ssq[:], 1.0 / D, RMS_EPS, ALU.mult, ALU.add).then_inc(s["r1a"], 1)
                    pool.wait_ge(s["r1a"], 1)
                    pool.tensor_tensor(r1[:], r1[:], mhalf[:, 0:NJ], ALU.pow).then_inc(s["r1d"], 1)
                    pool.wait_ge(s["ms_sb"], 1)
                    pool.tensor_tensor(r2[:], r2[:], mhalf[:], ALU.pow).then_inc(s["r2_sb"], 1)

                @block.vector
                def _(dve):
                    dve.wait_ge(s["x_in"], 16)
                    for j in range(NJ):
                        dve.bn_stats(stats[:, j, :], xn[:, j, :]).then_inc(s["stat"], 1)
                    for j in range(NJ):
                        dve.wait_ge(s["stat"], j + 1)
                        dve.bn_aggr(mv[:, j, :], stats[:, j, :]).then_inc(s["mvs"], 1)
                    dve.wait_ge(s["rst"], 1)
                    for j in range(NJ):
                        dve.tensor_scalar(xn[:, j, :], xn[:, j, :], mv[:, j, 0:1], rstd[:, j:j + 1], ALU.subtract, ALU.mult).then_inc(s["xnd"], 1)
                    for j in range(NJ):
                        dve.wait_ge(s["xnd"], j + 1)
                        if j:
                            dve.wait_ge(s["sqd"], j)
                        dve.tensor_tensor_reduce(junk[:], xn[:, j, :], xn[:, j, :], 1.0, 0.0, ALU.mult, ALU.add, ssq[:, j:j + 1]).then_inc(s["sqd"], 1)
                        if j:
                            dve.wait_ge(s["msk"], j)
                        dve.tensor_tensor_reduce(junk2[:], xn[:, j, :], wr_sb[:], 1.0, 0.0, ALU.mult, ALU.add, score[:, j:j + 1]).then_inc(s["msk"], 1)
                    dve.wait_ge(s["msk"], NJ)
                    dve.tensor_scalar(routed[:], score[:], br_sb[:, 0:1], 0.0, ALU.add, ALU.is_gt).then_inc(s["msk"], 1)
                    dve.wait_ge(s["msk"], NJ + 1)
                    dve.tensor_scalar(kept[:], routed[:], -1.0, 1.0, ALU.mult, ALU.add).then_inc(s["msk"], 1)
                    dve.wait_ge(s["r1d"], 1)
                    for j in range(NJ):
                        dve.tensor_scalar(h1[:, j, :], xn[:, j, :], r1[:, j:j + 1], None, ALU.mult).then_inc(s["h1d"], 1)
                    for j in range(NJ):
                        dve.wait_ge(s["tr"], 2 * j + 2)
                        dve.tensor_tensor(h1t[:, :, j * P:(j + 1) * P], bank[1][:].rearrange("p (k c) -> p k c", k=KT),
                                          n1_sb[:].unsqueeze(2).broadcast_to([P, KT, P]), ALU.mult).then_inc(s["h1td"], 1)
                    dve.wait_ge(s["xtd"], NJ)
                    for k in range(KT):
                        dve.wait_ge(s["a_ps"], k + 1)
                        dve.tensor_tensor(ht[:, k, :], bank[k % 2][:], xt[:, k, :], ALU.add).then_inc(s["h_sb"], 1)
                    dve.wait_ge(s["r2_sb"], 1)
                    for k in range(KT):
                        dve.scalar_tensor_tensor(out=h2t[:, k, :], in0=ht[:, k, :], scalar=n2_sb[:, k:k + 1], in1=r2[:],
                                                 op0=ALU.mult, op1=ALU.mult).then_inc(s["h2_sb"], 1)
                    for f in range(FT):
                        dve.wait_ge(s["u_ps"], f + 1)
                        dve.wait_ge(s["g_act"], f + 1)
                        dve.tensor_tensor(hid[:, f, :], bank[4 + f % 2][:], gate[:, f % 2, :], ALU.mult).then_inc(s["hid_sb"], 1)
                    dve.wait_ge(s["msk"], NJ + 2)
                    for j in range(NJ):
                        if j >= 2:
                            dve.wait_ge(s["g_done"], j - 1)
                        dve.tensor_scalar(sel[:, j % 2, :], xn[:, j, :], kept[:, j:j + 1], None, ALU.mult).then_inc(s["xk"], 1)
                        dve.wait_ge(s["xk"], j + 1)
                        dve.wait_ge(s["d_ps"], j + 1)
                        dve.scalar_tensor_tensor(out=sel[:, j % 2, :], in0=bank[6 + j % 2][:], scalar=routed[:, j:j + 1], in1=sel[:, j % 2, :],
                                                 op0=ALU.mult, op1=ALU.add).then_inc(s["selw"], 1)

                @block.scalar
                def _(act):
                    for j in range(NJ):
                        act.wait_ge(s["tr"], 2 * j + 1)
                        act.activation(xt[:, :, j * P:(j + 1) * P], bank[0][:].rearrange("p (k c) -> p k c", k=KT), ACT.Copy).then_inc(s["xtd"], 1)
                    for e in range(KT):
                        act.wait_ge(s["v_ps"], e + 1)
                        act.activation(vt[:, e, :], bank[2 + e % 2][:], ACT.Identity, bias=bv_sb[:, e:e + 1]).then_inc(s["v_sb"], 1)
                    for k in range(KT):
                        act.wait_ge(s["h_sb"], k + 1)
                        act.activation(hsq[:, k, :], ht[:, k, :], ACT.Square).then_inc(s["sq_sb"], 1)
                    act.wait_ge(s["ss_ps"], 1)
                    act.activation(r2[:], bank[2][:], ACT.Identity, scale=1.0 / D, bias=eps_sb[:, 0:1]).then_inc(s["ms_sb"], 1)
                    for f in range(FT):
                        act.wait_ge(s["g_ps"], f + 1)
                        if f >= 2:
                            act.wait_ge(s["hid_sb"], f - 1)
                        act.activation(gate[:, f % 2, :], bank[2 + f % 2][:], ACT.Silu).then_inc(s["g_act"], 1)
                    for j in range(NJ):
                        act.wait_ge(s["selw"], j + 1)
                        if j >= 2:
                            act.wait_ge(s[f"g_out{j % 2}"], 16 * (j // 2))
                        act.activation(g_sb[:, j % 2, :], sel[:, j % 2, :], ACT.Silu).then_inc(s["g_done"], 1)

                @block.tensor
                def _(pe):
                    for j in range(NJ):
                        pe.wait_ge(s["xnd"], j + 1)
                        if j:
                            pe.wait_ge(s["xtd"], j)
                        for k in range(KT):
                            i = pe.transpose(bank[0][:, k * P:(k + 1) * P], xn[:, j, k * P:(k + 1) * P], ident[:])
                        i.then_inc(s["tr"], 1)
                        pe.wait_ge(s["h1d"], j + 1)
                        if j:
                            pe.wait_ge(s["h1td"], j)
                        for k in range(KT):
                            i = pe.transpose(bank[1][:, k * P:(k + 1) * P], h1[:, j, k * P:(k + 1) * P], ident[:])
                        i.then_inc(s["tr"], 1)
                    pe.wait_ge(s["h1td"], NJ)
                    for e in range(KT):
                        if e >= 2:
                            pe.wait_ge(s["v_sb"], e - 1)
                        for k in range(KT):
                            i = pe.matmul(bank[2 + e % 2][:], wv_sb[:, k, e * P:(e + 1) * P], h1t[:, k, :], start=(k == 0), stop=(k == KT - 1))
                        i.then_inc(s["v_ps"], 1)
                    pe.wait_ge(s["v_sb"], KT)
                    pe.wait_ge(s["xtd"], NJ)
                    for c in range(KT):
                        if c >= 2:
                            pe.wait_ge(s["h_sb"], c - 1)
                        for k in range(KT):
                            i = pe.matmul(bank[c % 2][:], wo_sb[:, k, c * P:(c + 1) * P], vt[:, k, :], start=(k == 0), stop=(k == KT - 1))
                        i.then_inc(s["a_ps"], 1)
                    for k in range(KT):
                        pe.wait_ge(s["sq_sb"], k + 1)
                        i = pe.matmul(bank[2][:], ones[:], hsq[:, k, :], start=(k == 0), stop=(k == KT - 1))
                    i.then_inc(s["ss_ps"], 1)
                    pe.wait_ge(s["ms_sb"], 1)
                    pe.wait_ge(s["h2_sb"], KT)
                    for f in range(FT):
                        if f >= 2:
                            pe.wait_ge(s["g_act"], f - 1)
                        for k in range(KT):
                            i = pe.matmul(bank[2 + f % 2][:], wg_sb[:, k, f * P:(f + 1) * P], h2t[:, k, :], start=(k == 0), stop=(k == KT - 1))
                        i.then_inc(s["g_ps"], 1)
                        if f >= 2:
                            pe.wait_ge(s["hid_sb"], f - 1)
                        for k in range(KT):
                            i = pe.matmul(bank[4 + f % 2][:], wu_sb[:, k, f * P:(f + 1) * P], h2t[:, k, :], start=(k == 0), stop=(k == KT - 1))
                        i.then_inc(s["u_ps"], 1)
                    for j in range(NJ):
                        if j >= 2:
                            pe.wait_ge(s["selw"], j - 1)
                        out = bank[6 + j % 2]
                        for k in range(KT):
                            pe.matmul(out[:, k * P:(k + 1) * P], ht[:, k, j * P:(j + 1) * P], ident[:], start=(k == 0), stop=False, skip_group_check=True)
                        for f in range(FT):
                            pe.wait_ge(s["hid_sb"], f + 1)
                            i = pe.matmul(out[:], hid[:, f, j * P:(j + 1) * P], wd_sb[:, f, :], start=False, stop=(f == FT - 1), skip_group_check=True)
                        i.then_inc(s["d_ps"], 1)

            nc.gpsimd.sem_clear(range(first, last + 1))
            nc.all_engine_barrier()


def merged(*lists):
    at = [((i + 0.5) / len(steps), n, step) for n, steps in enumerate(lists) for i, step in enumerate(steps)]
    return [step for _, _, step in sorted(at, key=lambda x: x[:2])]


def attention(nc, bank, x, cst, w_qkvz, w_ba, conv_w, dt_bias, a_log, norm_weight, w_out, xt_d, g_d, part_d, out):
    with ExitStack() as ctx:
        def sb(name, shape):
            return ctx.enter_context(nc.sbuf_tensor(name, shape, F32))

        def sem(name):
            return ctx.enter_context(nc.semaphore(name))

        con = sb("con", [P, N_CONST, P])
        ident, le, gt, ones = (con[:, i, :] for i in (C_ID, C_LE, C_GT, C_ONE))
        wt = sb("wt", [P, KT, GROWS])
        wba = sb("wba", [P, KT, 4 * GK])
        wot = sb("wot", [P, GV, D])
        taps = sb("taps", [P, 4 * GK, TAPS])
        dtb, neg_a = sb("dtb", [P, GV]), sb("neg_a", [P, GV])
        nw = sb("nw", [P, 1])
        mhalf = sb("mhalf2", [P, 16])
        xtile = sb("xtile", [P, KT, WIN])
        raw = sb("raw", [P, 2, WIN])
        kraw = sb("kraw", [P, GK, TILE])
        vraw = sb("vraw", [P, GV, TILE])
        sq = sb("sq", [P, GK, TILE])
        qt, kt = sb("qt", [P, 2, GK, TILE]), sb("kt", [P, 2, GK, TILE])
        ktok = sb("ktok", [P, 2, CPT, GK, P])
        vtok, zs = sb("vtok", [P, 2, CPT, GV, P]), sb("zs", [P, 2, CPT, GV, P])
        ba = sb("ba", [P, CPT, GK, 2, REP])
        beta, gdec = sb("beta", [P, 2, CPT, GV]), sb("gdec", [P, 2, CPT, GV])
        rn = sb("rn", [P, 2, CPT, 2 * GK])
        bneg, ypos, yneg, ratio, ratio2 = (sb(n, [P, CPT, GV]) for n in ("bneg", "ypos", "yneg", "ratio", "ratio2"))
        gex = sb("gex", [P, 2, 3, GV])
        ngam, gamq, bend = sb("ngam", [P, 2, GV]), sb("gamq", [P, 2, GV]), sb("bend", [P, 2, GV])
        xnt = sb("xnt", [P, GV, P])
        xrow, grow, prow = sb("xrow", [P, D]), sb("grow", [P, D]), sb("prow", [P, D])
        pout, yout = sb("pout", [P, 2, D]), sb("yout", [P, 2, D])
        gm, kqm, gam = sb("gm", [P, HEADS, P]), sb("kqm", [P, 2 * KPB, P]), sb("gam", [P, HEADS, P])
        ltm, pt = sb("ltm", [P, HEADS, P]), sb("pt", [P, 2, HEADS, P])
        xinv, yinv, winv = sb("xinv", [P, HEADS, P]), sb("yinv", [P, 2, HEADS, P]), sb("winv", [P, HEADS, P])
        kend = sb("kend", [P, 2, HEADS, P])
        reps, tq = sb("reps", [P, HEADS, P]), sb("tq", [P, HEADS, P])
        osq = sb("osq", [P, HEADS, P])
        state = sb("state", [P, GV, P])
        ssq, rms = sb("ssq2", [P, HEADS]), sb("rms", [P, HEADS])

        proj, b_tr, b_a, b_i0, b_i1, b_s0, b_s1 = bank[0:2], bank[2], bank[3], bank[4], bank[5], bank[6], bank[7]

        c_in, c_set = sem("c_in"), sem("c_set")
        names = [
            "wrow0_in", "wrow1_in", "wtr_ps", "wtr_sb", "small_in", "nega",
            "x_in", "pj_ps", "pj_sb", "cv1", "cv2", "cv3", "cv", "silu", "sq_sb", "ss_ps", "ss_sb", "rn_sb",
            "tr_ps", "ktok_sb", "kt_sb", "v_sb", "gt_sb", "gt_exp",
            "gc_ps", "gc_sb", "gs_sb", "rows_in", "out_ps", "po_sb", "yg_sb", "yo_sb", "stored0", "stored1",
            "gm_sb", "kq_ps", "kq_sb", "gam_ps", "gam_sb", "lt_sb", "lti_sb", "y1_sb", "pt_sb", "kend_sb",
            "w_ps", "w_sb", "x_ps", "x_sb", "y_ps", "y_sb",
            "ks_ps", "qs_ps", "r_sb", "t_sb", "e_ps", "e_sb", "su_ps", "s_sb", "o_ps", "o_sb", "xf_sb", "sn_sb", "rm1_sb", "rm_sb", "xn_sb",
            "xt_ps", "xt_sb",
        ]
        s = {n: sem("a_" + n) for n in names}
        first, last = s[names[0]].num, s[names[-1]].num

        def next_round():
            nc.gpsimd.sem_clear(range(first, last + 1))
            nc.all_engine_barrier()

        with nc.Block() as block:
            @block.sync
            def _(sp):
                sp.dma_start(con[:], cst).then_inc(c_in, 16)
                sp.dma_start(nw[:], norm_weight.rearrange("(p a) -> p a", a=1)).then_inc(c_in, 16)
                sp.wait_ge(c_in, 32)

            @block.vector
            def _(dve):
                dve.memset(mhalf[:], -0.5).then_inc(c_set, 1)
                dve.wait_ge(c_set, 1)

        def load_weights(g):
            stage = [xnt[:].rearrange("p h c -> p (h c)"), ktok[:].rearrange("p a b h c -> p (a b h c)")[:, 0:GV * P]]
            loads = [("in", r) for r in range(GROWS // P)] + [("out", r) for r in range(D // P)] + [("ba", 0)]
            steps = [(n, kind, r, part) for n, (kind, r) in enumerate(loads) for part in range(GV // 4 if kind == "out" else 1)]
            last_of = {n: i for i, (n, _, _, _) in enumerate(steps)}
            with nc.Block() as block:
                @block.sync
                def _(sp):
                    for n, (kind, r) in enumerate(loads):
                        if n >= 2:
                            sp.wait_ge(s["wtr_ps"], last_of[n - 2] + 1)
                        if kind == "in":
                            sp.dma_start(stage[n % 2][:, 0:D], w_qkvz[bass.ds(g * GROWS + r * P, P), :]).then_inc(s[f"wrow{n % 2}_in"], 16)
                        elif kind == "out":
                            sp.dma_start(stage[n % 2], w_out[r * P:(r + 1) * P, bass.ds(g * (GV * P), GV * P)]).then_inc(s[f"wrow{n % 2}_in"], 16)
                        else:
                            sp.dma_start(stage[n % 2][0:4 * GK, 0:D], w_ba[bass.ds(g * (4 * GK), 4 * GK), :]).then_inc(s[f"wrow{n % 2}_in"], 16)
                    spans = [(0, GK, NUM_K * P, GK * P), (GK, 2 * GK, 0, GK * P), (2 * GK, 4 * GK, 2 * NUM_K * P, GV * P)]
                    for lo, hi, base, width in spans:
                        sp.dma_start(taps[:, lo:hi, :], conv_w[bass.ds(g * width + base, width), :].rearrange("(h p) t -> p h t", p=P)).then_inc(s["small_in"], 16)
                    sp.dma_start(dtb[:], dt_bias[bass.ds(g * GV, GV)].partition_broadcast(P)).then_inc(s["small_in"], 16)
                    sp.dma_start(neg_a[:], a_log[bass.ds(g * GV, GV)].partition_broadcast(P)).then_inc(s["small_in"], 16)
                    sp.wait_ge(s["small_in"], 80)

                @block.tensor
                def _(pe):
                    for i, (n, kind, r, part) in enumerate(steps):
                        pe.wait_ge(s[f"wrow{n % 2}_in"], 16 * (n // 2 + 1))
                        if i >= 2:
                            pe.wait_ge(s["wtr_sb"], i - 1)
                        rows = 4 * GK if kind == "ba" else P
                        for k in range(4):
                            c = (part * 4 + k) * P
                            t = pe.transpose(proj[i % 2][:, k * P:k * P + rows], stage[n % 2][0:rows, c:c + P], ident[0:rows, 0:rows])
                        t.then_inc(s["wtr_ps"], 1)

                @block.vector
                def _(dve):
                    for i, (n, kind, r, part) in enumerate(steps):
                        dve.wait_ge(s["wtr_ps"], i + 1)
                        src = proj[i % 2][:].rearrange("p (k c) -> p k c", k=4)
                        if kind == "in":
                            dve.tensor_copy(wt[:, :, r * P:(r + 1) * P], src).then_inc(s["wtr_sb"], 1)
                        elif kind == "out":
                            dve.tensor_copy(wot[:, part * 4:part * 4 + 4, r * P:(r + 1) * P], src).then_inc(s["wtr_sb"], 1)
                        else:
                            dve.tensor_copy(wba[:], src[:, :, 0:4 * GK]).then_inc(s["wtr_sb"], 1)
                    dve.wait_ge(s["nega"], 1)
                    dve.tensor_scalar(neg_a[:], neg_a[:], -1.0, None, ALU.mult).then_inc(s["nega"], 1)

                @block.scalar
                def _(act):
                    act.wait_ge(s["small_in"], 80)
                    act.activation(neg_a[:], neg_a[:], ACT.Exp).then_inc(s["nega"], 1)
            next_round()

        feats = [("k", h) for h in range(GK)] + [("q", h) for h in range(GK)] + [("v", h) for h in range(GV)]
        prods = feats + [("z", i) for i in range(CPT * NB)] + [("ba", cc) for cc in range(CPT)]
        NP, NF = len(prods), len(feats)
        N_TR = 2 * CPT + CPT * NB
        N_SILU = 4
        SERIES = 9
        N_GATE = SERIES + 12
        UPT = CPT * NB

        def feature(par, kind, h):
            if kind == "k":
                return kraw[:, h, :]
            return qt[:, par, h, :] if kind == "q" else vraw[:, h, :]

        def pe_product(pe, q, i):
            kind, h = prods[i]
            n = q * NP + i
            if i == 0:
                pe.wait_ge(s["x_in"], 16 * (q + 1))
            if n >= 2:
                pe.wait_ge(s["pj_sb"], n - 1)
            for k in range(KT):
                st = dict(start=(k == 0), stop=(k == KT - 1))
                if kind in "kqv":
                    c = {"q": h * ROWS_K, "k": h * ROWS_K + P, "v": h // REP * ROWS_K + 2 * P + h % REP * P}[kind]
                    j = pe.matmul(proj[n % 2][:, 0:WIN], wt[:, k, c:c + P], xtile[:, k, :], **st)
                elif kind == "z":
                    cc, m = divmod(h, NB)
                    w = wt[:, k, :].rearrange("p (h c) -> p h c", h=GK)[:, m * KPB:(m + 1) * KPB, 2 * P + REP * P:ROWS_K]
                    j = pe.matmul(proj[n % 2][:], xtile[:, k, HALO + cc * P:HALO + (cc + 1) * P], w, **st)
                else:
                    j = pe.matmul(proj[n % 2][:, 0:4 * GK], xtile[:, k, HALO + h * P:HALO + (h + 1) * P], wba[:, k, :], **st)
            j.then_inc(s["pj_ps"], 1)

        def act_product(act, q, par, i):
            kind, h = prods[i]
            n = q * NP + i
            act.wait_ge(s["pj_ps"], n + 1)
            if kind in "kqv":
                if q * NF + i >= 2:
                    act.wait_ge(s["cv"], q * NF + i - 1)
                act.activation(raw[:, i % 2, :], proj[n % 2][:, 0:WIN], ACT.Copy).then_inc(s["pj_sb"], 1)
            elif kind == "z":
                cc, m = divmod(h, NB)
                if q:
                    act.wait_ge(s["xf_sb"], q * UPT)
                act.activation(zs[:, par, cc, m * HEADS:(m + 1) * HEADS, :], proj[n % 2][:].rearrange("p (h c) -> p h c", h=HEADS), ACT.Silu).then_inc(s["pj_sb"], 1)
            else:
                act.activation(ba[:, h].rearrange("p k s r -> p (k s r)"), proj[n % 2][:, 0:4 * GK], ACT.Copy).then_inc(s["pj_sb"], 1)

        def dve_conv(dve, q, par, i):
            kind, h = feats[i]
            n = q * NF + i
            if q and h == 0:
                if kind == "k":
                    dve.wait_ge(s["sq_sb"], 2 * q - 1)
                    dve.wait_ge(s["tr_ps"], (q - 1) * N_TR + 2 * CPT)
                elif kind == "q":
                    dve.wait_ge(s["qs_ps"], q * UPT)
                    dve.wait_ge(s["kq_ps"], q * UPT)
                else:
                    dve.wait_ge(s["tr_ps"], q * N_TR)
            dve.wait_ge(s["pj_sb"], q * NP + i + 1)
            acc, src = feature(par, kind, h), raw[:, i % 2, :]
            dve.tensor_scalar(acc, src[:, 0:TILE], taps[:, i, 0:1], None, ALU.mult).then_inc(s["cv1"], 1)
            for t, (before, done) in enumerate([("cv1", "cv2"), ("cv2", "cv3"), ("cv3", "cv")], start=1):
                dve.wait_ge(s[before], n + 1)
                dve.scalar_tensor_tensor(out=acc, in0=src[:, t:t + TILE], scalar=taps[:, i, t:t + 1], in1=acc, op0=ALU.mult, op1=ALU.add).then_inc(s[done], 1)

        def act_silu(act, q, par):
            for a, upto in ((kraw[:], GK), (qt[:, par], 2 * GK), (vraw[:, 0:HEADS], 2 * GK + HEADS), (vraw[:, HEADS:GV], NF)):
                act.wait_ge(s["cv"], q * NF + upto)
                act.activation(a, a, ACT.Silu).then_inc(s["silu"], 1)

        def pool_squares(pool, q, par, j):
            pool.wait_ge(s["silu"], q * N_SILU + j + 1)
            if q or j:
                pool.wait_ge(s["ss_ps"], 2 * q + j)
            a = qt[:, par] if j else kraw[:]
            pool.tensor_tensor(sq[:], a, a, ALU.mult).then_inc(s["sq_sb"], 1)

        def pe_squares(pe, q, j):
            pe.wait_ge(s["sq_sb"], 2 * q + j + 1)
            if j:
                pe.wait_ge(s["ss_sb"], 2 * q + j)
            elif q:
                pe.wait_ge(s["v_sb"], q * UPT)
            for cc in range(CPT):
                for h in range(GK):
                    m = pe.matmul(b_tr[:, cc * GK + h:cc * GK + h + 1], sq[:, h, cc * P:(cc + 1) * P], ones[:, 0:1], start=True, stop=True)
            m.then_inc(s["ss_ps"], 1)

        def dve_squares(dve, q, par, j):
            dve.wait_ge(s["ss_ps"], 2 * q + j + 1)
            dve.tensor_scalar(rn[:, par, :, j * GK:(j + 1) * GK], b_tr[:, 0:CPT * GK].rearrange("p (c h) -> p c h", c=CPT), L2_EPS, None, ALU.add).then_inc(s["ss_sb"], 1)

        def pool_norms(pool, q, par, j):
            pool.wait_ge(s["ss_sb"], 2 * q + j + 1)
            r = rn[:, par, :, j * GK:(j + 1) * GK]
            pool.tensor_tensor(r, r, mhalf[:, 0:CPT * GK].rearrange("p (c h) -> p c h", c=CPT), ALU.pow).then_inc(s["rn_sb"], 1)

        def dve_qscale(dve, q, par):
            dve.wait_ge(s["rn_sb"], 3 * q + 2)
            r = rn[:, par, :, GK:2 * GK]
            dve.tensor_scalar(r, r, SCALE, None, ALU.mult).then_inc(s["rn_sb"], 1)

        def pe_keys(pe, q, par, cc):
            pe.wait_ge(s["silu"], q * N_SILU + 1)
            pe.wait_ge(s["ss_sb"], 2 * q + 2)
            if cc:
                pe.wait_ge(s["kt_sb"], q * CPT + cc)
            for h in range(GK):
                t = pe.transpose(b_tr[:, h * P:(h + 1) * P], kraw[:, h, cc * P:(cc + 1) * P], ident)
            t.then_inc(s["tr_ps"], 1)
            pe.wait_ge(s["ktok_sb"], q * CPT + cc + 1)
            for h in range(GK):
                t = pe.transpose(b_tr[:, h * P:(h + 1) * P], ktok[:, par, cc, h, :], ident)
            t.then_inc(s["tr_ps"], 1)

        def dve_keys(dve, q, par, cc):
            dve.wait_ge(s["tr_ps"], q * N_TR + 2 * cc + 1)
            dve.wait_ge(s["rn_sb"], 3 * q + 1)
            if q:
                dve.wait_ge(s["kend_sb"], q * UPT)
            dve.tensor_tensor(ktok[:, par, cc], b_tr[:].rearrange("p (h c) -> p h c", h=GK),
                              rn[:, par, cc, 0:GK].unsqueeze(2).broadcast_to([P, GK, P]), ALU.mult).then_inc(s["ktok_sb"], 1)

        def act_keys(act, q, par, cc):
            act.wait_ge(s["tr_ps"], q * N_TR + 2 * cc + 2)
            if q:
                act.wait_ge(s["qs_ps"], q * UPT)
            act.activation(kt[:, par, :, cc * P:(cc + 1) * P], b_tr[:].rearrange("p (h c) -> p h c", h=GK), ACT.Copy).then_inc(s["kt_sb"], 1)

        def pe_values(pe, q, m, cc):
            pe.wait_ge(s["silu"], q * N_SILU + 3 + m)
            if m == 0 and cc == 0:
                pe.wait_ge(s["kt_sb"], (q + 1) * CPT)
            else:
                pe.wait_ge(s["v_sb"], q * UPT + m * CPT + cc)
            for h in range(HEADS):
                t = pe.transpose(b_tr[:, h * P:(h + 1) * P], vraw[:, m * HEADS + h, cc * P:(cc + 1) * P], ident)
            t.then_inc(s["tr_ps"], 1)

        def act_values(act, q, par, m, cc):
            act.wait_ge(s["tr_ps"], q * N_TR + 2 * CPT + m * CPT + cc + 1)
            if q:
                act.wait_ge(s["r_sb"], q * UPT)
            act.activation(vtok[:, par, cc, m * HEADS:(m + 1) * HEADS, :], b_tr[:].rearrange("p (h c) -> p h c", h=HEADS), ACT.Copy).then_inc(s["v_sb"], 1)

        def act_gates(act, q):
            act.wait_ge(s["gt_sb"], q * N_GATE + 3)
            act.activation(bneg[:], bneg[:], ACT.Exp).then_inc(s["gt_exp"], 1)
            act.activation(yneg[:], yneg[:], ACT.Exp).then_inc(s["gt_exp"], 1)

        def dve_gates(dve, q, par, part):
            done = [q * N_GATE + (3 if part else 0)]

            def link(ins):
                ins.then_inc(s["gt_sb"], 1)
                done[0] += 1
                dve.wait_ge(s["gt_sb"], done[0])

            by_key = lambda a: a.rearrange("p c (k r) -> p c k r", r=REP)
            per_head = lambda a: a.unsqueeze(1).broadcast_to([P, CPT, GV])
            if part == 0:
                dve.wait_ge(s["pj_sb"], (q + 1) * NP)
                link(dve.tensor_scalar(by_key(bneg[:]), ba[:, :, :, 0, :], -1.0, 85.0, ALU.mult, ALU.min))
                for r in range(CPT):
                    ins = dve.tensor_tensor(ypos[:, r, :].rearrange("p (k r) -> p k r", r=REP), ba[:, r, :, 1, :], dtb[:].rearrange("p (k r) -> p k r", r=REP), ALU.add)
                link(ins)
                link(dve.scalar_tensor_tensor(out=yneg[:], in0=ypos[:], scalar=-1.0, in1=ypos[:], op0=ALU.mult, op1=ALU.min))
                return
            bt, gd = beta[:, par], gdec[:, par]
            if q:
                dve.wait_ge(s["gm_sb"], q * UPT)
                dve.wait_ge(s["gc_ps"], q * CPT)
            dve.wait_ge(s["gt_exp"], 2 * q + 2)
            link(dve.tensor_scalar(bneg[:], bneg[:], 1.0, None, ALU.add))
            link(dve.reciprocal(bt, bneg[:]))
            link(dve.tensor_scalar(ratio[:], yneg[:], 2.0, None, ALU.add))
            link(dve.reciprocal(ratio[:], ratio[:]))
            link(dve.tensor_tensor(ratio[:], ratio[:], yneg[:], ALU.mult))
            link(dve.tensor_tensor(ratio2[:], ratio[:], ratio[:], ALU.mult))
            link(dve.tensor_scalar(gd, ratio2[:], 1.0 / (2 * SERIES - 1), None, ALU.mult))
            for i in range(SERIES - 2, 0, -1):
                link(dve.scalar_tensor_tensor(out=gd, in0=gd, scalar=1.0 / (2 * i + 1), in1=ratio2[:], op0=ALU.add, op1=ALU.mult))
            link(dve.scalar_tensor_tensor(out=gd, in0=gd, scalar=1.0, in1=ratio[:], op0=ALU.add, op1=ALU.mult))
            link(dve.tensor_scalar(ypos[:], ypos[:], 0.0, None, ALU.max))
            link(dve.scalar_tensor_tensor(out=gd, in0=gd, scalar=2.0, in1=ypos[:], op0=ALU.mult, op1=ALU.add))
            link(dve.tensor_tensor(gd, gd, per_head(neg_a[:]), ALU.mult))
            assert done[0] == (q + 1) * N_GATE

        first_steps = [("product", i) for i in range(NF)]
        z_steps = [("product", i) for i in range(NF, NP)]
        last_steps = ([("silu",)] + z_steps + [("squares", 0), ("gates", 0), ("squares", 1), ("gates", 1)] + [("keys", cc) for cc in range(CPT)]
                      + [("values", m, cc) for m in range(NB) for cc in range(CPT)])
        tile_steps = first_steps + last_steps

        def pe_tile(pe, q, par, step):
            kind, *i = step
            if kind == "product":
                pe_product(pe, q, *i)
            elif kind == "squares":
                pe_squares(pe, q, *i)
            elif kind == "keys":
                pe_keys(pe, q, par, *i)
            elif kind == "values":
                pe_values(pe, q, *i)

        def act_tile(act, q, par, step):
            kind, *i = step
            if kind == "product":
                act_product(act, q, par, *i)
            elif kind == "silu":
                act_silu(act, q, par)
            elif kind == "gates" and i[0] == 0:
                act_gates(act, q)
            elif kind == "keys":
                act_keys(act, q, par, *i)
            elif kind == "values":
                act_values(act, q, par, *i)

        def dve_tile(dve, q, par, step):
            kind, *i = step
            if kind == "product" and i[0] < NF:
                dve_conv(dve, q, par, *i)
            elif kind == "squares":
                dve_squares(dve, q, par, *i)
                if i[0]:
                    dve_qscale(dve, q, par)
            elif kind == "gates":
                dve_gates(dve, q, par, *i)
            elif kind == "keys":
                dve_keys(dve, q, par, *i)

        def pool_tile(pool, q, par, step):
            kind, *i = step
            if kind == "squares":
                pool_squares(pool, q, par, *i)
                pool_norms(pool, q, par, *i)

        def load_tile(sp, q, column):
            if q:
                sp.wait_ge(s["pj_ps"], q * NP)
            sp.dma_start(xtile[:], xt_d[:, :, bass.ds(column, WIN)]).then_inc(s["x_in"], 16)

        def where(n):
            c, m = divmod(n, NB)
            return c, m, c // CPT, c % CPT

        def unit_heads(m):
            return slice(m * HEADS, (m + 1) * HEADS)

        quad = lambda b: b[:].rearrange("p (h c) -> p h c", h=HEADS)
        N_W, N_X, N_Y = LEVELS, LEVELS - 2, LEVELS - 1

        def pe_gate(pe, c):
            par, cc = divmod(c, CPT)
            if c:
                pe.wait_ge(s["gam_sb"], NB * c)
            if par:
                pe.wait_ge(s["gt_sb"], par * N_GATE)
            for i, a in enumerate((le, gt, ones)):
                j = pe.matmul(b_a[:, i * GV:(i + 1) * GV], a, gdec[:, par, cc, :], start=True, stop=True)
            j.then_inc(s["gc_ps"], 1)

        def act_gate(act, c):
            act.wait_ge(s["gc_ps"], c + 1)
            if c >= 2:
                act.wait_ge(s["s_sb"], NB * (c - 1))
                act.wait_ge(s["gs_sb"], 3 * (c - 1))
            act.activation(gex[:, c % 2].rearrange("p a h -> p (a h)"), b_a[:, 0:3 * GV], ACT.Exp).then_inc(s["gc_sb"], 1)

        def dve_gate(dve, c):
            par, cc = divmod(c, CPT)
            dve.wait_ge(s["gc_sb"], c + 1)
            if par:
                dve.wait_ge(s["rn_sb"], 3 * par)
            if c >= 2:
                dve.wait_ge(s["t_sb"], NB * (c - 1))
                dve.wait_ge(s["kend_sb"], NB * (c - 1))
                dve.wait_ge(s["r_sb"], NB * (c - 1))
            p = c % 2
            dve.tensor_scalar(ngam[:, p], gex[:, p, 0], -1.0, None, ALU.mult).then_inc(s["gs_sb"], 1)
            dve.tensor_tensor(gamq[:, p].rearrange("p (k r) -> p k r", r=REP), gex[:, p, 0].rearrange("p (k r) -> p k r", r=REP),
                              rn[:, par, cc, GK:2 * GK].unsqueeze(2).broadcast_to([P, GK, REP]), ALU.mult).then_inc(s["gs_sb"], 1)
            dve.tensor_tensor(bend[:, p], gex[:, p, 1], beta[:, par, cc], ALU.mult).then_inc(s["gs_sb"], 1)

        def pool_decay(pool, n):
            c, m, par, cc = where(n)
            if n:
                pool.wait_ge(s["gam_ps"], n)
            if par:
                pool.wait_ge(s["gt_sb"], par * N_GATE)
            pool.tensor_tensor(gm[:], le.unsqueeze(1).broadcast_to([P, HEADS, P]),
                               gdec[:, par, cc, unit_heads(m)].unsqueeze(2).broadcast_to([P, HEADS, P]), ALU.mult).then_inc(s["gm_sb"], 1)

        def pe_scores(pe, n):
            c, m, par, cc = where(n)
            if m == 0:
                pe.wait_ge(s["gc_sb"], c + 1)
            else:
                pe.wait_ge(s["gam_sb"], n)
            if par:
                pe.wait_ge(s["kt_sb"], par * CPT)
                pe.wait_ge(s["silu"], (par - 1) * N_SILU + 2)
            t = slice(cc * P, (cc + 1) * P)
            for j in range(KPB):
                h = m * KPB + j
                pe.matmul(b_a[:, j * P:(j + 1) * P], kt[:, par, h, t], kt[:, par, h, t], start=True, stop=True)
                i = pe.matmul(b_a[:, (KPB + j) * P:(KPB + j + 1) * P], kt[:, par, h, t], qt[:, par, h, t], start=True, stop=True)
            i.then_inc(s["kq_ps"], 1)

        def dve_scores(dve, n):
            dve.wait_ge(s["kq_ps"], n + 1)
            if n:
                dve.wait_ge(s["lt_sb"], n)
                dve.wait_ge(s["pt_sb"], n)
            dve.tensor_tensor(kqm[:], b_a[:].rearrange("p (h c) -> p h c", h=2 * KPB), con[:, C_LT:C_LT + 2 * KPB, :], ALU.mult).then_inc(s["kq_sb"], 1)

        def pe_decay(pe, n):
            pe.wait_ge(s["kq_sb"], n + 1)
            pe.wait_ge(s["gm_sb"], n + 1)
            pe.matmul(b_a[:], gt, gm[:].rearrange("p h c -> p (h c)"), start=True, stop=True).then_inc(s["gam_ps"], 1)

        def act_decay(act, n):
            act.wait_ge(s["gam_ps"], n + 1)
            if n:
                act.wait_ge(s["pt_sb"], n)
                act.wait_ge(s["lt_sb"], n)
            act.activation(gam[:], quad(b_a), ACT.Exp).then_inc(s["gam_sb"], 1)

        def dve_matrices(dve, n):
            c, m, par, cc = where(n)
            dve.wait_ge(s["gam_sb"], n + 1)
            dve.wait_ge(s["kq_sb"], n + 1)
            if n:
                dve.wait_ge(s["w_ps"], N_W * n)
                dve.wait_ge(s["y1_sb"], n)
            for h in range(HEADS):
                b = beta[:, par, cc, m * HEADS + h:m * HEADS + h + 1]
                i = dve.scalar_tensor_tensor(out=ltm[:, h], in0=gam[:, h], scalar=b, in1=kqm[:, h // REP], op0=ALU.mult, op1=ALU.mult)
            i.then_inc(s["lt_sb"], 1)
            if n >= 2:
                dve.wait_ge(s["o_ps"], n - 1)
            for h in range(HEADS):
                b = beta[:, par, cc, m * HEADS + h:m * HEADS + h + 1]
                i = dve.scalar_tensor_tensor(out=pt[:, n % 2, h], in0=gam[:, h], scalar=b, in1=kqm[:, KPB + h // REP], op0=ALU.mult, op1=ALU.mult)
            i.then_inc(s["pt_sb"], 1)

        def pool_matrices(pool, n):
            c, m, par, cc = where(n)
            pool.wait_ge(s["lt_sb"], n + 1)
            pool.tensor_tensor(ltm[:], ltm[:], ident.unsqueeze(1).broadcast_to([P, HEADS, P]), ALU.add).then_inc(s["lti_sb"], 1)
            pool.wait_ge(s["gs_sb"], 3 * (c + 1))
            if n >= 2:
                pool.wait_ge(s["su_ps"], n - 1)
            if par:
                pool.wait_ge(s["ktok_sb"], par * CPT)
            for r in range(KPB):
                h = m * HEADS + r * REP
                i = pool.tensor_tensor(kend[:, n % 2, r * REP:(r + 1) * REP], ktok[:, par, cc, m * KPB + r].unsqueeze(1).broadcast_to([P, REP, P]),
                                       bend[:, c % 2, h:h + REP].unsqueeze(2).broadcast_to([P, REP, P]), ALU.mult)
            i.then_inc(s["kend_sb"], 1)

        def pe_level(pe, n, lv):
            if lv == 0:
                pe.wait_ge(s["lti_sb"], n + 1)
                if n:
                    pe.wait_ge(s["y_sb"], N_Y * n)
            elif lv == 1:
                pe.wait_ge(s["w_sb"], N_W * n + 1)
            else:
                pe.wait_ge(s["x_sb"], N_X * n + lv - 1)
                pe.wait_ge(s["y_sb"], N_Y * n + lv - 1)
            for h in range(HEADS):
                i = pe.matmul(b_i0[:, h * P:(h + 1) * P], ltm[:, h], xinv[:, h] if lv else ident, start=True, stop=True)
            i.then_inc(s["w_ps"], 1)

        def pe_merge(pe, n, lv):
            if lv == 0:
                return
            pe.wait_ge(s["w_sb"], N_W * n + lv + 1)
            if lv == 1:
                pe.wait_ge(s["y1_sb"], n + 1)
                if n:
                    pe.wait_ge(s["x_sb"], N_X * n)
            if lv < LEVELS - 1:
                for h in range(HEADS):
                    i = pe.matmul(b_i1[:, h * P:(h + 1) * P], yinv[:, n % 2, h], winv[:, h], start=True, stop=True)
                i.then_inc(s["x_ps"], 1)
            for h in range(HEADS):
                i = pe.matmul(b_i0[:, h * P:(h + 1) * P], winv[:, h], yinv[:, n % 2, h], start=True, stop=True)
            i.then_inc(s["y_ps"], 1)

        def dve_level(dve, n, lv):
            mask = con[:, C_M + lv, :].unsqueeze(1).broadcast_to([P, HEADS, P])
            if lv == 0:
                dve.wait_ge(s["lti_sb"], n + 1)
                if n >= 2:
                    dve.wait_ge(s["e_ps"], n - 1)
                dve.tensor_tensor(yinv[:, n % 2], ltm[:], con[:, C_M0T, :].unsqueeze(1).broadcast_to([P, HEADS, P]), ALU.mult).then_inc(s["y1_sb"], 1)
            dve.wait_ge(s["w_ps"], N_W * n + lv + 1)
            dve.tensor_tensor(winv[:] if lv else xinv[:], quad(b_i0), mask, ALU.mult).then_inc(s["w_sb"], 1)

        def act_level(act, n, lv):
            if lv == 0:
                return
            if lv < LEVELS - 1:
                act.wait_ge(s["x_ps"], N_X * n + lv)
                act.activation(xinv[:], quad(b_i1), ACT.Copy).then_inc(s["x_sb"], 1)
            act.wait_ge(s["y_ps"], N_Y * n + lv)
            act.activation(yinv[:, n % 2], quad(b_i0), ACT.Copy).then_inc(s["y_sb"], 1)

        def pe_state(pe, n):
            c, m, par, cc = where(n)
            if n:
                pe.wait_ge(s["s_sb"], n)
            t = slice(cc * P, (cc + 1) * P)
            for j in range(KPB):
                h = m * KPB + j
                i = pe.matmul(b_s0[:, j * REP * P:(j + 1) * REP * P], kt[:, par, h, t], state[:, h * REP:(h + 1) * REP, :], start=True, stop=True)
            i.then_inc(s["ks_ps"], 1)
            if m:
                pe.wait_ge(s["xt_sb"], n)
            elif c:
                pe.wait_ge(s["po_sb"], c)
            for j in range(KPB):
                h = m * KPB + j
                i = pe.matmul(b_s1[:, j * REP * P:(j + 1) * REP * P], qt[:, par, h, t], state[:, h * REP:(h + 1) * REP, :], start=True, stop=True)
            i.then_inc(s["qs_ps"], 1)

        def dve_state(dve, n):
            c, m, par, cc = where(n)
            dve.wait_ge(s["ks_ps"], n + 1)
            dve.wait_ge(s["gs_sb"], 3 * (c + 1))
            if n:
                dve.wait_ge(s["o_ps"], n)
            if par:
                dve.wait_ge(s["v_sb"], par * UPT)
            for h in range(HEADS):
                v = m * HEADS + h
                i = dve.scalar_tensor_tensor(out=reps[:, h], in0=b_s0[:, h * P:(h + 1) * P], scalar=ngam[:, c % 2, v:v + 1],
                                             in1=vtok[:, par, cc, v], op0=ALU.mult, op1=ALU.add)
            i.then_inc(s["r_sb"], 1)

        def act_state(act, n):
            c, m, par, cc = where(n)
            act.wait_ge(s["qs_ps"], n + 1)
            act.wait_ge(s["gs_sb"], 3 * (c + 1))
            if n:
                act.wait_ge(s["xt_ps"], n)
            for h in range(HEADS):
                v = m * HEADS + h
                i = act.activation(tq[:, h], b_s1[:, h * P:(h + 1) * P], ACT.Identity, scale=gamq[:, c % 2, v:v + 1])
            i.then_inc(s["t_sb"], 1)

        def pe_eps(pe, n):
            pe.wait_ge(s["r_sb"], n + 1)
            pe.wait_ge(s["y_sb"], N_Y * (n + 1))
            for h in range(HEADS):
                i = pe.matmul(b_s0[:, h * P:(h + 1) * P], yinv[:, n % 2, h], reps[:, h], start=True, stop=True)
            i.then_inc(s["e_ps"], 1)

        def act_eps(act, n):
            act.wait_ge(s["e_ps"], n + 1)
            act.activation(reps[:], quad(b_s0), ACT.Copy).then_inc(s["e_sb"], 1)

        def pe_update(pe, n):
            pe.wait_ge(s["e_sb"], n + 1)
            pe.wait_ge(s["kend_sb"], n + 1)
            for h in range(HEADS):
                i = pe.matmul(b_s0[:, h * P:(h + 1) * P], kend[:, n % 2, h], reps[:, h], start=True, stop=True)
            i.then_inc(s["su_ps"], 1)
            pe.wait_ge(s["t_sb"], n + 1)
            pe.wait_ge(s["pt_sb"], n + 1)
            for h in range(HEADS):
                i = pe.matmul(b_s1[:, h * P:(h + 1) * P], pt[:, n % 2, h], reps[:, h], start=True, stop=True)
            i.then_inc(s["o_ps"], 1)

        def dve_update(dve, n):
            c, m, par, cc = where(n)
            dve.wait_ge(s["su_ps"], n + 1)
            dve.wait_ge(s["qs_ps"], n + 1)
            for h in range(HEADS):
                v = m * HEADS + h
                i = dve.scalar_tensor_tensor(out=state[:, v], in0=state[:, v], scalar=gex[:, c % 2, 2, v:v + 1], in1=b_s0[:, h * P:(h + 1) * P],
                                             op0=ALU.mult, op1=ALU.add)
            i.then_inc(s["s_sb"], 1)
            dve.wait_ge(s["o_ps"], n + 1)
            dve.wait_ge(s["t_sb"], n + 1)
            for j in range(KPB):
                h = slice(j * REP, (j + 1) * REP)
                i = dve.scalar_tensor_tensor(out=tq[:, h], in0=quad(b_s1)[:, h], scalar=rn[:, par, cc, GK + m * KPB + j:GK + m * KPB + j + 1], in1=tq[:, h],
                                             op0=ALU.mult, op1=ALU.add)
            i.then_inc(s["o_sb"], 1)

        def pool_gate_out(pool, n):
            c, m, par, cc = where(n)
            pool.wait_ge(s["o_sb"], n + 1)
            if par:
                pool.wait_ge(s["pj_sb"], par * NP)
            pool.tensor_tensor(tq[:], tq[:], zs[:, par, cc, unit_heads(m)], ALU.mult).then_inc(s["xf_sb"], 1)

        def act_squares(act, n):
            act.wait_ge(s["xf_sb"], n + 1)
            if n:
                act.wait_ge(s["rm1_sb"], n)
                act.wait_ge(s["sn_sb"], n)
            for h in range(HEADS):
                i = act.activation(osq[:, h], tq[:, h], ACT.Square, accum_out=ssq[:, h:h + 1])
            i.then_inc(s["sn_sb"], 1)

        def pool_rms(pool, n):
            pool.wait_ge(s["sn_sb"], n + 1)
            if n:
                pool.wait_ge(s["xn_sb"], n)
            pool.tensor_scalar(rms[:], ssq[:], 1.0 / P, RMS_EPS, ALU.mult, ALU.add).then_inc(s["rm1_sb"], 1)
            pool.wait_ge(s["rm1_sb"], n + 1)
            pool.tensor_tensor(rms[:], rms[:], mhalf[:, 0:HEADS], ALU.pow).then_inc(s["rm_sb"], 1)
            pool.wait_ge(s["rm_sb"], n + 1)
            pool.tensor_tensor(tq[:], tq[:], rms[:].unsqueeze(2).broadcast_to([P, HEADS, P]), ALU.mult).then_inc(s["xn_sb"], 1)

        def pe_turn(pe, n):
            pe.wait_ge(s["xn_sb"], n + 1)
            for h in range(HEADS):
                i = pe.transpose(b_s1[:, h * P:(h + 1) * P], tq[:, h], ident)
            i.then_inc(s["xt_ps"], 1)

        def act_turn(act, n):
            c, m, par, cc = where(n)
            act.wait_ge(s["xt_ps"], n + 1)
            if c:
                act.wait_ge(s["out_ps"], c)
            act.activation(xnt[:, unit_heads(m)], quad(b_s1), ACT.Identity, scale=nw[:, 0:1]).then_inc(s["xt_sb"], 1)

        def pe_out(pe, c):
            pe.wait_ge(s["xt_sb"], NB * (c + 1))
            for h in range(GV):
                i = pe.matmul(b_s1[:], xnt[:, h], wot[:, h], start=(h == 0), stop=(h == GV - 1))
            i.then_inc(s["out_ps"], 1)

        def dve_out(dve, c):
            dve.wait_ge(s["out_ps"], c + 1)
            dve.wait_ge(s["rows_in"], 48 * (c + 1))
            if c >= 2:
                dve.wait_ge(s[f"stored{c % 2}"], 32 * (c // 2))
                dve.wait_ge(s["yo_sb"], c - 1)
            dve.tensor_tensor(pout[:, c % 2], b_s1[:], prow[:], ALU.add).then_inc(s["po_sb"], 1)

        def pool_out(pool, c):
            pool.wait_ge(s["po_sb"], c + 1)
            if c >= 2:
                pool.wait_ge(s[f"stored{c % 2}"], 32 * (c // 2))
            pool.tensor_tensor(yout[:, c % 2], pout[:, c % 2], grow[:], ALU.mult).then_inc(s["yg_sb"], 1)
            pool.wait_ge(s["yg_sb"], c + 1)
            pool.tensor_tensor(yout[:, c % 2], yout[:, c % 2], xrow[:], ALU.add).then_inc(s["yo_sb"], 1)

        def store(sp, c, row):
            sp.dma_start(part_d[bass.ds(row + c * P, P), :], pout[:, c % 2]).then_inc(s[f"stored{c % 2}"], 16)
            sp.dma_start(out[bass.ds(row + c * P, P), :], yout[:, c % 2]).then_inc(s[f"stored{c % 2}"], 16)

        def invert_steps(n):
            c, m = divmod(n, NB)
            return ([("gate", c)] if m == 0 else []) + [("scores", n), ("decay", n), ("matrices", n)] + [("level", n, lv) for lv in range(LEVELS)]

        def state_steps(n):
            c, m = divmod(n, NB)
            return [("state", n), ("eps", n), ("update", n), ("norm", n), ("turn", n)] + ([("out", c)] if m == NB - 1 else [])

        def share(q, i, of):
            if i == of - 1:
                steps = last_steps
            else:
                steps = first_steps[i * NF // (of - 1):(i + 1) * NF // (of - 1)]
            return [("tile", q, step) for step in steps]

        order = merged(invert_steps(0), share(0, 0, UPT))
        for n in range(UNITS):
            lists = [state_steps(n)]
            if n + 1 < UNITS:
                lists.append(invert_steps(n + 1))
            if n + 1 < UPT:
                lists.append(share(0, n + 1, UPT))
            elif n >= UPT:
                lists.append(share(1, n - UPT, UPT))
            order += merged(*lists)

        with nc.Fori(0, GROUPS) as g:
            load_weights(g)

            with nc.Block() as block:
                @block.sync
                def _(sp):
                    load_tile(sp, 0, 0)

                @block.tensor
                def _(pe):
                    for step in tile_steps:
                        pe_tile(pe, 0, 0, step)

                @block.scalar
                def _(act):
                    for step in tile_steps:
                        act_tile(act, 0, 0, step)

                @block.vector
                def _(dve):
                    for step in tile_steps:
                        dve_tile(dve, 0, 0, step)

                @block.gpsimd
                def _(pool):
                    for step in tile_steps:
                        pool_tile(pool, 0, 0, step)
            next_round()

            with nc.Fori(0, BATCH) as b:
                with nc.Block() as block:
                    @block.vector
                    def _(dve):
                        dve.memset(state[:], 0.0).then_inc(s["s_sb"], 1)
                        dve.wait_ge(s["s_sb"], 1)
                next_round()

                with nc.Fori(0, T // (BODY_TILES * TILE)) as half:
                    row = b * T + half * (BODY_TILES * TILE)
                    with nc.Block() as block:
                        @block.sync
                        def _(sp):
                            load_tile(sp, 0, b * PADT + half * (BODY_TILES * TILE) + TILE)
                            for c in range(BODY_CHUNKS):
                                if c:
                                    sp.wait_ge(s["yo_sb"], c)
                                for dst, src in ((prow, part_d), (grow, g_d), (xrow, x)):
                                    sp.dma_start(dst[:], src[bass.ds(row + c * P, P), :]).then_inc(s["rows_in"], 16)
                                if c == CPT:
                                    load_tile(sp, 1, b * PADT + half * (BODY_TILES * TILE + HALO) + BODY_TILES * TILE)
                                if c:
                                    store(sp, c - 1, row)
                            sp.wait_ge(s["yo_sb"], BODY_CHUNKS)
                            store(sp, BODY_CHUNKS - 1, row)
                            for p in range(2):
                                sp.wait_ge(s[f"stored{p}"], 16 * BODY_CHUNKS)

                        @block.tensor
                        def _(pe):
                            for kind, *i in order:
                                if kind == "tile":
                                    pe_tile(pe, i[0], 1 - i[0], i[1])
                                elif kind == "gate":
                                    pe_gate(pe, *i)
                                elif kind == "scores":
                                    pe_scores(pe, *i)
                                elif kind == "decay":
                                    pe_decay(pe, *i)
                                elif kind == "level":
                                    pe_level(pe, *i)
                                    pe_merge(pe, *i)
                                elif kind == "state":
                                    pe_state(pe, *i)
                                elif kind == "eps":
                                    pe_eps(pe, *i)
                                elif kind == "update":
                                    pe_update(pe, *i)
                                elif kind == "turn":
                                    pe_turn(pe, *i)
                                elif kind == "out":
                                    pe_out(pe, *i)

                        @block.scalar
                        def _(act):
                            for kind, *i in order:
                                if kind == "tile":
                                    act_tile(act, i[0], 1 - i[0], i[1])
                                elif kind == "gate":
                                    act_gate(act, *i)
                                elif kind == "decay":
                                    act_decay(act, *i)
                                elif kind == "level":
                                    act_level(act, *i)
                                elif kind == "state":
                                    act_state(act, *i)
                                elif kind == "eps":
                                    act_eps(act, *i)
                                elif kind == "norm":
                                    act_squares(act, *i)
                                elif kind == "turn":
                                    act_turn(act, *i)

                        @block.vector
                        def _(dve):
                            for kind, *i in order:
                                if kind == "tile":
                                    dve_tile(dve, i[0], 1 - i[0], i[1])
                                elif kind == "gate":
                                    dve_gate(dve, *i)
                                elif kind == "scores":
                                    dve_scores(dve, *i)
                                elif kind == "matrices":
                                    dve_matrices(dve, *i)
                                elif kind == "level":
                                    dve_level(dve, *i)
                                elif kind == "state":
                                    dve_state(dve, *i)
                                elif kind == "update":
                                    dve_update(dve, *i)
                                elif kind == "out":
                                    dve_out(dve, *i)

                        @block.gpsimd
                        def _(pool):
                            for kind, *i in order:
                                if kind == "tile":
                                    pool_tile(pool, i[0], 1 - i[0], i[1])
                                elif kind == "decay":
                                    pool_decay(pool, *i)
                                elif kind == "matrices":
                                    pool_matrices(pool, *i)
                                elif kind == "update":
                                    pool_gate_out(pool, *i)
                                elif kind == "norm":
                                    pool_rms(pool, *i)
                                elif kind == "out":
                                    pool_out(pool, *i)
                    next_round()


def program(nc, x, cst, w_qkvz, w_ba, conv_w, dt_bias, a_log, norm_weight, w_out,
            w_router, b_router, norm1_w, wv, bv, wo, norm2_w, w_gate, w_up, w_down, out):
    xt_d = nc.dram_tensor("xt_scratch", (P, KT, BATCH * PADT + WIN), F32, kind="Internal").ap()
    g_d = nc.dram_tensor("g_scratch", (BATCH * T, D), F32, kind="Internal").ap()
    part_d = nc.dram_tensor("part_scratch", (BATCH * T, D), F32, kind="Internal").ap()
    with ExitStack() as ctx:
        bank = [ctx.enter_context(nc.psum_tensor(f"bank{i}", [P, 512], F32)) for i in range(8)]
        feed_forward(nc, bank, x, cst, w_router, b_router, norm1_w, wv, bv, wo, norm2_w, w_gate, w_up, w_down, xt_d, g_d, part_d)
        attention(nc, bank, x, cst, w_qkvz, w_ba, conv_w, dt_bias, a_log, norm_weight, w_out, xt_d, g_d, part_d, out)


_INS = ["w_qkvz", "w_ba", "conv_w", "dt_bias", "A_log", "norm_weight", "w_out"]
_FFN = ["w_router", "b_router", "norm1_w", "wv", "bv", "wo", "norm2_w", "w_gate", "w_up", "w_down"]


def kernel(**inputs):
    import concourse.bacc as bacc
    from concourse.bass_utils import run_bass_kernel_spmd

    nc = bacc.Bacc("TRN2", target_bir_lowering=False, num_devices=1)
    arrays, args = {}, []

    def give(name, a):
        a = np.ascontiguousarray(a)
        arrays[name] = a
        args.append(nc.dram_tensor(name, a.shape, mybir.dt.from_np(a.dtype), kind="ExternalInput").ap())

    give("x", np.asarray(inputs["L0_attn_hidden_states"]).reshape(BATCH * T, D))
    give("cst", constants())
    for name in _INS:
        give(name, np.asarray(inputs["L0_attn_" + name]))
    for name in _FFN:
        a = np.asarray(inputs["L0_ffn_" + name])
        if name == "b_router":
            a = a.reshape(1)
        elif name in ("norm1_w", "norm2_w", "bv"):
            a = a.reshape(KT, P).T
        give(name, a)
    args.append(nc.dram_tensor("out", (BATCH * T, D), F32, kind="ExternalOutput").ap())
    program(nc, *args)
    r = run_bass_kernel_spmd(nc, [arrays], core_ids=[0])
    return r.results[0]["out"].reshape(BATCH, T, D)
```

```python
from contextlib import ExitStack

import numpy as np

import concourse.bass as bass
from concourse import mybir

ALU = mybir.AluOpType
ACT = mybir.ActivationFunctionType
F32 = mybir.dt.float32
F16 = mybir.dt.float16

P = 128
BATCH, T, D = 4, 1024, 512
KT = D // P
FF = 1408
FT = FF // P
NUM_K, NUM_V, TAPS = 8, 16, 4
REP = NUM_V // NUM_K
GROUPS = 2
GK, GV = NUM_K // GROUPS, NUM_V // GROUPS
ROWS_K = 2 * P + 2 * REP * P
GROWS = GK * ROWS_K
HALO = TAPS - 1
PADT = T + HALO
TILE = 256
CPT = TILE // P
WIN = TILE + HALO
FTILE = 512
RUN_TILES = 4
HEADS = 4
KPB = HEADS // REP
NB = GV // HEADS
BODY_TILES = 2
BODY_CHUNKS = BODY_TILES * CPT
UNITS = BODY_CHUNKS * NB
LEVELS = 7
HALVES = 2
HALF = HEADS // HALVES
PIPE = 3
SCALED = 64.0
HANDOVER, SLACK = 0.1, 0.2
LN_EPS = 1e-5
RMS_EPS = 1e-6
L2_EPS = 1e-6
SCALE = float(P) ** -0.5

C_ID, C_GT, C_ONE, C_LE = range(4)
N_CONST = 4
M_LT, M_LE, M_ID, M_NEG, M_L0T, M_L = 0, 2, 4, 5, 6, 7
N_MASK = M_L + LEVELS


def constants():
    r = np.arange(P)
    c, m = np.zeros((P, N_CONST, P), np.float32), np.zeros((P, N_MASK, P), np.float16)
    c[:, C_ID] = m[:, M_ID] = np.eye(P)
    m[:, M_NEG] = -SCALED * np.eye(P)
    c[:, C_GT] = r[:, None] > r[None, :]
    c[:, C_LE] = r[:, None] <= r[None, :]
    c[:, C_ONE] = 1.0
    for i in range(KPB):
        m[:, M_LT + i] = SCALED * (r[:, None] < r[None, :])
        m[:, M_LE + i] = r[:, None] <= r[None, :]
    for lv in range(LEVELS):
        s = 1 << lv
        a, b = r[:, None] // s, r[None, :] // s
        off = (a // 2 == b // 2) & (a % 2 == 1) & (b % 2 == 0)
        m[:, M_L + lv] = (np.eye(P) - off) / SCALED
    m[:, M_L0T] = m[:, M_L].T
    return c, m


def feed_forward(nc, bank, x, cst, w_router, b_router, norm1_w, wv, bv, wo, norm2_w, w_gate, w_up, w_down, xt_d, g_d, part_d):
    with ExitStack() as ctx:
        def sb(name, shape, dtype=F32):
            return ctx.enter_context(nc.sbuf_tensor(name, shape, dtype))

        def sem(name):
            return ctx.enter_context(nc.semaphore(name))

        NJ = FTILE // P
        BUFS = 3
        ident = sb("f_ident", [P, P])
        ones = sb("f_ones", [P, P])
        wv_sb, wo_sb = sb("wv_sb", [P, KT, D]), sb("wo_sb", [P, KT, D])
        wg_sb, wu_sb = sb("wg_sb", [P, KT, FF]), sb("wu_sb", [P, KT, FF])
        wd_sb = sb("wd_sb", [P, FT, D])
        wr_sb, br_sb = sb("wr_sb", [P, D]), sb("br_sb", [P, 1])
        n1_sb, n2_sb, bv_sb = sb("n1_sb", [P, KT]), sb("n2_sb", [P, KT]), sb("bv_sb", [P, KT])
        eps_sb, mhalf = sb("eps_sb", [P, 1]), sb("mhalf", [P, NJ])
        xn = sb("xn", [P, BUFS, NJ, D])
        junk, junk2 = sb("junk", [P, D], F16), sb("junk2", [P, D], F16)
        stats, mv = sb("stats", [P, NJ, 6]), sb("mv", [P, NJ, 2])
        rstd, ssq, r1 = sb("rstd", [P, NJ]), sb("ssq", [P, NJ]), sb("r1", [P, NJ])
        score, routed, kept = sb("score", [P, NJ]), sb("routed", [P, BUFS, NJ]), sb("kept", [P, BUFS, NJ])
        h1 = sb("h1", [P, 2, D])
        xt, h1t = sb("xt", [P, KT, FTILE]), sb("h1t", [P, KT, FTILE])
        vt = sb("vt", [P, KT, FTILE])
        hsq = vt
        ht, h2t = sb("ht", [P, 2, KT, FTILE]), sb("h2t", [P, 2, KT, FTILE])
        r2, r2diag = sb("r2", [P, NJ]), sb("r2diag", [P, NJ, P])
        gate = sb("gate", [P, 2, FTILE])
        zero = gate[:, 0]
        hid = sb("hid", [P, FT, FTILE])
        sel = sb("sel", [P, 2, D])

        w_in, z_set, z_out = sem("w_in"), sem("z_set"), sem("z_out")
        names = ["x_in", "stat", "mvs", "var", "rst", "xnd", "sqd", "scr", "r1a", "r1d", "rtd", "kpt", "h1d", "trx", "trh", "xtd", "h1td",
                 "xt_out", "v_ps", "v_sb", "a_ps", "h_sb", "sq_sb", "ss_ps", "ms_sb", "r2_sb", "r2diag", "r2_ps", "h2_sb", "g_ps", "u_ps", "g_act",
                 "hid_sb", "d_ps", "xk", "selw", "g_done", "g_out0", "g_out1"]
        s = {n: sem("f_" + n) for n in names}
        first, last = s[names[0]].num, s[names[-1]].num

        with nc.Block() as block:
            @block.sync
            def _(sp):
                kp = lambda a: a.rearrange("(k p) n -> p k n", p=P)
                loads = [(ident[:], cst[:, C_ID, :]), (ones[:], cst[:, C_ONE, :]), (wv_sb[:], kp(wv)), (wo_sb[:], kp(wo)), (wg_sb[:], kp(w_gate)), (wu_sb[:], kp(w_up)),
                         (wd_sb[:], kp(w_down)), (wr_sb[:], w_router.partition_broadcast(P)), (br_sb[:], b_router.partition_broadcast(P)),
                         (n1_sb[:], norm1_w), (n2_sb[:], norm2_w), (bv_sb[:], bv)]
                for dst, src in loads:
                    sp.dma_start(dst, src).then_inc(w_in, 16)
                sp.wait_ge(z_set, 1)
                n = 0
                for b in range(BATCH):
                    sp.dma_start(xt_d[:, :, b * PADT:b * PADT + HALO], zero[:, 0:KT * HALO].rearrange("p (k c) -> p k c", k=KT)).then_inc(z_out, 16)
                    n += 1
                for k in range(KT):
                    sp.dma_start(xt_d[:, k, BATCH * PADT:BATCH * PADT + WIN], zero[:, 0:WIN]).then_inc(z_out, 16)
                    n += 1
                for r in range(BATCH * T // P):
                    sp.dma_start(part_d[r * P:(r + 1) * P, :], zero).then_inc(z_out, 16)
                    n += 1
                sp.wait_ge(z_out, 16 * n)
                sp.wait_ge(w_in, 16 * len(loads))

            @block.gpsimd
            def _(pool):
                pool.memset(zero, 0.0).then_inc(z_set, 1)
                pool.memset(eps_sb[:], RMS_EPS)
                pool.memset(mhalf[:], -0.5)

        def pool_layernorm(pool, u):
            pool.wait_ge(s["mvs"], NJ * (u + 1))
            pool.tensor_scalar(rstd[:], mv[:, :, 1], LN_EPS, None, ALU.add).then_inc(s["var"], 1)
            pool.wait_ge(s["var"], u + 1)
            pool.tensor_tensor(rstd[:], rstd[:], mhalf[:], ALU.pow).then_inc(s["rst"], 1)
            pool.wait_ge(s["sqd"], NJ * (u + 1))
            if u:
                pool.wait_ge(s["h1d"], NJ * u)
            pool.tensor_scalar(r1[:], ssq[:], 1.0 / D, RMS_EPS, ALU.mult, ALU.add).then_inc(s["r1a"], 1)
            pool.wait_ge(s["r1a"], u + 1)
            pool.tensor_tensor(r1[:], r1[:], mhalf[:], ALU.pow).then_inc(s["r1d"], 1)

        def pool_rms(pool, u):
            pool.wait_ge(s["ms_sb"], u + 1)
            pool.tensor_tensor(r2[:], r2[:], mhalf[:], ALU.pow).then_inc(s["r2_sb"], 1)

        def dve_stats(dve, u):
            dve.wait_ge(s["x_in"], 16 * (u + 1))
            for j in range(NJ):
                dve.bn_stats(stats[:, j, :], xn[:, u % BUFS, j, :]).then_inc(s["stat"], 1)
            if u:
                dve.wait_ge(s["xnd"], NJ * u)
                dve.wait_ge(s["var"], u)
            for j in range(NJ):
                dve.wait_ge(s["stat"], NJ * u + j + 1)
                dve.bn_aggr(mv[:, j, :], stats[:, j, :]).then_inc(s["mvs"], 1)

        def dve_normalise(dve, u):
            dve.wait_ge(s["rst"], u + 1)
            for j in range(NJ):
                rows = xn[:, u % BUFS, j, :]
                dve.tensor_scalar(rows, rows, mv[:, j, 0:1], rstd[:, j:j + 1], ALU.subtract, ALU.mult).then_inc(s["xnd"], 1)

        def dve_router(dve, u):
            for j in range(NJ):
                n, rows = NJ * u + j, xn[:, u % BUFS, j, :]
                dve.wait_ge(s["xnd"], n + 1)
                if n:
                    dve.wait_ge(s["sqd"], n)
                    dve.wait_ge(s["scr"], n)
                if u and j == 0:
                    dve.wait_ge(s["r1a"], u)
                dve.tensor_tensor_reduce(junk[:], rows, rows, 1.0, 0.0, ALU.mult, ALU.add, ssq[:, j:j + 1]).then_inc(s["sqd"], 1)
                dve.tensor_tensor_reduce(junk2[:], rows, wr_sb[:], 1.0, 0.0, ALU.mult, ALU.add, score[:, j:j + 1]).then_inc(s["scr"], 1)
            dve.wait_ge(s["scr"], NJ * (u + 1))
            dve.tensor_scalar(routed[:, u % BUFS], score[:], br_sb[:, 0:1], 0.0, ALU.add, ALU.is_gt).then_inc(s["rtd"], 1)
            dve.wait_ge(s["rtd"], u + 1)
            dve.tensor_scalar(kept[:, u % BUFS], routed[:, u % BUFS], -1.0, 1.0, ALU.mult, ALU.add).then_inc(s["kpt"], 1)

        def pe_columns(pe, u):
            for j in range(NJ):
                n = NJ * u + j
                pe.wait_ge(s["xnd"], n + 1)
                if n:
                    pe.wait_ge(s["xtd"], n)
                if u and j == 0:
                    pe.wait_ge(s["h_sb"], KT * u)
                for k in range(KT):
                    i = pe.transpose(bank[0][:, k * P:(k + 1) * P], xn[:, u % BUFS, j, k * P:(k + 1) * P], ident[:])
                i.then_inc(s["trx"], 1)
                pe.wait_ge(s["h1d"], n + 1)
                if n:
                    pe.wait_ge(s["h1td"], n)
                for k in range(KT):
                    i = pe.transpose(bank[1][:, k * P:(k + 1) * P], h1[:, j % 2, k * P:(k + 1) * P], ident[:])
                i.then_inc(s["trh"], 1)

        def act_columns(act, u):
            if u:
                act.wait_ge(s["h_sb"], KT * u)
                act.wait_ge(s["xt_out"], 16 * u)
            for j in range(NJ):
                act.wait_ge(s["trx"], NJ * u + j + 1)
                act.activation(xt[:, :, j * P:(j + 1) * P], bank[0][:].rearrange("p (k c) -> p k c", k=KT), ACT.Copy).then_inc(s["xtd"], 1)

        def dve_columns(dve, u):
            dve.wait_ge(s["r1d"], u + 1)
            for j in range(NJ + 1):
                if j < NJ:
                    n = NJ * u + j
                    if n >= 2:
                        dve.wait_ge(s["trh"], n - 1)
                    dve.tensor_scalar(h1[:, j % 2], xn[:, u % BUFS, j, :], r1[:, j:j + 1], None, ALU.mult).then_inc(s["h1d"], 1)
                if j:
                    dve.wait_ge(s["trh"], NJ * u + j)
                    if u and j == 1:
                        dve.wait_ge(s["v_ps"], KT * u)
                    dve.tensor_tensor(h1t[:, :, (j - 1) * P:j * P], bank[1][:].rearrange("p (k c) -> p k c", k=KT),
                                      n1_sb[:].unsqueeze(2).broadcast_to([P, KT, P]), ALU.mult).then_inc(s["h1td"], 1)

        def pe_attn(pe, u):
            pe.wait_ge(s["h1td"], NJ * (u + 1))
            for e in range(KT):
                if e >= 2:
                    pe.wait_ge(s["v_sb"], KT * u + e - 1)
                elif u > 1:
                    pe.wait_ge(s["g_act"], FT * (u - 1))
                for k in range(KT):
                    i = pe.matmul(bank[2 + e % 2][:], wv_sb[:, k, e * P:(e + 1) * P], h1t[:, k, :], start=(k == 0), stop=(k == KT - 1))
                i.then_inc(s["v_ps"], 1)
            pe.wait_ge(s["v_sb"], KT * (u + 1))
            pe.wait_ge(s["xtd"], NJ * (u + 1))
            for c in range(KT):
                if c >= 2:
                    pe.wait_ge(s["h_sb"], KT * u + c - 1)
                for k in range(KT):
                    i = pe.matmul(bank[c % 2][:], wo_sb[:, k, c * P:(c + 1) * P], vt[:, k, :], start=(k == 0), stop=(k == KT - 1))
                i.then_inc(s["a_ps"], 1)

        def act_attn(act, u):
            if u:
                act.wait_ge(s["ss_ps"], u)
            for e in range(KT):
                act.wait_ge(s["v_ps"], KT * u + e + 1)
                act.activation(vt[:, e, :], bank[2 + e % 2][:], ACT.Identity, bias=bv_sb[:, e:e + 1]).then_inc(s["v_sb"], 1)
            act.wait_ge(s["a_ps"], KT * (u + 1))
            for k in range(KT):
                act.wait_ge(s["h_sb"], KT * u + k + 1)
                act.activation(hsq[:, k, :], ht[:, u % 2, k, :], ACT.Square).then_inc(s["sq_sb"], 1)

        def dve_attn(dve, u):
            dve.wait_ge(s["xtd"], NJ * (u + 1))
            if u > 1:
                dve.wait_ge(s["d_ps"], NJ * (u - 1))
            for k in range(KT):
                dve.wait_ge(s["a_ps"], KT * u + k + 1)
                dve.tensor_tensor(ht[:, u % 2, k, :], bank[k % 2][:], xt[:, k, :], ALU.add).then_inc(s["h_sb"], 1)

        def pe_sums(pe, u):
            pe.wait_ge(s["sq_sb"], KT * (u + 1))
            if u > 1:
                pe.wait_ge(s["selw"], NJ * (u - 1))
            for j in range(NJ):
                for k in range(KT):
                    i = pe.matmul(bank[7][:, j:j + 1], hsq[:, k, j * P:(j + 1) * P], ones[:, 0:1], start=(k == 0), stop=(k == KT - 1))
            i.then_inc(s["ss_ps"], 1)

        def act_sums(act, u):
            act.wait_ge(s["ss_ps"], u + 1)
            if u:
                act.wait_ge(s["r2diag"], NJ * u)
            act.activation(r2[:], bank[7][:, 0:NJ], ACT.Identity, scale=1.0 / D, bias=eps_sb[:, 0:1]).then_inc(s["ms_sb"], 1)

        def dve_diagonal(dve, u):
            dve.wait_ge(s["r2_sb"], u + 1)
            if u:
                dve.wait_ge(s["r2_ps"], u)
            for j in range(NJ):
                dve.tensor_scalar(r2diag[:, j], ident[:], r2[:, j:j + 1], None, ALU.mult).then_inc(s["r2diag"], 1)

        def pe_factors(pe, u):
            pe.wait_ge(s["ms_sb"], u + 1)
            for j in range(NJ):
                pe.wait_ge(s["r2diag"], NJ * u + j + 1)
                i = pe.matmul(bank[7][:, j * P:(j + 1) * P], ones[:], r2diag[:, j], start=True, stop=True)
            i.then_inc(s["r2_ps"], 1)

        def dve_norm2(dve, u):
            dve.wait_ge(s["r2_ps"], u + 1)
            if u > 1:
                dve.wait_ge(s["u_ps"], FT * (u - 1))
            for k in range(KT):
                dve.scalar_tensor_tensor(out=h2t[:, u % 2, k, :], in0=ht[:, u % 2, k, :], scalar=n2_sb[:, k:k + 1], in1=bank[7][:],
                                         op0=ALU.mult, op1=ALU.mult).then_inc(s["h2_sb"], 1)

        def pe_gate_up(pe, u, f):
            n = FT * u + f
            if f == 0:
                pe.wait_ge(s["h2_sb"], KT * (u + 1))
                pe.wait_ge(s["v_sb"], KT * min(u + 2, RUN_TILES))
            if n >= 2:
                pe.wait_ge(s["g_act"], n - 1)
            for k in range(KT):
                i = pe.matmul(bank[2 + f % 2][:], wg_sb[:, k, f * P:(f + 1) * P], h2t[:, u % 2, k, :], start=(k == 0), stop=(k == KT - 1))
            i.then_inc(s["g_ps"], 1)
            if n >= 2:
                pe.wait_ge(s["hid_sb"], n - 1 if f >= 2 else FT * u)
            for k in range(KT):
                i = pe.matmul(bank[4 + f % 2][:], wu_sb[:, k, f * P:(f + 1) * P], h2t[:, u % 2, k, :], start=(k == 0), stop=(k == KT - 1))
            i.then_inc(s["u_ps"], 1)

        def act_gate(act, u, f):
            n = FT * u + f
            act.wait_ge(s["g_ps"], n + 1)
            if f >= 2:
                act.wait_ge(s["hid_sb"], n - 1)
            elif u:
                act.wait_ge(s["hid_sb"], FT * u)
            act.activation(gate[:, f % 2, :], bank[2 + f % 2][:], ACT.Silu).then_inc(s["g_act"], 1)

        def dve_hidden(dve, u, f):
            n = FT * u + f
            dve.wait_ge(s["u_ps"], n + 1)
            dve.wait_ge(s["g_act"], n + 1)
            if u and f == 0:
                dve.wait_ge(s["d_ps"], NJ * u)
            dve.tensor_tensor(hid[:, f, :], bank[4 + f % 2][:], gate[:, f % 2, :], ALU.mult).then_inc(s["hid_sb"], 1)

        def pe_down(pe, u, j):
            n, out = NJ * u + j, bank[6 + j % 2]
            if n >= 2:
                pe.wait_ge(s["selw"], n - 1)
            if j == 1:
                pe.wait_ge(s["h2_sb"], KT * min(u + 2, RUN_TILES))
            for k in range(KT):
                pe.matmul(out[:, k * P:(k + 1) * P], ht[:, u % 2, k, j * P:(j + 1) * P], ident[:], start=(k == 0), stop=False, skip_group_check=True)
            pe.wait_ge(s["hid_sb"], FT * (u + 1))
            for f in range(FT):
                i = pe.matmul(out[:], hid[:, f, j * P:(j + 1) * P], wd_sb[:, f, :], start=False, stop=(f == FT - 1), skip_group_check=True)
            i.then_inc(s["d_ps"], 1)

        def dve_select(dve, u, j):
            n = NJ * u + j
            if n >= 2:
                dve.wait_ge(s[f"g_out{j % 2}"], 16 * (n // 2))
            dve.wait_ge(s["kpt"], u + 1)
            dve.tensor_scalar(sel[:, j % 2, :], xn[:, u % BUFS, j, :], kept[:, u % BUFS, j:j + 1], None, ALU.mult).then_inc(s["xk"], 1)
            dve.wait_ge(s["xk"], n + 1)
            dve.wait_ge(s["d_ps"], n + 1)
            dve.scalar_tensor_tensor(out=sel[:, j % 2, :], in0=bank[6 + j % 2][:], scalar=routed[:, u % BUFS, j:j + 1], in1=sel[:, j % 2, :],
                                     op0=ALU.mult, op1=ALU.add).then_inc(s["selw"], 1)

        def act_select(act, u, j):
            act.wait_ge(s["selw"], NJ * u + j + 1)
            act.activation(sel[:, j % 2, :], sel[:, j % 2, :], ACT.Silu).then_inc(s["g_done"], 1)

        with nc.Fori(0, BATCH * T // (RUN_TILES * FTILE)) as run:
            row = run * (RUN_TILES * FTILE)
            column = run * (RUN_TILES * FTILE // T * PADT)
            with nc.Block() as block:
                @block.sync
                def _(sp):
                    def load(u):
                        sp.dma_start(xn[:, u % BUFS], x[bass.ds(row + u * FTILE, FTILE), :].rearrange("(j p) d -> p j d", p=P)).then_inc(s["x_in"], 16)

                    load(0)
                    for u in range(RUN_TILES + 1):
                        if u + 1 < RUN_TILES:
                            if u >= 2:
                                sp.wait_ge(s["xk"], NJ * (u - 1))
                                sp.wait_ge(s["h1d"], NJ * (u - 1))
                            sp.wait_ge(s["x_in"], 16 * (u + 1))
                            load(u + 1)
                        if u < RUN_TILES:
                            sp.wait_ge(s["xtd"], NJ * (u + 1))
                            at = u * FTILE // T * PADT + HALO + u * FTILE % T
                            sp.dma_start(xt_d[:, :, bass.ds(column + at, FTILE)], xt[:]).then_inc(s["xt_out"], 16)
                        if u:
                            for j in range(NJ):
                                sp.wait_ge(s["g_done"], NJ * (u - 1) + j + 1)
                                sp.dma_start(g_d[bass.ds(row + (u - 1) * FTILE + j * P, P), :], sel[:, j % 2, :]).then_inc(s[f"g_out{j % 2}"], 16)
                    sp.wait_ge(s["xt_out"], 16 * RUN_TILES)
                    for p in range(2):
                        sp.wait_ge(s[f"g_out{p}"], 8 * NJ * RUN_TILES)

                @block.gpsimd
                def _(pool):
                    pool_layernorm(pool, 0)
                    for u in range(RUN_TILES):
                        pool_rms(pool, u)
                        if u + 1 < RUN_TILES:
                            pool_layernorm(pool, u + 1)

                @block.vector
                def _(dve):
                    dve_stats(dve, 0)
                    dve_normalise(dve, 0)
                    dve_router(dve, 0)
                    for u in range(RUN_TILES + 1):
                        if u < RUN_TILES:
                            dve_columns(dve, u)
                            dve_attn(dve, u)
                        for f in range(FT):
                            if u:
                                dve_hidden(dve, u - 1, f)
                            if u < RUN_TILES and f == 0:
                                dve_diagonal(dve, u)
                            if u < RUN_TILES and f == 2:
                                dve_norm2(dve, u)
                            if u + 1 < RUN_TILES and f == 4:
                                dve_stats(dve, u + 1)
                            if u + 1 < RUN_TILES and f == 6:
                                dve_normalise(dve, u + 1)
                            if u + 1 < RUN_TILES and f == 8:
                                dve_router(dve, u + 1)
                        if u:
                            for j in range(NJ):
                                dve_select(dve, u - 1, j)

                @block.scalar
                def _(act):
                    for u in range(RUN_TILES + 1):
                        if u < RUN_TILES:
                            act_columns(act, u)
                            act_attn(act, u)
                            act_sums(act, u)
                        if u:
                            for f in range(FT):
                                act_gate(act, u - 1, f)
                            for j in range(NJ):
                                act_select(act, u - 1, j)

                @block.tensor
                def _(pe):
                    for u in range(RUN_TILES + 1):
                        if u < RUN_TILES:
                            pe_columns(pe, u)
                            pe_attn(pe, u)
                            pe_sums(pe, u)
                        for f in range(FT):
                            if u:
                                pe_gate_up(pe, u - 1, f)
                            if u < RUN_TILES and f == 2:
                                pe_factors(pe, u)
                        if u:
                            for j in range(NJ):
                                pe_down(pe, u - 1, j)

            nc.gpsimd.sem_clear(range(first, last + 1))
            nc.all_engine_barrier()


def scheduled(streams, length, needs, loose, slack=SLACK):
    free, end, order = {}, {}, []
    at, behind = [0] * len(streams), [0.0] * len(streams)
    while len(order) < sum(map(len, streams)):
        could = []
        for i, stream in enumerate(streams):
            if at[i] < len(stream):
                after = needs(stream[at[i]])
                if all(a in end for a in after):
                    engine = length(stream[at[i]])[0][0]
                    could.append((max([free.get(engine, 0.0), behind[i]] + [end[a] for a in after]), i))
        first = min(could)[0]
        when, i = min((c for c in could if c[0] <= first + slack), key=lambda c: c[1])
        step = streams[i][at[i]]
        for engine, time in length(step):
            when = max(when, free.get(engine, 0.0)) + time
            free[engine] = when
            when += HANDOVER
        end[step] = when
        behind[i] = 0.0 if step[0] in loose else when
        at[i] += 1
        order.append(step)
    return order


def merged(*lists):
    at = [((i + 0.5) / len(steps), n, step) for n, steps in enumerate(lists) for i, step in enumerate(steps)]
    return [step for _, _, step in sorted(at, key=lambda x: x[:2])]


def attention(nc, bank, x, cst, masks, w_qkvz, w_ba, conv_w, dt_bias, a_log, norm_weight, w_out, xt_d, g_d, part_d, out):
    with ExitStack() as ctx:
        def sb(name, shape, dtype=F32):
            return ctx.enter_context(nc.sbuf_tensor(name, shape, dtype))

        def sem(name):
            return ctx.enter_context(nc.semaphore(name))

        con, mask = sb("con", [P, N_CONST, P]), sb("mask", [P, N_MASK, P], F16)
        ident, le, gt, ones = (con[:, i, :] for i in (C_ID, C_LE, C_GT, C_ONE))
        wt = sb("wt", [P, KT, GROWS])
        wba = sb("wba", [P, KT, 4 * GK])
        wot = sb("wot", [P, GV, D])
        taps = sb("taps", [P, 4 * GK, TAPS])
        dtb, neg_a = sb("dtb", [P, GV]), sb("neg_a", [P, GV])
        nw = sb("nw", [P, 1])
        mhalf = sb("mhalf2", [P, 16])
        xtile = sb("xtile", [P, KT, WIN])
        raw = sb("raw", [P, 2, WIN])
        kraw = sb("kraw", [P, GK, TILE])
        vraw = sb("vraw", [P, GV, TILE])
        sq = sb("sq", [P, GK, TILE])
        qt, kt = sb("qt", [P, 2, GK, TILE]), sb("kt", [P, 2, GK, TILE])
        ktok = sb("ktok", [P, 2, CPT, GK, P])
        vtok, zs = sb("vtok", [P, 2, CPT, GV, P]), sb("zs", [P, 2, CPT, GV, P])
        ba = sb("ba", [P, CPT, GK, 2, REP])
        beta, gdec = sb("beta", [P, 2, CPT, GV]), sb("gdec", [P, 2, CPT, GV])
        rn = sb("rn", [P, 2, CPT, 2 * GK])
        bneg, ypos, yneg, ratio, ratio2 = (sb(n, [P, CPT, GV]) for n in ("bneg", "ypos", "yneg", "ratio", "ratio2"))
        gex = sb("gex", [P, 2, 3, GV])
        ngam, gamq, bend = sb("ngam", [P, 2, GV]), sb("gamq", [P, 2, GV]), sb("bend", [P, 2, GV])
        xnt = sb("xnt", [P, GV, P])
        xrow, grow, prow = sb("xrow", [P, D]), sb("grow", [P, D]), sb("prow", [P, D])
        pout, yout = sb("pout", [P, D]), sb("yout", [P, D])
        gm, kqm, gam = sb("gm", [P, HEADS, P]), sb("kqm", [P, 2 * KPB, P]), sb("gam", [P, HEADS, P])
        ltm, pt = sb("ltm", [P, HEADS, P]), sb("pt", [P, PIPE, HEADS, P])
        lth, ltl = sb("lth", [P, 2, HEADS, P], F16), sb("ltl", [P, 2, HEADS, P], F16)
        xyinv, winv = sb("xyinv", [P, HALVES, 2, HALF, P], F16), sb("winv", [P, HALVES, HALF, P], F16)
        errh, errl, cor1, cor2 = (sb(n, [P, HEADS, P], F16) for n in ("errh", "errl", "cor1", "cor2"))
        yfin = sb("yfin", [P, 2, HEADS, P])
        kend = sb("kend", [P, 2, HEADS, P])
        reps, tq = sb("reps", [P, HEADS, P]), sb("tq", [P, 2, HEADS, P])
        osq = sb("osq", [P, HEADS, P], F16)
        state = sb("state", [P, GV, P])
        ssq, rms = sb("ssq2", [P, HEADS]), sb("rms", [P, HEADS])

        b_p, b_o, b_tr, b_a, b_i0, b_i1, b_s0, b_s1 = bank

        c_in, c_set = sem("c_in"), sem("c_set")
        names = [
            "wrow0_in", "wrow1_in", "wtr_ps", "wtr_sb", "small_in", "nega",
            "x_in", "pj_ps", "pj_sb", "cv1", "cv2", "cv3", "cv", "silu", "sq_sb", "ss_ps", "ss_sb", "rn_sb",
            "tr_ps", "ktok_sb", "kt_sb", "v_sb", "gt_sb", "gt_exp",
            "gc_ps", "gc_sb", "gs_sb", "rows_in", "out_ps", "po_sb", "yg_sb", "yo_sb", "stored",
            "gm_sb", "kq_ps", "kq_sb", "gam_ps", "gam_sb", "lt_sb", "lti_sb", "lth_sb", "ltl_sb", "pt_sb", "kend_sb",
            *(f"{n}{j}" for j in range(HALVES) for n in
              ("y1_sb", "w_ps", "w_sb", "xy_ps", "xy_sb", "er_ps", "eh_sb", "el_sb", "c1_ps", "c1_sb", "c2_ps", "c2_sb", "c3_ps", "yf_sb")),
            "ks_ps", "qs_ps", "r_sb", "t_sb", "e_ps", "e_sb", "su_ps", "s_sb", "o_ps", "o_sb", "xf_sb", "sn_sb", "rm1_sb", "rm_sb", "xn_sb",
            "xt_ps", "xt_sb",
        ]
        s = {n: sem("a_" + n) for n in names}
        first, last = s[names[0]].num, s[names[-1]].num

        def next_round():
            nc.gpsimd.sem_clear(range(first, last + 1))
            nc.all_engine_barrier()

        with nc.Block() as block:
            @block.sync
            def _(sp):
                sp.dma_start(con[:], cst).then_inc(c_in, 16)
                sp.dma_start(mask[:], masks).then_inc(c_in, 16)
                sp.dma_start(nw[:], norm_weight.rearrange("(p a) -> p a", a=1)).then_inc(c_in, 16)
                sp.wait_ge(c_in, 48)

            @block.vector
            def _(dve):
                dve.memset(mhalf[:], -0.5).then_inc(c_set, 1)
                dve.wait_ge(c_set, 1)

        def load_weights(g):
            stage = [xnt[:].rearrange("p h c -> p (h c)"), ktok[:].rearrange("p a b h c -> p (a b h c)")[:, 0:GV * P]]
            loads = [("in", r) for r in range(GROWS // P)] + [("out", r) for r in range(D // P)] + [("ba", 0)]
            steps = [(n, kind, r, part) for n, (kind, r) in enumerate(loads) for part in range(GV // 4 if kind == "out" else 1)]
            last_of = {n: i for i, (n, _, _, _) in enumerate(steps)}
            with nc.Block() as block:
                @block.sync
                def _(sp):
                    for n, (kind, r) in enumerate(loads):
                        if n >= 2:
                            sp.wait_ge(s["wtr_ps"], last_of[n - 2] + 1)
                        if kind == "in":
                            sp.dma_start(stage[n % 2][:, 0:D], w_qkvz[bass.ds(g * GROWS + r * P, P), :]).then_inc(s[f"wrow{n % 2}_in"], 16)
                        elif kind == "out":
                            sp.dma_start(stage[n % 2], w_out[r * P:(r + 1) * P, bass.ds(g * (GV * P), GV * P)]).then_inc(s[f"wrow{n % 2}_in"], 16)
                        else:
                            sp.dma_start(stage[n % 2][0:4 * GK, 0:D], w_ba[bass.ds(g * (4 * GK), 4 * GK), :]).then_inc(s[f"wrow{n % 2}_in"], 16)
                    spans = [(0, GK, NUM_K * P, GK * P), (GK, 2 * GK, 0, GK * P), (2 * GK, 4 * GK, 2 * NUM_K * P, GV * P)]
                    for lo, hi, base, width in spans:
                        sp.dma_start(taps[:, lo:hi, :], conv_w[bass.ds(g * width + base, width), :].rearrange("(h p) t -> p h t", p=P)).then_inc(s["small_in"], 16)
                    sp.dma_start(dtb[:], dt_bias[bass.ds(g * GV, GV)].partition_broadcast(P)).then_inc(s["small_in"], 16)
                    sp.dma_start(neg_a[:], a_log[bass.ds(g * GV, GV)].partition_broadcast(P)).then_inc(s["small_in"], 16)
                    sp.wait_ge(s["small_in"], 80)

                @block.tensor
                def _(pe):
                    for i, (n, kind, r, part) in enumerate(steps):
                        pe.wait_ge(s[f"wrow{n % 2}_in"], 16 * (n // 2 + 1))
                        if i >= 2:
                            pe.wait_ge(s["wtr_sb"], i - 1)
                        rows = 4 * GK if kind == "ba" else P
                        for k in range(4):
                            c = (part * 4 + k) * P
                            t = pe.transpose(bank[i % 2][:, k * P:k * P + rows], stage[n % 2][0:rows, c:c + P], ident[0:rows, 0:rows])
                        t.then_inc(s["wtr_ps"], 1)

                @block.vector
                def _(dve):
                    for i, (n, kind, r, part) in enumerate(steps):
                        dve.wait_ge(s["wtr_ps"], i + 1)
                        src = bank[i % 2][:].rearrange("p (k c) -> p k c", k=4)
                        if kind == "in":
                            dve.tensor_copy(wt[:, :, r * P:(r + 1) * P], src).then_inc(s["wtr_sb"], 1)
                        elif kind == "out":
                            dve.tensor_copy(wot[:, part * 4:part * 4 + 4, r * P:(r + 1) * P], src).then_inc(s["wtr_sb"], 1)
                        else:
                            dve.tensor_copy(wba[:], src[:, :, 0:4 * GK]).then_inc(s["wtr_sb"], 1)
                    dve.wait_ge(s["nega"], 1)
                    dve.tensor_scalar(neg_a[:], neg_a[:], -1.0, None, ALU.mult).then_inc(s["nega"], 1)

                @block.scalar
                def _(act):
                    act.wait_ge(s["small_in"], 80)
                    act.activation(neg_a[:], neg_a[:], ACT.Exp).then_inc(s["nega"], 1)
            next_round()

        feats = [("k", h) for h in range(GK)] + [("q", h) for h in range(GK)] + [("v", h) for h in range(GV)]
        prods = feats[:2 * GK] + [("ba", cc) for cc in range(CPT)] + feats[2 * GK:] + [("z", i) for i in range(CPT * NB)]
        NP, NF = len(prods), len(feats)
        feat_of = {i: feats.index(p) for i, p in enumerate(prods) if p in feats}
        prod_of = {f: i for i, f in feat_of.items()}
        BA_DONE = 2 * GK + CPT
        N_TR = 2 * CPT + CPT * NB
        N_SILU = 4
        SERIES = 9
        N_GATE = SERIES + 12
        UPT = CPT * NB

        def feature(par, kind, h):
            if kind == "k":
                return kraw[:, h, :]
            return qt[:, par, h, :] if kind == "q" else vraw[:, h, :]

        def pe_product(pe, q, i, k):
            kind, h = prods[i]
            n = q * NP + i
            if k == 0:
                if i == 0:
                    pe.wait_ge(s["x_in"], 16 * (q + 1))
                if n:
                    pe.wait_ge(s["pj_sb"], n)
            st = dict(start=(k == 0), stop=(k == KT - 1))
            if kind in "kqv":
                c = {"q": h * ROWS_K, "k": h * ROWS_K + P, "v": h // REP * ROWS_K + 2 * P + h % REP * P}[kind]
                j = pe.matmul(b_p[:, 0:WIN], wt[:, k, c:c + P], xtile[:, k, :], **st)
            elif kind == "z":
                cc, m = divmod(h, NB)
                w = wt[:, k, :].rearrange("p (h c) -> p h c", h=GK)[:, m * KPB:(m + 1) * KPB, 2 * P + REP * P:ROWS_K]
                j = pe.matmul(b_p[:], xtile[:, k, HALO + cc * P:HALO + (cc + 1) * P], w, **st)
            else:
                j = pe.matmul(b_p[:, 0:4 * GK], xtile[:, k, HALO + h * P:HALO + (h + 1) * P], wba[:, k, :], **st)
            if k == KT - 1:
                j.then_inc(s["pj_ps"], 1)

        def act_product(act, q, par, i):
            kind, h = prods[i]
            n = q * NP + i
            act.wait_ge(s["pj_ps"], n + 1)
            if kind in "kqv":
                f = feat_of[i]
                if q * NF + f >= 2:
                    act.wait_ge(s["cv"], q * NF + f - 1)
                act.activation(raw[:, f % 2, :], b_p[:, 0:WIN], ACT.Copy).then_inc(s["pj_sb"], 1)
            elif kind == "z":
                cc, m = divmod(h, NB)
                if q:
                    act.wait_ge(s["xf_sb"], q * UPT)
                act.activation(zs[:, par, cc, m * HEADS:(m + 1) * HEADS, :], b_p[:].rearrange("p (h c) -> p h c", h=HEADS), ACT.Silu).then_inc(s["pj_sb"], 1)
            else:
                act.activation(ba[:, h].rearrange("p k s r -> p (k s r)"), b_p[:, 0:4 * GK], ACT.Copy).then_inc(s["pj_sb"], 1)

        def dve_conv(dve, q, par, i, tap):
            kind, h = feats[i]
            n = q * NF + i
            acc, src = feature(par, kind, h), raw[:, i % 2, tap:tap + TILE]
            done = ("cv1", "cv2", "cv3", "cv")
            if tap:
                dve.wait_ge(s[done[tap - 1]], n + 1)
                dve.scalar_tensor_tensor(out=acc, in0=src, scalar=taps[:, i, tap:tap + 1], in1=acc, op0=ALU.mult, op1=ALU.add).then_inc(s[done[tap]], 1)
                return
            if q and h == 0:
                if kind == "k":
                    dve.wait_ge(s["sq_sb"], 2 * q - 1)
                    dve.wait_ge(s["tr_ps"], (q - 1) * N_TR + 2 * CPT)
                elif kind == "q":
                    dve.wait_ge(s["qs_ps"], q * UPT)
                    dve.wait_ge(s["kq_ps"], q * UPT)
                else:
                    dve.wait_ge(s["tr_ps"], q * N_TR)
            dve.wait_ge(s["pj_sb"], q * NP + prod_of[i] + 1)
            dve.tensor_scalar(acc, src, taps[:, i, 0:1], None, ALU.mult).then_inc(s["cv1"], 1)

        def act_silu(act, q, par, j):
            a, upto = ((kraw[:], GK), (qt[:, par], 2 * GK), (vraw[:, 0:HEADS], 2 * GK + HEADS), (vraw[:, HEADS:GV], NF))[j]
            act.wait_ge(s["cv"], q * NF + upto)
            act.activation(a, a, ACT.Silu).then_inc(s["silu"], 1)

        def pool_squares(pool, q, par, j):
            pool.wait_ge(s["silu"], q * N_SILU + j + 1)
            if q or j:
                pool.wait_ge(s["ss_ps"], 2 * q + j)
            a = qt[:, par] if j else kraw[:]
            pool.tensor_tensor(sq[:], a, a, ALU.mult).then_inc(s["sq_sb"], 1)

        def pe_squares(pe, q, j):
            pe.wait_ge(s["sq_sb"], 2 * q + j + 1)
            if j:
                pe.wait_ge(s["ss_sb"], 2 * q + j)
            elif q:
                pe.wait_ge(s["v_sb"], q * UPT)
            for cc in range(CPT):
                for h in range(GK):
                    m = pe.matmul(b_tr[:, cc * GK + h:cc * GK + h + 1], sq[:, h, cc * P:(cc + 1) * P], ones[:, 0:1], start=True, stop=True)
            m.then_inc(s["ss_ps"], 1)

        def dve_squares(dve, q, par, j):
            dve.wait_ge(s["ss_ps"], 2 * q + j + 1)
            dve.tensor_scalar(rn[:, par, :, j * GK:(j + 1) * GK], b_tr[:, 0:CPT * GK].rearrange("p (c h) -> p c h", c=CPT), L2_EPS, None, ALU.add).then_inc(s["ss_sb"], 1)

        def pool_norms(pool, q, par, j):
            pool.wait_ge(s["ss_sb"], 2 * q + j + 1)
            r = rn[:, par, :, j * GK:(j + 1) * GK]
            pool.tensor_tensor(r, r, mhalf[:, 0:CPT * GK].rearrange("p (c h) -> p c h", c=CPT), ALU.pow).then_inc(s["rn_sb"], 1)

        def dve_qscale(dve, q, par):
            dve.wait_ge(s["rn_sb"], 3 * q + 2)
            r = rn[:, par, :, GK:2 * GK]
            dve.tensor_scalar(r, r, SCALE, None, ALU.mult).then_inc(s["rn_sb"], 1)

        def pe_keys(pe, q, par, cc):
            pe.wait_ge(s["silu"], q * N_SILU + 1)
            pe.wait_ge(s["ss_sb"], 2 * q + 2)
            if cc:
                pe.wait_ge(s["kt_sb"], q * CPT + cc)
            for h in range(GK):
                t = pe.transpose(b_tr[:, h * P:(h + 1) * P], kraw[:, h, cc * P:(cc + 1) * P], ident)
            t.then_inc(s["tr_ps"], 1)
            pe.wait_ge(s["ktok_sb"], q * CPT + cc + 1)
            for h in range(GK):
                t = pe.transpose(b_tr[:, h * P:(h + 1) * P], ktok[:, par, cc, h, :], ident)
            t.then_inc(s["tr_ps"], 1)

        def dve_keys(dve, q, par, cc):
            dve.wait_ge(s["tr_ps"], q * N_TR + 2 * cc + 1)
            dve.wait_ge(s["rn_sb"], 3 * q + 1)
            if q:
                dve.wait_ge(s["kend_sb"], q * UPT)
            dve.tensor_tensor(ktok[:, par, cc], b_tr[:].rearrange("p (h c) -> p h c", h=GK),
                              rn[:, par, cc, 0:GK].unsqueeze(2).broadcast_to([P, GK, P]), ALU.mult).then_inc(s["ktok_sb"], 1)

        def act_keys(act, q, par, cc):
            act.wait_ge(s["tr_ps"], q * N_TR + 2 * cc + 2)
            if q:
                act.wait_ge(s["qs_ps"], q * UPT)
            act.activation(kt[:, par, :, cc * P:(cc + 1) * P], b_tr[:].rearrange("p (h c) -> p h c", h=GK), ACT.Copy).then_inc(s["kt_sb"], 1)

        def pe_values(pe, q, m, cc):
            pe.wait_ge(s["silu"], q * N_SILU + 3 + m)
            if m == 0 and cc == 0:
                pe.wait_ge(s["kt_sb"], (q + 1) * CPT)
            else:
                pe.wait_ge(s["v_sb"], q * UPT + m * CPT + cc)
            for h in range(HEADS):
                t = pe.transpose(b_tr[:, h * P:(h + 1) * P], vraw[:, m * HEADS + h, cc * P:(cc + 1) * P], ident)
            t.then_inc(s["tr_ps"], 1)

        def act_values(act, q, par, m, cc):
            act.wait_ge(s["tr_ps"], q * N_TR + 2 * CPT + m * CPT + cc + 1)
            if q:
                act.wait_ge(s["r_sb"], q * UPT)
            act.activation(vtok[:, par, cc, m * HEADS:(m + 1) * HEADS, :], b_tr[:].rearrange("p (h c) -> p h c", h=HEADS), ACT.Copy).then_inc(s["v_sb"], 1)

        def act_gates(act, q):
            act.wait_ge(s["gt_sb"], q * N_GATE + 3)
            act.activation(bneg[:], bneg[:], ACT.Exp).then_inc(s["gt_exp"], 1)
            act.activation(yneg[:], yneg[:], ACT.Exp).then_inc(s["gt_exp"], 1)

        def dve_gates(dve, q, par, part):
            done = [q * N_GATE + (3 if part else 0)]

            def link(ins):
                ins.then_inc(s["gt_sb"], 1)
                done[0] += 1
                dve.wait_ge(s["gt_sb"], done[0])

            by_key = lambda a: a.rearrange("p c (k r) -> p c k r", r=REP)
            per_head = lambda a: a.unsqueeze(1).broadcast_to([P, CPT, GV])
            if part == 0:
                dve.wait_ge(s["pj_sb"], q * NP + BA_DONE)
                link(dve.tensor_scalar(by_key(bneg[:]), ba[:, :, :, 0, :], -1.0, 85.0, ALU.mult, ALU.min))
                for r in range(CPT):
                    ins = dve.tensor_tensor(ypos[:, r, :].rearrange("p (k r) -> p k r", r=REP), ba[:, r, :, 1, :], dtb[:].rearrange("p (k r) -> p k r", r=REP), ALU.add)
                link(ins)
                link(dve.scalar_tensor_tensor(out=yneg[:], in0=ypos[:], scalar=-1.0, in1=ypos[:], op0=ALU.mult, op1=ALU.min))
                return
            bt, gd = beta[:, par], gdec[:, par]
            if q:
                dve.wait_ge(s["gm_sb"], q * UPT)
                dve.wait_ge(s["gc_ps"], q * CPT)
            dve.wait_ge(s["gt_exp"], 2 * q + 2)
            link(dve.tensor_scalar(bneg[:], bneg[:], 1.0, None, ALU.add))
            link(dve.reciprocal(bt, bneg[:]))
            link(dve.tensor_scalar(ratio[:], yneg[:], 2.0, None, ALU.add))
            link(dve.reciprocal(ratio[:], ratio[:]))
            link(dve.tensor_tensor(ratio[:], ratio[:], yneg[:], ALU.mult))
            link(dve.tensor_tensor(ratio2[:], ratio[:], ratio[:], ALU.mult))
            link(dve.tensor_scalar(gd, ratio2[:], 1.0 / (2 * SERIES - 1), None, ALU.mult))
            for i in range(SERIES - 2, 0, -1):
                link(dve.scalar_tensor_tensor(out=gd, in0=gd, scalar=1.0 / (2 * i + 1), in1=ratio2[:], op0=ALU.add, op1=ALU.mult))
            link(dve.scalar_tensor_tensor(out=gd, in0=gd, scalar=1.0, in1=ratio[:], op0=ALU.add, op1=ALU.mult))
            link(dve.tensor_scalar(ypos[:], ypos[:], 0.0, None, ALU.max))
            link(dve.scalar_tensor_tensor(out=gd, in0=gd, scalar=2.0, in1=ypos[:], op0=ALU.mult, op1=ALU.add))
            link(dve.tensor_tensor(gd, gd, per_head(neg_a[:]), ALU.mult))
            assert done[0] == (q + 1) * N_GATE

        def product_steps(*kinds):
            steps, taps_left = [], []
            for i, (kind, _) in enumerate(prods):
                if kind in kinds:
                    steps += merged([("product", i, k) for k in range(KT)], taps_left)
                    taps_left = [("conv", feat_of[i], tap) for tap in range(TAPS)] if i in feat_of else []
            return steps + taps_left

        key_steps = product_steps("k", "q")
        mid_steps = merged(product_steps("ba", "v"), [("silu", 0), ("silu", 1), ("squares", 0), ("squares", 1), ("gates", 0), ("gates", 1)]
                           + [("keys", cc) for cc in range(CPT)])
        end_steps = merged(product_steps("z"), [("silu", 2), ("silu", 3)]) + [("values", m, cc) for m in range(NB) for cc in range(CPT)]
        tile_steps = key_steps + mid_steps + end_steps

        def pe_tile(pe, q, par, step):
            kind, *i = step
            if kind == "product":
                pe_product(pe, q, *i)
            elif kind == "squares":
                pe_squares(pe, q, *i)
            elif kind == "keys":
                pe_keys(pe, q, par, *i)
            elif kind == "values":
                pe_values(pe, q, *i)

        def act_tile(act, q, par, step):
            kind, *i = step
            if kind == "product":
                if i[1] == KT - 1:
                    act_product(act, q, par, i[0])
            elif kind == "silu":
                act_silu(act, q, par, *i)
            elif kind == "gates" and i[0] == 0:
                act_gates(act, q)
            elif kind == "keys":
                act_keys(act, q, par, *i)
            elif kind == "values":
                act_values(act, q, par, *i)

        def dve_tile(dve, q, par, step):
            kind, *i = step
            if kind == "conv":
                dve_conv(dve, q, par, *i)
            elif kind == "squares":
                dve_squares(dve, q, par, *i)
                if i[0]:
                    dve_qscale(dve, q, par)
            elif kind == "gates":
                dve_gates(dve, q, par, *i)
            elif kind == "keys":
                dve_keys(dve, q, par, *i)

        def pool_tile(pool, q, par, step):
            kind, *i = step
            if kind == "squares":
                pool_squares(pool, q, par, *i)
                pool_norms(pool, q, par, *i)

        def load_tile(sp, q, column):
            if q:
                sp.wait_ge(s["pj_ps"], q * NP)
            sp.dma_start(xtile[:], xt_d[:, :, bass.ds(column, WIN)]).then_inc(s["x_in"], 16)

        def where(n):
            c, m = divmod(n, NB)
            return c, m, c // CPT, c % CPT

        def unit_heads(m):
            return slice(m * HEADS, (m + 1) * HEADS)

        quad = lambda b: b[:].rearrange("p (h c) -> p h c", h=HEADS)
        ident16 = mask[:, M_ID, :]

        def pe_gate(pe, c):
            par, cc = divmod(c, CPT)
            if c:
                pe.wait_ge(s["gam_sb"], NB * c)
            if par:
                pe.wait_ge(s["gt_sb"], par * N_GATE)
            for i, a in enumerate((le, gt, ones)):
                j = pe.matmul(b_a[:, i * GV:(i + 1) * GV], a, gdec[:, par, cc, :], start=True, stop=True)
            j.then_inc(s["gc_ps"], 1)

        def act_gate(act, c):
            act.wait_ge(s["gc_ps"], c + 1)
            if c >= 2:
                act.wait_ge(s["s_sb"], NB * (c - 1))
                act.wait_ge(s["gs_sb"], 3 * (c - 1))
            act.activation(gex[:, c % 2].rearrange("p a h -> p (a h)"), b_a[:, 0:3 * GV], ACT.Exp).then_inc(s["gc_sb"], 1)

        def dve_gate(dve, c):
            par, cc = divmod(c, CPT)
            dve.wait_ge(s["gc_sb"], c + 1)
            if par:
                dve.wait_ge(s["rn_sb"], 3 * par)
            if c >= 2:
                dve.wait_ge(s["t_sb"], NB * (c - 1))
                dve.wait_ge(s["kend_sb"], NB * (c - 1))
                dve.wait_ge(s["r_sb"], NB * (c - 1))
            p = c % 2
            dve.tensor_scalar(ngam[:, p], gex[:, p, 0], -1.0, None, ALU.mult).then_inc(s["gs_sb"], 1)
            dve.tensor_tensor(gamq[:, p].rearrange("p (k r) -> p k r", r=REP), gex[:, p, 0].rearrange("p (k r) -> p k r", r=REP),
                              rn[:, par, cc, GK:2 * GK].unsqueeze(2).broadcast_to([P, GK, REP]), ALU.mult).then_inc(s["gs_sb"], 1)
            dve.tensor_tensor(bend[:, p], gex[:, p, 1], beta[:, par, cc], ALU.mult).then_inc(s["gs_sb"], 1)

        def pool_decay(pool, n):
            c, m, par, cc = where(n)
            if n:
                pool.wait_ge(s["gam_ps"], n)
            if par:
                pool.wait_ge(s["gt_sb"], par * N_GATE)
            pool.tensor_tensor(gm[:], le.unsqueeze(1).broadcast_to([P, HEADS, P]),
                               gdec[:, par, cc, unit_heads(m)].unsqueeze(2).broadcast_to([P, HEADS, P]), ALU.mult).then_inc(s["gm_sb"], 1)

        def pe_scores(pe, n):
            c, m, par, cc = where(n)
            if m == 0:
                pe.wait_ge(s["gc_sb"], c + 1)
            else:
                pe.wait_ge(s["gam_sb"], n)
            if par:
                pe.wait_ge(s["kt_sb"], par * CPT)
                pe.wait_ge(s["silu"], (par - 1) * N_SILU + 2)
            t = slice(cc * P, (cc + 1) * P)
            for j in range(KPB):
                h = m * KPB + j
                pe.matmul(b_a[:, j * P:(j + 1) * P], kt[:, par, h, t], kt[:, par, h, t], start=True, stop=True)
                i = pe.matmul(b_a[:, (KPB + j) * P:(KPB + j + 1) * P], kt[:, par, h, t], qt[:, par, h, t], start=True, stop=True)
            i.then_inc(s["kq_ps"], 1)

        def dve_scores(dve, n):
            dve.wait_ge(s["kq_ps"], n + 1)
            if n:
                dve.wait_ge(s["lt_sb"], n)
                dve.wait_ge(s["pt_sb"], n)
            dve.tensor_tensor(kqm[:], b_a[:].rearrange("p (h c) -> p h c", h=2 * KPB), mask[:, M_LT:M_LT + 2 * KPB, :], ALU.mult).then_inc(s["kq_sb"], 1)

        def pe_decay(pe, n):
            pe.wait_ge(s["kq_sb"], n + 1)
            pe.wait_ge(s["gm_sb"], n + 1)
            pe.matmul(b_a[:], gt, gm[:].rearrange("p h c -> p (h c)"), start=True, stop=True).then_inc(s["gam_ps"], 1)

        def act_decay(act, n):
            act.wait_ge(s["gam_ps"], n + 1)
            if n:
                act.wait_ge(s["pt_sb"], n)
                act.wait_ge(s["lt_sb"], n)
            act.activation(gam[:], quad(b_a), ACT.Exp).then_inc(s["gam_sb"], 1)

        def dve_matrices(dve, n):
            c, m, par, cc = where(n)
            dve.wait_ge(s["gam_sb"], n + 1)
            dve.wait_ge(s["kq_sb"], n + 1)
            if n:
                dve.wait_ge(s["ltl_sb"], n)
            for h in range(HEADS):
                b = beta[:, par, cc, m * HEADS + h:m * HEADS + h + 1]
                i = dve.scalar_tensor_tensor(out=ltm[:, h], in0=gam[:, h], scalar=b, in1=kqm[:, h // REP], op0=ALU.mult, op1=ALU.mult)
            i.then_inc(s["lt_sb"], 1)
            if n >= PIPE:
                dve.wait_ge(s["o_ps"], n - PIPE + 1)
            for h in range(HEADS):
                b = beta[:, par, cc, m * HEADS + h:m * HEADS + h + 1]
                i = dve.scalar_tensor_tensor(out=pt[:, n % PIPE, h], in0=gam[:, h], scalar=b, in1=kqm[:, KPB + h // REP], op0=ALU.mult, op1=ALU.mult)
            i.then_inc(s["pt_sb"], 1)

        def pool_matrices(pool, n):
            pool.wait_ge(s["lt_sb"], n + 1)
            pool.tensor_tensor(ltm[:], ltm[:], mask[:, M_NEG, :].unsqueeze(1).broadcast_to([P, HEADS, P]), ALU.subtract).then_inc(s["lti_sb"], 1)
            pool.wait_ge(s["lth_sb"], n + 1)
            if n >= 2:
                for j in range(HALVES):
                    pool.wait_ge(s[f"er_ps{j}"], n - 1)
            pool.tensor_tensor(ltl[:, n % 2], ltm[:], lth[:, n % 2], ALU.subtract).then_inc(s["ltl_sb"], 1)

        def act_matrices(act, n):
            act.wait_ge(s["lti_sb"], n + 1)
            if n >= 2:
                for j in range(HALVES):
                    act.wait_ge(s[f"er_ps{j}"], n - 1)
                    act.wait_ge(s[f"y1_sb{j}"], n - 1)
                act.wait_ge(s["ltl_sb"], n - 1)
            act.activation(lth[:, n % 2], ltm[:], ACT.Copy).then_inc(s["lth_sb"], 1)

        def pool_kend(pool, n):
            c, m, par, cc = where(n)
            pool.wait_ge(s["gs_sb"], 3 * (c + 1))
            if n >= 2:
                pool.wait_ge(s["su_ps"], n - 1)
            if par:
                pool.wait_ge(s["ktok_sb"], par * CPT)
            for r in range(KPB):
                h = m * HEADS + r * REP
                i = pool.tensor_tensor(kend[:, n % 2, r * REP:(r + 1) * REP], ktok[:, par, cc, m * KPB + r].unsqueeze(1).broadcast_to([P, REP, P]),
                                       bend[:, c % 2, h:h + REP].unsqueeze(2).broadcast_to([P, REP, P]), ALU.mult)
            i.then_inc(s["kend_sb"], 1)

        b_inv = (b_i0, b_i1)
        left = lambda j: b_inv[j][:, 0:HALF * P]
        right = lambda j: b_inv[j][:, HALF * P:2 * HALF * P]
        pair = lambda a: a.rearrange("p (h c) -> p h c", h=HALF)
        both = lambda i: mask[:, i, :].unsqueeze(1).broadcast_to([P, HALF, P])
        half_heads = lambda j: slice(j * HALF, (j + 1) * HALF)

        def at_level(n, lv):
            return LEVELS * n + lv + 1

        def at_merge(n, lv):
            return (LEVELS - 1) * n + lv

        def each_head(pe, dst, lhsT, rhs, done=None, start=True, stop=True):
            for h in range(HALF):
                i = pe.matmul(dst[:, h * P:(h + 1) * P], lhsT(h), rhs(h), start=start and h == 0, stop=stop, skip_group_check=True)
            if done:
                i.then_inc(s[done], 1)

        def pe_level(pe, n, j, lv):
            if lv == 0:
                pe.wait_ge(s["lth_sb"], n + 1)
                if n:
                    pe.wait_ge(s[f"yf_sb{j}"], n)
            elif lv == 1:
                pe.wait_ge(s[f"w_sb{j}"], at_level(n, 0))
            else:
                pe.wait_ge(s[f"xy_sb{j}"], at_merge(n, lv - 1))
            each_head(pe, left(j), lambda h: lth[:, n % 2, j * HALF + h], lambda h: xyinv[:, j, 0, h] if lv else ident16, f"w_ps{j}")

        def pe_merge(pe, n, j, lv):
            pe.wait_ge(s[f"w_sb{j}"], at_level(n, lv))
            if lv == 1:
                pe.wait_ge(s[f"y1_sb{j}"], n + 1)
            each_head(pe, left(j), lambda h: xyinv[:, j, 1, h], lambda h: winv[:, j, h], start=True, stop=True)
            each_head(pe, right(j), lambda h: winv[:, j, h], lambda h: xyinv[:, j, 1, h], f"xy_ps{j}", start=True, stop=True)

        def dve_level(dve, n, j, lv):
            if lv == 0:
                dve.wait_ge(s["lth_sb"], n + 1)
                if n:
                    dve.wait_ge(s[f"c3_ps{j}"], n)
                dve.tensor_tensor(xyinv[:, j, 1], lth[:, n % 2, half_heads(j)], both(M_L0T), ALU.mult).then_inc(s[f"y1_sb{j}"], 1)
            dve.wait_ge(s[f"w_ps{j}"], at_level(n, lv))
            dve.tensor_tensor(winv[:, j] if lv else xyinv[:, j, 0], pair(left(j)), both(M_L + lv), ALU.mult).then_inc(s[f"w_sb{j}"], 1)

        def act_merge(act, n, j, lv):
            act.wait_ge(s[f"xy_ps{j}"], at_merge(n, lv))
            act.activation(xyinv[:, j].rearrange("p a h c -> p (a h c)"), b_inv[j][:], ACT.Copy).then_inc(s[f"xy_sb{j}"], 1)

        def pe_error(pe, n, j):
            pe.wait_ge(s[f"xy_sb{j}"], at_merge(n, LEVELS - 1))
            pe.wait_ge(s["ltl_sb"], n + 1)
            each_head(pe, left(j), lambda h: ident16, lambda h: mask[:, M_NEG, :], start=True, stop=False)
            each_head(pe, left(j), lambda h: lth[:, n % 2, j * HALF + h], lambda h: xyinv[:, j, 0, h], start=False, stop=False)
            each_head(pe, left(j), lambda h: ltl[:, n % 2, j * HALF + h], lambda h: xyinv[:, j, 0, h], f"er_ps{j}", start=False, stop=True)

        def act_error(act, n, j):
            act.wait_ge(s[f"er_ps{j}"], n + 1)
            if n:
                act.wait_ge(s[f"c3_ps{j}"], n)
                act.wait_ge(s[f"el_sb{j}"], n)
            act.activation(errh[:, half_heads(j)], pair(left(j)), ACT.Copy).then_inc(s[f"eh_sb{j}"], 1)

        def dve_error(dve, n, j):
            dve.wait_ge(s[f"eh_sb{j}"], n + 1)
            if n:
                dve.wait_ge(s[f"c1_ps{j}"], n)
            dve.tensor_tensor(errl[:, half_heads(j)], pair(left(j)), errh[:, half_heads(j)], ALU.subtract).then_inc(s[f"el_sb{j}"], 1)

        def pe_first(pe, n, j):
            pe.wait_ge(s[f"el_sb{j}"], n + 1)
            each_head(pe, right(j), lambda h: errh[:, j * HALF + h], lambda h: xyinv[:, j, 1, h], start=True, stop=False)
            each_head(pe, right(j), lambda h: errl[:, j * HALF + h], lambda h: xyinv[:, j, 1, h], f"c1_ps{j}", start=False, stop=True)

        def act_first(act, n, j):
            act.wait_ge(s[f"c1_ps{j}"], n + 1)
            if n:
                act.wait_ge(s[f"c2_ps{j}"], n)
                act.wait_ge(s[f"c2_sb{j}"], n)
            act.activation(cor1[:, half_heads(j)], pair(right(j)), ACT.Copy, scale=-1.0 / SCALED).then_inc(s[f"c1_sb{j}"], 1)

        def pe_second(pe, n, j):
            pe.wait_ge(s[f"c1_sb{j}"], n + 1)
            each_head(pe, left(j), lambda h: errh[:, j * HALF + h], lambda h: cor1[:, j * HALF + h], f"c2_ps{j}", start=True, stop=True)

        def dve_second(dve, n, j):
            dve.wait_ge(s[f"c2_ps{j}"], n + 1)
            if n:
                dve.wait_ge(s[f"c3_ps{j}"], n)
            dve.scalar_tensor_tensor(out=cor2[:, half_heads(j)], in0=pair(left(j)), scalar=-1.0 / SCALED, in1=cor1[:, half_heads(j)],
                                     op0=ALU.mult, op1=ALU.add).then_inc(s[f"c2_sb{j}"], 1)

        def pe_third(pe, n, j):
            pe.wait_ge(s[f"c2_sb{j}"], n + 1)
            each_head(pe, right(j), lambda h: mask[:, M_NEG, :], lambda h: xyinv[:, j, 1, h], stop=False)
            each_head(pe, right(j), lambda h: errh[:, j * HALF + h], lambda h: xyinv[:, j, 1, h], start=False, stop=False)
            each_head(pe, right(j), lambda h: errl[:, j * HALF + h], lambda h: xyinv[:, j, 1, h], start=False, stop=False)
            each_head(pe, right(j), lambda h: errh[:, j * HALF + h], lambda h: cor2[:, j * HALF + h], f"c3_ps{j}", start=False)

        def act_third(act, n, j):
            act.wait_ge(s[f"c3_ps{j}"], n + 1)
            if n >= 2:
                act.wait_ge(s["e_ps"], n - 1)
            act.activation(yfin[:, n % 2, half_heads(j)], pair(right(j)), ACT.Copy, scale=-1.0 / SCALED).then_inc(s[f"yf_sb{j}"], 1)

        def pe_recall(pe, n):
            c, m, par, cc = where(n)
            if n:
                pe.wait_ge(s["s_sb"], n)
            for j in range(KPB):
                h = m * KPB + j
                i = pe.matmul(b_s0[:, j * REP * P:(j + 1) * REP * P], kt[:, par, h, cc * P:(cc + 1) * P], state[:, h * REP:(h + 1) * REP, :], start=True, stop=True)
            i.then_inc(s["ks_ps"], 1)

        def dve_recall(dve, n):
            c, m, par, cc = where(n)
            dve.wait_ge(s["ks_ps"], n + 1)
            dve.wait_ge(s["gs_sb"], 3 * (c + 1))
            if n:
                dve.wait_ge(s["o_ps"], n)
            if par:
                dve.wait_ge(s["v_sb"], par * UPT)
            for h in range(HEADS):
                v = m * HEADS + h
                i = dve.scalar_tensor_tensor(out=reps[:, h], in0=b_s0[:, h * P:(h + 1) * P], scalar=ngam[:, c % 2, v:v + 1],
                                             in1=vtok[:, par, cc, v], op0=ALU.mult, op1=ALU.add)
            i.then_inc(s["r_sb"], 1)

        def pe_query(pe, n):
            c, m, par, cc = where(n)
            if n:
                pe.wait_ge(s["s_sb"], n)
                pe.wait_ge(s["o_sb"], n)
            for j in range(KPB):
                h = m * KPB + j
                i = pe.matmul(b_s1[:, j * REP * P:(j + 1) * REP * P], qt[:, par, h, cc * P:(cc + 1) * P], state[:, h * REP:(h + 1) * REP, :], start=True, stop=True)
            i.then_inc(s["qs_ps"], 1)

        def act_query(act, n):
            c, m, par, cc = where(n)
            act.wait_ge(s["qs_ps"], n + 1)
            act.wait_ge(s["gs_sb"], 3 * (c + 1))
            if n >= 2:
                act.wait_ge(s["xt_ps"], n - 1)
            for h in range(HEADS):
                v = m * HEADS + h
                i = act.activation(tq[:, n % 2, h], b_s1[:, h * P:(h + 1) * P], ACT.Identity, scale=gamq[:, c % 2, v:v + 1])
            i.then_inc(s["t_sb"], 1)

        def pe_eps(pe, n):
            pe.wait_ge(s["r_sb"], n + 1)
            for j in range(HALVES):
                pe.wait_ge(s[f"yf_sb{j}"], n + 1)
            for h in range(HEADS):
                i = pe.matmul(b_s0[:, h * P:(h + 1) * P], yfin[:, n % 2, h], reps[:, h], start=True, stop=True)
            i.then_inc(s["e_ps"], 1)

        def act_eps(act, n):
            act.wait_ge(s["e_ps"], n + 1)
            act.activation(reps[:], quad(b_s0), ACT.Copy).then_inc(s["e_sb"], 1)

        def pe_learn(pe, n):
            pe.wait_ge(s["e_sb"], n + 1)
            pe.wait_ge(s["kend_sb"], n + 1)
            for h in range(HEADS):
                i = pe.matmul(b_s0[:, h * P:(h + 1) * P], kend[:, n % 2, h], reps[:, h], start=True, stop=True)
            i.then_inc(s["su_ps"], 1)

        def dve_learn(dve, n):
            c, m, par, cc = where(n)
            dve.wait_ge(s["su_ps"], n + 1)
            dve.wait_ge(s["qs_ps"], n + 1)
            for h in range(HEADS):
                v = m * HEADS + h
                i = dve.scalar_tensor_tensor(out=state[:, v], in0=state[:, v], scalar=gex[:, c % 2, 2, v:v + 1], in1=b_s0[:, h * P:(h + 1) * P],
                                             op0=ALU.mult, op1=ALU.add)
            i.then_inc(s["s_sb"], 1)

        def pe_answer(pe, n):
            pe.wait_ge(s["e_sb"], n + 1)
            pe.wait_ge(s["t_sb"], n + 1)
            pe.wait_ge(s["pt_sb"], n + 1)
            for h in range(HEADS):
                i = pe.matmul(b_s1[:, h * P:(h + 1) * P], pt[:, n % PIPE, h], reps[:, h], start=True, stop=True)
            i.then_inc(s["o_ps"], 1)

        def dve_answer(dve, n):
            c, m, par, cc = where(n)
            dve.wait_ge(s["o_ps"], n + 1)
            dve.wait_ge(s["t_sb"], n + 1)
            for j in range(KPB):
                h = slice(j * REP, (j + 1) * REP)
                i = dve.scalar_tensor_tensor(out=tq[:, n % 2, h], in0=quad(b_s1)[:, h], scalar=rn[:, par, cc, GK + m * KPB + j:GK + m * KPB + j + 1], in1=tq[:, n % 2, h],
                                             op0=ALU.mult, op1=ALU.add)
            i.then_inc(s["o_sb"], 1)

        def pool_gate_out(pool, n):
            c, m, par, cc = where(n)
            pool.wait_ge(s["o_sb"], n + 1)
            if par:
                pool.wait_ge(s["pj_sb"], par * NP)
            pool.tensor_tensor(tq[:, n % 2], tq[:, n % 2], zs[:, par, cc, unit_heads(m)], ALU.mult).then_inc(s["xf_sb"], 1)

        def act_squares(act, n):
            act.wait_ge(s["xf_sb"], n + 1)
            if n:
                act.wait_ge(s["rm1_sb"], n)
                act.wait_ge(s["sn_sb"], n)
            for h in range(HEADS):
                i = act.activation(osq[:, h], tq[:, n % 2, h], ACT.Square, accum_out=ssq[:, h:h + 1])
            i.then_inc(s["sn_sb"], 1)

        def pool_rms(pool, n):
            pool.wait_ge(s["sn_sb"], n + 1)
            if n:
                pool.wait_ge(s["xn_sb"], n)
            pool.tensor_scalar(rms[:], ssq[:], 1.0 / P, RMS_EPS, ALU.mult, ALU.add).then_inc(s["rm1_sb"], 1)
            pool.wait_ge(s["rm1_sb"], n + 1)
            pool.tensor_tensor(rms[:], rms[:], mhalf[:, 0:HEADS], ALU.pow).then_inc(s["rm_sb"], 1)
            pool.wait_ge(s["rm_sb"], n + 1)
            pool.tensor_tensor(tq[:, n % 2], tq[:, n % 2], rms[:].unsqueeze(2).broadcast_to([P, HEADS, P]), ALU.mult).then_inc(s["xn_sb"], 1)

        def pe_turn(pe, n):
            pe.wait_ge(s["xn_sb"], n + 1)
            if n:
                pe.wait_ge(s["xt_sb"], n)
            if n >= NB and n % NB == 0:
                pe.wait_ge(s["po_sb"], n // NB)
            for h in range(HEADS):
                i = pe.transpose(b_o[:, h * P:(h + 1) * P], tq[:, n % 2, h], ident)
            i.then_inc(s["xt_ps"], 1)

        def act_turn(act, n):
            c, m, par, cc = where(n)
            act.wait_ge(s["xt_ps"], n + 1)
            if c:
                act.wait_ge(s["out_ps"], c)
            act.activation(xnt[:, unit_heads(m)], quad(b_o), ACT.Identity, scale=nw[:, 0:1]).then_inc(s["xt_sb"], 1)

        def pe_out(pe, c, h):
            if h == 0:
                pe.wait_ge(s["xt_sb"], NB * (c + 1))
            i = pe.matmul(b_o[:], xnt[:, h], wot[:, h], start=(h == 0), stop=(h == GV - 1))
            if h == GV - 1:
                i.then_inc(s["out_ps"], 1)

        def dve_out(dve, c):
            dve.wait_ge(s["out_ps"], c + 1)
            dve.wait_ge(s["rows_in"], 48 * (c + 1))
            if c:
                dve.wait_ge(s["stored"], 32 * c)
                dve.wait_ge(s["yo_sb"], c)
            dve.tensor_tensor(pout[:], b_o[:], prow[:], ALU.add).then_inc(s["po_sb"], 1)

        def pool_out(pool, c):
            pool.wait_ge(s["po_sb"], c + 1)
            if c:
                pool.wait_ge(s["stored"], 32 * c)
            pool.tensor_tensor(yout[:], pout[:], grow[:], ALU.mult).then_inc(s["yg_sb"], 1)
            pool.wait_ge(s["yg_sb"], c + 1)
            pool.tensor_tensor(yout[:], yout[:], xrow[:], ALU.add).then_inc(s["yo_sb"], 1)

        def store(sp, c, row):
            sp.dma_start(part_d[bass.ds(row + c * P, P), :], pout[:]).then_inc(s["stored"], 16)
            sp.dma_start(out[bass.ds(row + c * P, P), :], yout[:]).then_inc(s["stored"], 16)

        def build_steps(n):
            c, m = divmod(n, NB)
            return ([("gate", c)] if m == 0 else []) + [("scores", n), ("decay", n), ("matrices", n)]

        def invert_steps(n, j):
            steps = [("level", n, j, 0)]
            for lv in range(1, LEVELS):
                steps += [("level", n, j, lv), ("merge", n, j, lv)]
            return steps + [(kind, n, j) for kind in ("error", "first", "second", "third")]

        def core_steps(n):
            return [("kend", n), ("recall", n), ("query", n), ("eps", n), ("learn", n), ("answer", n)]

        def out_steps(n):
            c, m = divmod(n, NB)
            return [("gated", n), ("norm", n), ("turn", n)] + ([("out", c, h) for h in range(GV)] if m == NB - 1 else [])

        lengths = {
            "gate": [("pe", .1), ("act", .3), ("dve", .4)], "scores": [("pe", .9), ("dve", .6)], "decay": [("pool", 1.2), ("pe", .9), ("act", .6)],
            "matrices": [("dve", 2.1), ("pool", 1.2), ("act", .5), ("pool", 1.2)], "kend": [("pool", 2.4)],
            "level": [("pe", .1), ("dve", .4)], "merge": [("pe", .2), ("act", .5)], "error": [("pe", .35), ("act", .3), ("dve", .4)],
            "first": [("pe", .2), ("act", .3)], "second": [("pe", .1), ("dve", .4)], "third": [("pe", .2), ("act", .3)],
            "recall": [("pe", .9), ("dve", 1.1)], "query": [("pe", .9), ("act", 1.0)], "eps": [("pe", .9), ("act", .5)],
            "learn": [("pe", .9), ("dve", 1.1)], "answer": [("pe", .9), ("dve", .8)], "gated": [("pool", 1.2)], "norm": [("act", 1.2), ("pool", 2.2)], "turn": [("pe", .4), ("act", .6)],
        }

        def length(step):
            kind, *i = step
            if kind == "out":
                return [("pe", .9)] + ([("dve", .6), ("pool", 2.4)] if i[1] == GV - 1 else [])
            if kind != "tile":
                return lengths[kind]
            kind, *i = i[1]
            if kind == "product":
                what = prods[i[0]][0]
                pe = [("pe", {"z": .9, "ba": .1}.get(what, .45))]
                return pe + ({"z": [("act", .6)], "ba": [("act", .2)]}.get(what, [("act", .35)]) if i[1] == KT - 1 else [])
            return {"conv": [("dve", .37)], "silu": [("act", 1.5)], "squares": [("pool", 2.3), ("pe", .2), ("dve", .2), ("pool", 1.5)], "keys": [("pe", .45), ("dve", .6), ("pe", .45), ("act", .5)],
                    "values": [("pe", .45), ("act", .5)], "gates": [("dve", .3), ("act", .5)] if i[0] == 0 else [("dve", 2.5)]}[kind]

        def needs(step):
            kind, *i = step
            n = i[0]
            units = lambda *pairs: [(kind, u) for kind, u in pairs if u >= 0]
            if kind == "gate":
                return units(("answer", NB * (n - 1) - 1), ("learn", NB * (n - 1) - 1)) + ([("tile", 0, mid_steps[-1])] if n == CPT else [])
            if kind == "matrices":
                return units(("answer", n - PIPE)) + ([("error", n - 2, j) for j in range(HALVES)] if n >= 2 else [])
            if kind == "level" and i[2] == 0:
                return [("matrices", n)]
            if kind == "third":
                return units(("eps", n - 2))
            if kind == "kend":
                return units(("matrices", n), ("learn", n - 2))
            if kind == "recall":
                return units(("learn", n - 1), ("answer", n - 1)) + ([("tile", 0, tile_steps[-1])] if n == UPT else [])
            if kind == "query":
                return units(("learn", n - NB), ("answer", n - 1), ("turn", n - 2))
            if kind == "eps":
                return [("recall", n)] + [("third", n, j) for j in range(HALVES)]
            if kind == "learn":
                return [("eps", n), ("kend", n), ("query", n)]
            if kind == "answer":
                return [("eps", n), ("query", n)]
            if kind == "gated":
                return [("answer", n)] + ([("tile", 0, tile_steps[-1])] if n == UPT else [])
            if kind == "out":
                return units(("turn", NB * n + NB - 1))
            if kind != "tile":
                return []
            q, (kind, *i) = i
            before = []
            if kind == "product" and i[1] == 0 and i[0]:
                before = [("product", i[0] - 1, KT - 1)]
            elif kind == "conv":
                before = [("product", prod_of[i[0]], KT - 1)]
            elif kind == "silu":
                before = [("conv", (GK, 2 * GK, 2 * GK + HEADS, NF)[i[0]] - 1, TAPS - 1)]
            elif kind == "squares":
                before = [("silu", i[0])]
            elif kind == "keys":
                before = [("squares", 1)]
            elif kind == "gates":
                before = [("gates", 0)] if i[0] else [("product", BA_DONE - 1, KT - 1)]
            elif kind == "values":
                before = [("silu", 2 + i[0])]
            taken = {("product", 0, 0): ("recall", UPT - 2), ("product", GK, 0): ("answer", UPT - 1), ("product", BA_DONE, 0): ("gated", UPT - 1)}
            return [("tile", q, b) for b in before] + ([taken[(kind, *i)]] if q and (kind, *i) in taken else [])

        units = range(UNITS)
        streams = {
            "core": [step for n in units for step in core_steps(n)], "out": [step for n in units for step in out_steps(n)],
            "halves": [[step for n in units for step in invert_steps(n, j)] for j in range(HALVES)],
            "build": [step for n in units for step in build_steps(n)], "tiles": [("tile", q, step) for q in range(2) for step in tile_steps],
        }
        order = scheduled([*streams["halves"], streams["tiles"], streams["build"], streams["core"], streams["out"]], length, needs,
                          loose=("tile", "out", "kend", "recall", "query", "eps", "learn", "answer"))

        with nc.Fori(0, GROUPS) as g:
            load_weights(g)

            with nc.Block() as block:
                @block.sync
                def _(sp):
                    load_tile(sp, 0, 0)

                @block.tensor
                def _(pe):
                    for step in tile_steps:
                        pe_tile(pe, 0, 0, step)

                @block.scalar
                def _(act):
                    for step in tile_steps:
                        act_tile(act, 0, 0, step)

                @block.vector
                def _(dve):
                    for step in tile_steps:
                        dve_tile(dve, 0, 0, step)

                @block.gpsimd
                def _(pool):
                    for step in tile_steps:
                        pool_tile(pool, 0, 0, step)
            next_round()

            with nc.Fori(0, BATCH) as b:
                with nc.Block() as block:
                    @block.vector
                    def _(dve):
                        dve.memset(state[:], 0.0).then_inc(s["s_sb"], 1)
                        dve.wait_ge(s["s_sb"], 1)
                next_round()

                with nc.Fori(0, T // (BODY_TILES * TILE)) as half:
                    row = b * T + half * (BODY_TILES * TILE)
                    with nc.Block() as block:
                        @block.sync
                        def _(sp):
                            load_tile(sp, 0, b * PADT + half * (BODY_TILES * TILE) + TILE)
                            for c in range(BODY_CHUNKS):
                                if c:
                                    sp.wait_ge(s["yo_sb"], c)
                                for dst, src in ((prow, part_d), (grow, g_d), (xrow, x)):
                                    sp.dma_start(dst[:], src[bass.ds(row + c * P, P), :]).then_inc(s["rows_in"], 16)
                                if c:
                                    store(sp, c - 1, row)
                                if c == CPT - 1:
                                    load_tile(sp, 1, b * PADT + half * (BODY_TILES * TILE + HALO) + BODY_TILES * TILE)
                            sp.wait_ge(s["yo_sb"], BODY_CHUNKS)
                            store(sp, BODY_CHUNKS - 1, row)
                            sp.wait_ge(s["stored"], 32 * BODY_CHUNKS)

                        @block.tensor
                        def _(pe):
                            for kind, *i in order:
                                if kind == "tile":
                                    pe_tile(pe, i[0], 1 - i[0], i[1])
                                elif kind == "gate":
                                    pe_gate(pe, *i)
                                elif kind == "scores":
                                    pe_scores(pe, *i)
                                elif kind == "decay":
                                    pe_decay(pe, *i)
                                elif kind == "level":
                                    pe_level(pe, *i)
                                elif kind == "merge":
                                    pe_merge(pe, *i)
                                elif kind == "error":
                                    pe_error(pe, *i)
                                elif kind == "first":
                                    pe_first(pe, *i)
                                elif kind == "second":
                                    pe_second(pe, *i)
                                elif kind == "third":
                                    pe_third(pe, *i)
                                elif kind == "recall":
                                    pe_recall(pe, *i)
                                elif kind == "query":
                                    pe_query(pe, *i)
                                elif kind == "eps":
                                    pe_eps(pe, *i)
                                elif kind == "learn":
                                    pe_learn(pe, *i)
                                elif kind == "answer":
                                    pe_answer(pe, *i)
                                elif kind == "turn":
                                    pe_turn(pe, *i)
                                elif kind == "out":
                                    pe_out(pe, *i)

                        @block.scalar
                        def _(act):
                            for kind, *i in order:
                                if kind == "tile":
                                    act_tile(act, i[0], 1 - i[0], i[1])
                                elif kind == "gate":
                                    act_gate(act, *i)
                                elif kind == "decay":
                                    act_decay(act, *i)
                                elif kind == "matrices":
                                    act_matrices(act, *i)
                                elif kind == "merge":
                                    act_merge(act, *i)
                                elif kind == "error":
                                    act_error(act, *i)
                                elif kind == "first":
                                    act_first(act, *i)
                                elif kind == "third":
                                    act_third(act, *i)
                                elif kind == "query":
                                    act_query(act, *i)
                                elif kind == "eps":
                                    act_eps(act, *i)
                                elif kind == "norm":
                                    act_squares(act, *i)
                                elif kind == "turn":
                                    act_turn(act, *i)

                        @block.vector
                        def _(dve):
                            for kind, *i in order:
                                if kind == "tile":
                                    dve_tile(dve, i[0], 1 - i[0], i[1])
                                elif kind == "gate":
                                    dve_gate(dve, *i)
                                elif kind == "scores":
                                    dve_scores(dve, *i)
                                elif kind == "matrices":
                                    dve_matrices(dve, *i)
                                elif kind == "level":
                                    dve_level(dve, *i)
                                elif kind == "error":
                                    dve_error(dve, *i)
                                elif kind == "second":
                                    dve_second(dve, *i)
                                elif kind == "recall":
                                    dve_recall(dve, *i)
                                elif kind == "learn":
                                    dve_learn(dve, *i)
                                elif kind == "answer":
                                    dve_answer(dve, *i)
                                elif kind == "out":
                                    if i[1] == GV - 1:
                                        dve_out(dve, i[0])

                        @block.gpsimd
                        def _(pool):
                            for kind, *i in order:
                                if kind == "tile":
                                    pool_tile(pool, i[0], 1 - i[0], i[1])
                                elif kind == "decay":
                                    pool_decay(pool, *i)
                                elif kind == "matrices":
                                    pool_matrices(pool, *i)
                                elif kind == "kend":
                                    pool_kend(pool, *i)
                                elif kind == "gated":
                                    pool_gate_out(pool, *i)
                                elif kind == "norm":
                                    pool_rms(pool, *i)
                                elif kind == "out":
                                    if i[1] == GV - 1:
                                        pool_out(pool, i[0])
                    next_round()


def program(nc, x, cst, masks, w_qkvz, w_ba, conv_w, dt_bias, a_log, norm_weight, w_out,
            w_router, b_router, norm1_w, wv, bv, wo, norm2_w, w_gate, w_up, w_down, out):
    xt_d = nc.dram_tensor("xt_scratch", (P, KT, BATCH * PADT + WIN), F32, kind="Internal").ap()
    g_d = nc.dram_tensor("g_scratch", (BATCH * T, D), F32, kind="Internal").ap()
    part_d = nc.dram_tensor("part_scratch", (BATCH * T, D), F32, kind="Internal").ap()
    with ExitStack() as ctx:
        bank = [ctx.enter_context(nc.psum_tensor(f"bank{i}", [P, 512], F32)) for i in range(8)]
        feed_forward(nc, bank, x, cst, w_router, b_router, norm1_w, wv, bv, wo, norm2_w, w_gate, w_up, w_down, xt_d, g_d, part_d)
        attention(nc, bank, x, cst, masks, w_qkvz, w_ba, conv_w, dt_bias, a_log, norm_weight, w_out, xt_d, g_d, part_d, out)


_INS = ["w_qkvz", "w_ba", "conv_w", "dt_bias", "A_log", "norm_weight", "w_out"]
_FFN = ["w_router", "b_router", "norm1_w", "wv", "bv", "wo", "norm2_w", "w_gate", "w_up", "w_down"]


def kernel(**inputs):
    import concourse.bacc as bacc
    from concourse.bass_utils import run_bass_kernel_spmd

    nc = bacc.Bacc("TRN2", target_bir_lowering=False, num_devices=1)
    arrays, args = {}, []

    def give(name, a):
        a = np.ascontiguousarray(a)
        arrays[name] = a
        args.append(nc.dram_tensor(name, a.shape, mybir.dt.from_np(a.dtype), kind="ExternalInput").ap())

    give("x", np.asarray(inputs["L0_attn_hidden_states"]).reshape(BATCH * T, D))
    for name, a in zip(("cst", "masks"), constants()):
        give(name, a)
    for name in _INS:
        give(name, np.asarray(inputs["L0_attn_" + name]))
    for name in _FFN:
        a = np.asarray(inputs["L0_ffn_" + name])
        if name == "b_router":
            a = a.reshape(1)
        elif name in ("norm1_w", "norm2_w", "bv"):
            a = a.reshape(KT, P).T
        give(name, a)
    args.append(nc.dram_tensor("out", (BATCH * T, D), F32, kind="ExternalOutput").ap())
    program(nc, *args)
    r = run_bass_kernel_spmd(nc, [arrays], core_ids=[0])
    return r.results[0]["out"].reshape(BATCH, T, D)
```

```python
from contextlib import ExitStack

import numpy as np

import concourse.bass as bass
from concourse import mybir

ALU = mybir.AluOpType
ACT = mybir.ActivationFunctionType
F32 = mybir.dt.float32
F16 = mybir.dt.float16

P = 128
BATCH, T, D = 4, 1024, 512
KT = D // P
FF = 1408
FT = FF // P
NUM_K, NUM_V, TAPS = 8, 16, 4
REP = NUM_V // NUM_K
GROUPS = 2
GK, GV = NUM_K // GROUPS, NUM_V // GROUPS
ROWS_K = 2 * P + 2 * REP * P
GROWS = GK * ROWS_K
HALO = TAPS - 1
PADT = T + HALO
TILE = 256
CPT = TILE // P
WIN = TILE + HALO
FTILE = 512
RUN_TILES = 4
HEADS = 4
KPB = HEADS // REP
NB = GV // HEADS
BODY_TILES = T // TILE
BODY_CHUNKS = BODY_TILES * CPT
UNITS = BODY_CHUNKS * NB
LEVELS = 7
HALVES = 2
HALF = HEADS // HALVES
PIPE = 3
SCALED = 64.0
HANDOVER, SLACK = 0.163, 0.108
LN_EPS = 1e-5
RMS_EPS = 1e-6
L2_EPS = 1e-6
SCALE = float(P) ** -0.5

C_ID, C_GT, C_ONE, C_LE = range(4)
N_CONST = 4
M_LT, M_LE, M_ID, M_NEG, M_L0T, M_L = 0, 2, 4, 5, 6, 7
N_MASK = M_L + LEVELS


def constants():
    r = np.arange(P)
    c, m = np.zeros((P, N_CONST, P), np.float32), np.zeros((P, N_MASK, P), np.float16)
    c[:, C_ID] = m[:, M_ID] = np.eye(P)
    m[:, M_NEG] = -SCALED * np.eye(P)
    c[:, C_GT] = r[:, None] > r[None, :]
    c[:, C_LE] = r[:, None] <= r[None, :]
    c[:, C_ONE] = 1.0
    for i in range(KPB):
        m[:, M_LT + i] = SCALED * (r[:, None] < r[None, :])
        m[:, M_LE + i] = r[:, None] <= r[None, :]
    for lv in range(LEVELS):
        s = 1 << lv
        a, b = r[:, None] // s, r[None, :] // s
        off = (a // 2 == b // 2) & (a % 2 == 1) & (b % 2 == 0)
        m[:, M_L + lv] = (np.eye(P) - off) / SCALED
    m[:, M_L0T] = m[:, M_L].T
    return c, m


def feed_forward(nc, bank, x, cst, w_router, b_router, norm1_w, wv, bv, wo, norm2_w, w_gate, w_up, w_down, xt_d, g_d, part_d):
    with ExitStack() as ctx:
        def sb(name, shape, dtype=F32):
            return ctx.enter_context(nc.sbuf_tensor(name, shape, dtype))

        def sem(name):
            return ctx.enter_context(nc.semaphore(name))

        NJ = FTILE // P
        BUFS = 3
        ident = sb("f_ident", [P, P])
        ones = sb("f_ones", [P, P])
        wv_sb, wo_sb = sb("wv_sb", [P, KT, D]), sb("wo_sb", [P, KT, D])
        wg_sb, wu_sb = sb("wg_sb", [P, KT, FF]), sb("wu_sb", [P, KT, FF])
        wd_sb = sb("wd_sb", [P, FT, D])
        wr_sb, br_sb = sb("wr_sb", [P, D]), sb("br_sb", [P, 1])
        n1_sb, n2_sb, bv_sb = sb("n1_sb", [P, KT]), sb("n2_sb", [P, KT]), sb("bv_sb", [P, KT])
        eps_sb, mhalf = sb("eps_sb", [P, 1]), sb("mhalf", [P, NJ])
        xn = sb("xn", [P, BUFS, NJ, D])
        junk, junk2 = sb("junk", [P, D], F16), sb("junk2", [P, D], F16)
        stats, mv = sb("stats", [P, NJ, 6]), sb("mv", [P, NJ, 2])
        rstd, ssq, r1 = sb("rstd", [P, NJ]), sb("ssq", [P, NJ]), sb("r1", [P, NJ])
        score, routed, kept = sb("score", [P, NJ]), sb("routed", [P, BUFS, NJ]), sb("kept", [P, BUFS, NJ])
        h1 = sb("h1", [P, 2, D])
        xt, h1t = sb("xt", [P, KT, FTILE]), sb("h1t", [P, KT, FTILE])
        vt = sb("vt", [P, KT, FTILE])
        hsq = vt
        ht, h2t = sb("ht", [P, 2, KT, FTILE]), sb("h2t", [P, 2, KT, FTILE])
        r2, r2diag = sb("r2", [P, NJ]), sb("r2diag", [P, NJ, P])
        gate = sb("gate", [P, 2, FTILE])
        zero = gate[:, 0]
        hid = sb("hid", [P, FT, FTILE])
        sel = sb("sel", [P, 2, D])

        w_in, w_late, z_set, z_out = (sem(n) for n in ("w_in", "w_late", "z_set", "z_out"))
        names = ["x_in", "stat", "mvs", "var", "rst", "xnd", "sqd", "scr", "r1a", "r1d", "rtd", "kpt", "h1d", "trx", "trh", "xtd", "h1td",
                 "xt_out", "v_ps", "v_sb", "a_ps", "h_sb", "sq_sb", "ss_ps", "ms_sb", "r2_sb", "r2diag", "r2_ps", "h2_sb", "g_ps", "u_ps", "g_act",
                 "hid_sb", "d_ps", "xk", "selw", "g_done", "g_out0", "g_out1"]
        s = {n: sem("f_" + n) for n in names}
        first, last = s[names[0]].num, s[names[-1]].num

        kp = lambda a: a.rearrange("(k p) n -> p k n", p=P)
        tail = xt_d.shape[2] - BATCH * PADT
        zeros = [(xt_d[:, :, b * PADT:b * PADT + HALO], zero[:, 0:KT * HALO].rearrange("p (k c) -> p k c", k=KT)) for b in range(BATCH)]
        zeros += [(xt_d[:, k, BATCH * PADT:], zero[:, 0:tail]) for k in range(KT)]
        zeros += [(part_d.rearrange("(r p) d -> p r d", p=P), zero.unsqueeze(1).broadcast_to([P, BATCH * T // P, D]))]
        late = [(wg_sb[:], kp(w_gate)), (wu_sb[:], kp(w_up)), (wd_sb[:], kp(w_down))]
        early = [(ident[:], cst[:, C_ID, :]), (ones[:], cst[:, C_ONE, :]), (wv_sb[:], kp(wv)), (wo_sb[:], kp(wo)),
                 (wr_sb[:], w_router.partition_broadcast(P)), (br_sb[:], b_router.partition_broadcast(P)),
                 (n1_sb[:], norm1_w), (n2_sb[:], norm2_w), (bv_sb[:], bv)]
        with nc.Block() as block:
            @block.sync
            def _(sp):
                for dst, src in early:
                    sp.dma_start(dst, src).then_inc(w_in, 16)
                sp.wait_ge(w_in, 16 * len(early))

            @block.scalar
            def _(act):
                act.wait_ge(w_in, 16 * len(early))
                for dst, src in late:
                    act.dma_start(dst, src).then_inc(w_late, 16)
                act.wait_ge(z_set, 1)
                for dst, src in zeros:
                    act.dma_start(dst, src).then_inc(z_out, 16)

            @block.gpsimd
            def _(pool):
                pool.memset(zero, 0.0).then_inc(z_set, 1)
                pool.memset(eps_sb[:], RMS_EPS)
                pool.memset(mhalf[:], -0.5)

        def pool_layernorm(pool, u):
            pool.wait_ge(s["mvs"], NJ * (u + 1))
            pool.tensor_scalar(rstd[:], mv[:, :, 1], LN_EPS, None, ALU.add).then_inc(s["var"], 1)
            pool.wait_ge(s["var"], u + 1)
            pool.tensor_tensor(rstd[:], rstd[:], mhalf[:], ALU.pow).then_inc(s["rst"], 1)
            pool.wait_ge(s["sqd"], NJ * (u + 1))
            if u:
                pool.wait_ge(s["h1d"], NJ * u)
            pool.tensor_scalar(r1[:], ssq[:], 1.0 / D, RMS_EPS, ALU.mult, ALU.add).then_inc(s["r1a"], 1)
            pool.wait_ge(s["r1a"], u + 1)
            pool.tensor_tensor(r1[:], r1[:], mhalf[:], ALU.pow).then_inc(s["r1d"], 1)

        def pool_rms(pool, u):
            pool.wait_ge(s["ms_sb"], u + 1)
            pool.tensor_tensor(r2[:], r2[:], mhalf[:], ALU.pow).then_inc(s["r2_sb"], 1)

        def dve_stats(dve, u):
            dve.wait_ge(s["x_in"], 16 * (u + 1))
            for j in range(NJ):
                dve.bn_stats(stats[:, j, :], xn[:, u % BUFS, j, :]).then_inc(s["stat"], 1)
            if u:
                dve.wait_ge(s["xnd"], NJ * u)
                dve.wait_ge(s["var"], u)
            for j in range(NJ):
                dve.wait_ge(s["stat"], NJ * u + j + 1)
                dve.bn_aggr(mv[:, j, :], stats[:, j, :]).then_inc(s["mvs"], 1)

        def dve_normalise(dve, u):
            dve.wait_ge(s["rst"], u + 1)
            for j in range(NJ):
                rows = xn[:, u % BUFS, j, :]
                dve.tensor_scalar(rows, rows, mv[:, j, 0:1], rstd[:, j:j + 1], ALU.subtract, ALU.mult).then_inc(s["xnd"], 1)

        def dve_router(dve, u):
            for j in range(NJ):
                n, rows = NJ * u + j, xn[:, u % BUFS, j, :]
                dve.wait_ge(s["xnd"], n + 1)
                if n:
                    dve.wait_ge(s["sqd"], n)
                    dve.wait_ge(s["scr"], n)
                if u and j == 0:
                    dve.wait_ge(s["r1a"], u)
                dve.tensor_tensor_reduce(junk[:], rows, rows, 1.0, 0.0, ALU.mult, ALU.add, ssq[:, j:j + 1]).then_inc(s["sqd"], 1)
                dve.tensor_tensor_reduce(junk2[:], rows, wr_sb[:], 1.0, 0.0, ALU.mult, ALU.add, score[:, j:j + 1]).then_inc(s["scr"], 1)
            dve.wait_ge(s["scr"], NJ * (u + 1))
            dve.tensor_scalar(routed[:, u % BUFS], score[:], br_sb[:, 0:1], 0.0, ALU.add, ALU.is_gt).then_inc(s["rtd"], 1)
            dve.wait_ge(s["rtd"], u + 1)
            dve.tensor_scalar(kept[:, u % BUFS], routed[:, u % BUFS], -1.0, 1.0, ALU.mult, ALU.add).then_inc(s["kpt"], 1)

        def pe_columns(pe, u, j):
            n = NJ * u + j
            pe.wait_ge(s["xnd"], n + 1)
            if n:
                pe.wait_ge(s["xtd"], n)
            if u and j == 0:
                pe.wait_ge(s["h_sb"], KT * u)
            for k in range(KT):
                i = pe.transpose(bank[0][:, k * P:(k + 1) * P], xn[:, u % BUFS, j, k * P:(k + 1) * P], ident[:])
            i.then_inc(s["trx"], 1)
            pe.wait_ge(s["h1d"], n + 1)
            if n:
                pe.wait_ge(s["h1td"], n)
            for k in range(KT):
                i = pe.transpose(bank[1][:, k * P:(k + 1) * P], h1[:, j % 2, k * P:(k + 1) * P], ident[:])
            i.then_inc(s["trh"], 1)

        def act_columns(act, u, j):
            if u and j == 0:
                act.wait_ge(s["h_sb"], KT * u)
                act.wait_ge(s["xt_out"], 16 * u)
            act.wait_ge(s["trx"], NJ * u + j + 1)
            act.activation(xt[:, :, j * P:(j + 1) * P], bank[0][:].rearrange("p (k c) -> p k c", k=KT), ACT.Copy).then_inc(s["xtd"], 1)

        def dve_norm1(dve, u, j):
            n = NJ * u + j
            dve.wait_ge(s["r1d"], u + 1)
            if n >= 2:
                dve.wait_ge(s["trh"], n - 1)
            dve.tensor_scalar(h1[:, j % 2], xn[:, u % BUFS, j, :], r1[:, j:j + 1], None, ALU.mult).then_inc(s["h1d"], 1)

        def dve_columns(dve, u, j):
            dve.wait_ge(s["trh"], NJ * u + j + 1)
            if u and j == 0:
                dve.wait_ge(s["v_ps"], KT * u)
            dve.tensor_tensor(h1t[:, :, j * P:(j + 1) * P], bank[1][:].rearrange("p (k c) -> p k c", k=KT),
                              n1_sb[:].unsqueeze(2).broadcast_to([P, KT, P]), ALU.mult).then_inc(s["h1td"], 1)

        def pe_value(pe, u, e):
            if e == 0:
                pe.wait_ge(s["h1td"], NJ * (u + 1))
                pe.wait_ge(s["xtd"], NJ * (u + 1))
            elif e >= 2:
                pe.wait_ge(s["v_sb"], KT * u + e - 1)
            for k in range(KT):
                i = pe.matmul(bank[e % 2][:], wv_sb[:, k, e * P:(e + 1) * P], h1t[:, k, :], start=(k == 0), stop=(k == KT - 1))
            i.then_inc(s["v_ps"], 1)

        def act_value(act, u, e):
            if u and e == 0:
                act.wait_ge(s["ss_ps"], u)
            act.wait_ge(s["v_ps"], KT * u + e + 1)
            act.activation(vt[:, e, :], bank[e % 2][:], ACT.Identity, bias=bv_sb[:, e:e + 1]).then_inc(s["v_sb"], 1)

        def pe_attn(pe, u, c):
            if c == 0:
                pe.wait_ge(s["v_sb"], KT * (u + 1))
            elif c >= 2:
                pe.wait_ge(s["h_sb"], KT * u + c - 1)
            for k in range(KT):
                i = pe.matmul(bank[c % 2][:], wo_sb[:, k, c * P:(c + 1) * P], vt[:, k, :], start=(k == 0), stop=(k == KT - 1))
            i.then_inc(s["a_ps"], 1)

        def dve_attn(dve, u, c):
            if c == 0:
                dve.wait_ge(s["xtd"], NJ * (u + 1))
                if u > 1:
                    dve.wait_ge(s["d_ps"], NJ * (u - 1))
            dve.wait_ge(s["a_ps"], KT * u + c + 1)
            dve.tensor_tensor(ht[:, u % 2, c, :], bank[c % 2][:], xt[:, c, :], ALU.add).then_inc(s["h_sb"], 1)

        def act_squares(act, u):
            act.wait_ge(s["a_ps"], KT * (u + 1))
            for k in range(KT):
                act.wait_ge(s["h_sb"], KT * u + k + 1)
                act.activation(hsq[:, k, :], ht[:, u % 2, k, :], ACT.Square).then_inc(s["sq_sb"], 1)

        def pe_sums(pe, u):
            pe.wait_ge(s["sq_sb"], KT * (u + 1))
            if u > 1:
                pe.wait_ge(s["selw"], NJ * (u - 1))
            for j in range(NJ):
                for k in range(KT):
                    i = pe.matmul(bank[7][:, j:j + 1], hsq[:, k, j * P:(j + 1) * P], ones[:, 0:1], start=(k == 0), stop=(k == KT - 1))
            i.then_inc(s["ss_ps"], 1)

        def act_sums(act, u):
            act.wait_ge(s["ss_ps"], u + 1)
            if u:
                act.wait_ge(s["r2diag"], NJ * u)
            act.activation(r2[:], bank[7][:, 0:NJ], ACT.Identity, scale=1.0 / D, bias=eps_sb[:, 0:1]).then_inc(s["ms_sb"], 1)

        def dve_diagonal(dve, u):
            dve.wait_ge(s["r2_sb"], u + 1)
            if u:
                dve.wait_ge(s["r2_ps"], u)
            for j in range(NJ):
                dve.tensor_scalar(r2diag[:, j], ident[:], r2[:, j:j + 1], None, ALU.mult).then_inc(s["r2diag"], 1)

        def pe_factors(pe, u):
            pe.wait_ge(s["ms_sb"], u + 1)
            for j in range(NJ):
                pe.wait_ge(s["r2diag"], NJ * u + j + 1)
                i = pe.matmul(bank[7][:, j * P:(j + 1) * P], ones[:], r2diag[:, j], start=True, stop=True)
            i.then_inc(s["r2_ps"], 1)

        def dve_norm2(dve, u):
            dve.wait_ge(s["r2_ps"], u + 1)
            if u > 1:
                dve.wait_ge(s["u_ps"], FT * (u - 1))
            for k in range(KT):
                dve.scalar_tensor_tensor(out=h2t[:, u % 2, k, :], in0=ht[:, u % 2, k, :], scalar=n2_sb[:, k:k + 1], in1=bank[7][:],
                                         op0=ALU.mult, op1=ALU.mult).then_inc(s["h2_sb"], 1)

        def pe_gate_up(pe, u, f):
            n = FT * u + f
            if f == 0:
                pe.wait_ge(s["h2_sb"], KT * (u + 1))
            if n == 0:
                pe.wait_ge(w_late, 16 * len(late))
            if n >= 2:
                pe.wait_ge(s["g_act"], n - 1)
            for k in range(KT):
                i = pe.matmul(bank[2 + f % 2][:], wg_sb[:, k, f * P:(f + 1) * P], h2t[:, u % 2, k, :], start=(k == 0), stop=(k == KT - 1))
            i.then_inc(s["g_ps"], 1)
            if n >= 2:
                pe.wait_ge(s["hid_sb"], n - 1 if f >= 2 else FT * u)
            for k in range(KT):
                i = pe.matmul(bank[4 + f % 2][:], wu_sb[:, k, f * P:(f + 1) * P], h2t[:, u % 2, k, :], start=(k == 0), stop=(k == KT - 1))
            i.then_inc(s["u_ps"], 1)

        def act_gate(act, u, f):
            n = FT * u + f
            act.wait_ge(s["g_ps"], n + 1)
            if f >= 2:
                act.wait_ge(s["hid_sb"], n - 1)
            elif u:
                act.wait_ge(s["hid_sb"], FT * u)
            else:
                act.wait_ge(z_out, 16 * len(zeros))
            act.activation(gate[:, f % 2, :], bank[2 + f % 2][:], ACT.Silu).then_inc(s["g_act"], 1)

        def dve_hidden(dve, u, f):
            n = FT * u + f
            dve.wait_ge(s["u_ps"], n + 1)
            dve.wait_ge(s["g_act"], n + 1)
            if u and f == 0:
                dve.wait_ge(s["d_ps"], NJ * u)
            dve.tensor_tensor(hid[:, f, :], bank[4 + f % 2][:], gate[:, f % 2, :], ALU.mult).then_inc(s["hid_sb"], 1)

        def pe_down(pe, u, j):
            n, out = NJ * u + j, bank[6 + j % 2]
            if n >= 2:
                pe.wait_ge(s["selw"], n - 1)
            if j == 1:
                pe.wait_ge(s["h2_sb"], KT * min(u + 2, RUN_TILES))
            for k in range(KT):
                pe.matmul(out[:, k * P:(k + 1) * P], ht[:, u % 2, k, j * P:(j + 1) * P], ident[:], start=(k == 0), stop=False, skip_group_check=True)
            pe.wait_ge(s["hid_sb"], FT * (u + 1))
            for f in range(FT):
                i = pe.matmul(out[:], hid[:, f, j * P:(j + 1) * P], wd_sb[:, f, :], start=False, stop=(f == FT - 1), skip_group_check=True)
            i.then_inc(s["d_ps"], 1)

        def dve_select(dve, u, j):
            n = NJ * u + j
            if n >= 2:
                dve.wait_ge(s[f"g_out{j % 2}"], 16 * (n // 2))
            dve.wait_ge(s["kpt"], u + 1)
            dve.tensor_scalar(sel[:, j % 2, :], xn[:, u % BUFS, j, :], kept[:, u % BUFS, j:j + 1], None, ALU.mult).then_inc(s["xk"], 1)
            dve.wait_ge(s["xk"], n + 1)
            dve.wait_ge(s["d_ps"], n + 1)
            dve.scalar_tensor_tensor(out=sel[:, j % 2, :], in0=bank[6 + j % 2][:], scalar=routed[:, u % BUFS, j:j + 1], in1=sel[:, j % 2, :],
                                     op0=ALU.mult, op1=ALU.add).then_inc(s["selw"], 1)

        def act_select(act, u, j):
            act.wait_ge(s["selw"], NJ * u + j + 1)
            act.activation(sel[:, j % 2, :], sel[:, j % 2, :], ACT.Silu).then_inc(s["g_done"], 1)

        columns = [("norm1", 0)] + [step for j in range(NJ) for step in ([("norm1", j + 1)] if j + 1 < NJ else []) + [("columns", j)]]
        first_half = (columns + [("value", e) for e in range(KT)] + [("attn", c) for c in range(KT)]
                      + [("sums",), ("factors",), ("norm2",)])
        order = [(step, 0) for step in (("stats",), ("normalise",), ("router",))]
        for u in range(RUN_TILES + 1):
            lists = []
            if u < RUN_TILES:
                lists.append([(step, u) for step in first_half])
            if u:
                lists.append([(("gate", f), u - 1) for f in range(FT)])
            order += merged(*lists)
            lists = []
            if u:
                lists.append([(("down", j), u - 1) for j in range(NJ)])
            if u + 1 < RUN_TILES:
                lists.append([(step, u + 1) for step in (("stats",), ("normalise",), ("router",))])
            order += merged(*lists)

        with nc.Fori(0, BATCH * T // (RUN_TILES * FTILE)) as run:
            row = run * (RUN_TILES * FTILE)
            column = run * (RUN_TILES * FTILE // T * PADT)
            with nc.Block() as block:
                @block.sync
                def _(sp):
                    def load(u):
                        sp.dma_start(xn[:, u % BUFS], x[bass.ds(row + u * FTILE, FTILE), :].rearrange("(j p) d -> p j d", p=P)).then_inc(s["x_in"], 16)

                    load(0)
                    for u in range(RUN_TILES + 1):
                        if u + 1 < RUN_TILES:
                            if u >= 2:
                                sp.wait_ge(s["xk"], NJ * (u - 1))
                                sp.wait_ge(s["h1d"], NJ * (u - 1))
                            sp.wait_ge(s["x_in"], 16 * (u + 1))
                            load(u + 1)
                        if u < RUN_TILES:
                            sp.wait_ge(s["xtd"], NJ * (u + 1))
                            at = u * FTILE // T * PADT + HALO + u * FTILE % T
                            sp.dma_start(xt_d[:, :, bass.ds(column + at, FTILE)], xt[:]).then_inc(s["xt_out"], 16)
                        if u:
                            for j in range(NJ):
                                sp.wait_ge(s["g_done"], NJ * (u - 1) + j + 1)
                                sp.dma_start(g_d[bass.ds(row + (u - 1) * FTILE + j * P, P), :], sel[:, j % 2, :]).then_inc(s[f"g_out{j % 2}"], 16)
                    sp.wait_ge(s["xt_out"], 16 * RUN_TILES)
                    for p in range(2):
                        sp.wait_ge(s[f"g_out{p}"], 8 * NJ * RUN_TILES)

                @block.gpsimd
                def _(pool):
                    pool_layernorm(pool, 0)
                    for u in range(RUN_TILES):
                        pool_rms(pool, u)
                        if u + 1 < RUN_TILES:
                            pool_layernorm(pool, u + 1)

                @block.vector
                def _(dve):
                    for (kind, *i), u in order:
                        if kind == "stats":
                            dve_stats(dve, u)
                        elif kind == "normalise":
                            dve_normalise(dve, u)
                        elif kind == "router":
                            dve_router(dve, u)
                        elif kind == "norm1":
                            dve_norm1(dve, u, *i)
                        elif kind == "columns":
                            dve_columns(dve, u, *i)
                        elif kind == "attn":
                            dve_attn(dve, u, *i)
                        elif kind == "factors":
                            dve_diagonal(dve, u)
                        elif kind == "norm2":
                            dve_norm2(dve, u)
                        elif kind == "gate":
                            dve_hidden(dve, u, *i)
                        elif kind == "down":
                            dve_select(dve, u, *i)

                @block.scalar
                def _(act):
                    for (kind, *i), u in order:
                        if kind == "columns":
                            act_columns(act, u, *i)
                        elif kind == "value":
                            act_value(act, u, *i)
                        elif kind == "sums":
                            act_squares(act, u)
                            act_sums(act, u)
                        elif kind == "gate":
                            act_gate(act, u, *i)
                        elif kind == "down":
                            act_select(act, u, *i)

                @block.tensor
                def _(pe):
                    for (kind, *i), u in order:
                        if kind == "columns":
                            pe_columns(pe, u, *i)
                        elif kind == "value":
                            pe_value(pe, u, *i)
                        elif kind == "attn":
                            pe_attn(pe, u, *i)
                        elif kind == "sums":
                            pe_sums(pe, u)
                        elif kind == "factors":
                            pe_factors(pe, u)
                        elif kind == "gate":
                            pe_gate_up(pe, u, *i)
                        elif kind == "down":
                            pe_down(pe, u, *i)

            nc.gpsimd.sem_clear(range(first, last + 1))
            nc.all_engine_barrier()


def scheduled(streams, length, needs, loose, slack=SLACK):
    free, end, order = {}, {}, []
    at, behind = [0] * len(streams), [0.0] * len(streams)
    while len(order) < sum(map(len, streams)):
        could = []
        for i, stream in enumerate(streams):
            if at[i] < len(stream):
                after = needs(stream[at[i]])
                if all(a in end for a in after):
                    engine = length(stream[at[i]])[0][0]
                    could.append((max([free.get(engine, 0.0), behind[i]] + [end[a] for a in after]), i))
        first = min(could)[0]
        when, i = min((c for c in could if c[0] <= first + slack), key=lambda c: c[1])
        step = streams[i][at[i]]
        for engine, time in length(step):
            when = max(when, free.get(engine, 0.0)) + time
            free[engine] = when
            when += HANDOVER
        end[step] = when
        behind[i] = 0.0 if step[0] in loose else when
        at[i] += 1
        order.append(step)
    return order


def merged(*lists):
    at = [((i + 0.5) / len(steps), n, step) for n, steps in enumerate(lists) for i, step in enumerate(steps)]
    return [step for _, _, step in sorted(at, key=lambda x: x[:2])]


def attention(nc, bank, x, cst, masks, w_qkvz, w_ba, conv_w, dt_bias, a_log, norm_weight, w_out, xt_d, g_d, part_d, out):
    with ExitStack() as ctx:
        def sb(name, shape, dtype=F32):
            return ctx.enter_context(nc.sbuf_tensor(name, shape, dtype))

        def sem(name):
            return ctx.enter_context(nc.semaphore(name))

        con, mask = sb("con", [P, N_CONST, P]), sb("mask", [P, N_MASK, P], F16)
        ident, le, gt, ones = (con[:, i, :] for i in (C_ID, C_LE, C_GT, C_ONE))
        wt = sb("wt", [P, KT, GROWS])
        wba = sb("wba", [P, KT, 4 * GK])
        wot = sb("wot", [P, GV, D])
        taps = sb("taps", [P, 4 * GK, TAPS])
        dtb, neg_a = sb("dtb", [P, GV]), sb("neg_a", [P, GV])
        nw = sb("nw", [P, 1])
        mhalf = sb("mhalf2", [P, 16])
        xtile = sb("xtile", [P, 2, KT, WIN])
        raw = sb("raw", [P, 2, WIN])
        kraw = sb("kraw", [P, GK, TILE])
        vraw = sb("vraw", [P, GV, TILE])
        sq = sb("sq", [P, GK, TILE])
        qt, kt = sb("qt", [P, 2, GK, TILE]), sb("kt", [P, 2, GK, TILE])
        ktok = sb("ktok", [P, 2, CPT, GK, P])
        vtok, zs = sb("vtok", [P, 2, CPT, GV, P]), sb("zs", [P, 2, CPT, GV, P])
        ba = sb("ba", [P, CPT, GK, 2, REP])
        beta, gdec = sb("beta", [P, 2, CPT, GV]), sb("gdec", [P, 2, CPT, GV])
        rn = sb("rn", [P, 2, CPT, 2 * GK])
        bneg, ypos, yneg, ratio, ratio2 = (sb(n, [P, CPT, GV]) for n in ("bneg", "ypos", "yneg", "ratio", "ratio2"))
        gex = sb("gex", [P, 2, 3, GV])
        ngam, gamq, bend = sb("ngam", [P, 2, GV]), sb("gamq", [P, 2, GV]), sb("bend", [P, 2, GV])
        xnt = sb("xnt", [P, GV, P])
        xrow, grow, prow = sb("xrow", [P, D]), sb("grow", [P, D]), sb("prow", [P, D])
        pout, yout = prow, sb("yout", [P, D])
        gm, kqm, gam = sb("gm", [P, HEADS, P]), sb("kqm", [P, 2 * KPB, P]), sb("gam", [P, HEADS, P])
        ltm, pt = sb("ltm", [P, HEADS, P]), sb("pt", [P, PIPE, HEADS, P])
        lth, ltl = sb("lth", [P, 2, HEADS, P], F16), sb("ltl", [P, 2, HEADS, P], F16)
        xyinv, winv = sb("xyinv", [P, HALVES, 2, HALF, P], F16), sb("winv", [P, HALVES, HALF, P], F16)
        errh, cor2 = (sb(n, [P, HEADS, P], F16) for n in ("errh", "cor2"))
        errl, cor1 = winv, xyinv[:, :, 0]
        yfin = sb("yfin", [P, 2, HEADS, P])
        kend = sb("kend", [P, 2, HEADS, P])
        reps, tq = sb("reps", [P, HEADS, P]), sb("tq", [P, 2, HEADS, P])
        osq = sb("osq", [P, HEADS, P], F16)
        state = sb("state", [P, GV, P])
        ssq, rms = sb("ssq2", [P, HEADS]), sb("rms", [P, HEADS])

        b_o, b_a, b_i0, b_i1, b_s0, b_s1 = bank[2:]

        c_in, c_set = sem("c_in"), sem("c_set")
        names = [
            "wrow0_in", "wrow1_in", "wtr_ps", "wtr_sb", "small_in", "nega",
            "x_in0", "x_in1", "pj_ps", "pj_sb", "cv1", "cv2", "cv3", "cv", "silu", "sq_sb", "ss_ps", "ss_sb", "rn_sb",
            "tr_ps", "ktok_sb", "kt_sb", "v_sb", "gt_sb", "gt_exp",
            "gc_ps", "gc_sb", "gs_sb", "rows_in", "out_ps", "po_sb", "yg_sb", "yo_sb", "stored",
            "gm_sb", "kq_ps", "kq_sb", "gam_ps", "gam_sb", "lt_sb", "lti_sb", "lth_sb", "ltl_sb", "pt_sb", "kend_sb",
            *(f"{n}{j}" for j in range(HALVES) for n in
              ("y1_sb", "w_ps", "w_sb", "xy_ps", "xy_sb", "er_ps", "eh_sb", "el_sb", "c1_ps", "c1_sb", "c2_ps", "c2_sb", "c3_ps", "yf_sb")),
            "s_set", "ks_ps", "qs_ps", "r_sb", "t_sb", "e_ps", "e_sb", "su_ps", "s_sb", "o_ps", "o_sb", "xf_sb", "sn_sb", "rm1_sb", "rm_sb", "xn_sb",
            "xt_ps", "xt_sb",
        ]
        s = {n: sem("a_" + n) for n in names}
        first, last = s[names[0]].num, s[names[-1]].num

        def next_round():
            nc.gpsimd.sem_clear(range(first, last + 1))
            nc.all_engine_barrier()

        with nc.Block() as block:
            @block.sync
            def _(sp):
                sp.dma_start(con[:], cst).then_inc(c_in, 16)
                sp.dma_start(mask[:], masks).then_inc(c_in, 16)
                sp.dma_start(nw[:], norm_weight.rearrange("(p a) -> p a", a=1)).then_inc(c_in, 16)
                sp.wait_ge(c_in, 48)

            @block.vector
            def _(dve):
                dve.memset(mhalf[:], -0.5).then_inc(c_set, 1)
                dve.wait_ge(c_set, 1)

        def load_weights(g):
            stage = [xnt[:].rearrange("p h c -> p (h c)"), ktok[:].rearrange("p a b h c -> p (a b h c)")[:, 0:GV * P]]
            loads = [("in", r) for r in range(GROWS // (2 * P))] + [("out", r) for r in range(D // P)] + [("ba", 0)]
            steps = [(n, kind, r, part) for n, (kind, r) in enumerate(loads) for part in range({"in": 2, "out": GV // 4, "ba": 1}[kind])]
            last_of = {n: i for i, (n, _, _, _) in enumerate(steps)}
            with nc.Block() as block:
                @block.sync
                def _(sp):
                    for n, (kind, r) in enumerate(loads):
                        if n >= 2:
                            sp.wait_ge(s["wtr_ps"], last_of[n - 2] + 1)
                        if kind == "in":
                            sp.dma_start(stage[n % 2].rearrange("p (a d) -> p a d", a=2), w_qkvz[bass.ds(g * GROWS + r * 2 * P, 2 * P), :].rearrange("(a p) d -> p a d", p=P)).then_inc(s[f"wrow{n % 2}_in"], 16)
                        elif kind == "out":
                            sp.dma_start(stage[n % 2], w_out[r * P:(r + 1) * P, bass.ds(g * (GV * P), GV * P)]).then_inc(s[f"wrow{n % 2}_in"], 16)
                        else:
                            sp.dma_start(stage[n % 2][0:4 * GK, 0:D], w_ba[bass.ds(g * (4 * GK), 4 * GK), :]).then_inc(s[f"wrow{n % 2}_in"], 16)
                    spans = [(0, GK, NUM_K * P, GK * P), (GK, 2 * GK, 0, GK * P), (2 * GK, 4 * GK, 2 * NUM_K * P, GV * P)]
                    for lo, hi, base, width in spans:
                        sp.dma_start(taps[:, lo:hi, :], conv_w[bass.ds(g * width + base, width), :].rearrange("(h p) t -> p h t", p=P)).then_inc(s["small_in"], 16)
                    sp.dma_start(dtb[:], dt_bias[bass.ds(g * GV, GV)].partition_broadcast(P)).then_inc(s["small_in"], 16)
                    sp.dma_start(neg_a[:], a_log[bass.ds(g * GV, GV)].partition_broadcast(P)).then_inc(s["small_in"], 16)
                    sp.wait_ge(s["small_in"], 80)

                @block.tensor
                def _(pe):
                    for i, (n, kind, r, part) in enumerate(steps):
                        pe.wait_ge(s[f"wrow{n % 2}_in"], 16 * (n // 2 + 1))
                        if i >= 2:
                            pe.wait_ge(s["wtr_sb"], i - 1)
                        rows = 4 * GK if kind == "ba" else P
                        for k in range(4):
                            c = (part * 4 + k) * P
                            t = pe.transpose(bank[i % 2][:, k * P:k * P + rows], stage[n % 2][0:rows, c:c + P], ident[0:rows, 0:rows])
                        t.then_inc(s["wtr_ps"], 1)

                @block.vector
                def _(dve):
                    for i, (n, kind, r, part) in enumerate(steps):
                        dve.wait_ge(s["wtr_ps"], i + 1)
                        src = bank[i % 2][:].rearrange("p (k c) -> p k c", k=4)
                        if kind == "in":
                            dve.tensor_copy(wt[:, :, (2 * r + part) * P:(2 * r + part + 1) * P], src).then_inc(s["wtr_sb"], 1)
                        elif kind == "out":
                            dve.tensor_copy(wot[:, part * 4:part * 4 + 4, r * P:(r + 1) * P], src).then_inc(s["wtr_sb"], 1)
                        else:
                            dve.tensor_copy(wba[:], src[:, :, 0:4 * GK]).then_inc(s["wtr_sb"], 1)
                    dve.wait_ge(s["nega"], 1)
                    dve.tensor_scalar(neg_a[:], neg_a[:], -1.0, None, ALU.mult).then_inc(s["nega"], 1)

                @block.scalar
                def _(act):
                    act.wait_ge(s["small_in"], 80)
                    act.activation(neg_a[:], neg_a[:], ACT.Exp).then_inc(s["nega"], 1)
            next_round()

        feats = [("k", h) for h in range(GK)] + [("q", h) for h in range(GK)] + [("v", h) for h in range(GV)]
        prods = feats[:2 * GK] + [("ba", cc) for cc in range(CPT)] + feats[2 * GK:] + [("z", i) for i in range(CPT * NB)]
        NP, NF = len(prods), len(feats)
        feat_of = {i: feats.index(p) for i, p in enumerate(prods) if p in feats}
        prod_of = {f: i for i, f in feat_of.items()}
        BA_DONE = 2 * GK + CPT
        N_TR = 2 * CPT + CPT * NB
        N_SILU = 4
        SERIES = 9
        N_GATE = SERIES + 12
        UPT = CPT * NB

        def product_steps(*kinds):
            steps, taps_left = [], []
            for i, (kind, _) in enumerate(prods):
                if kind in kinds:
                    steps += merged([("product", i, k) for k in range(KT)], taps_left)
                    taps_left = [("conv", feat_of[i], tap) for tap in range(TAPS)] if i in feat_of else []
            return steps + taps_left

        key_steps = product_steps("k", "q")
        mid_steps = merged(product_steps("ba", "v"), [("silu", 0), ("silu", 1), ("squares", 0), ("sums", 0), ("squares", 1), ("sums", 1), ("gates", 0), ("gates", 1)]
                           + [(kind, cc) for cc in range(CPT) for kind in ("keys", "keys back")])
        end_steps = merged(product_steps("z"), [("silu", 2), ("silu", 3)]) + [("values", m, cc) for m in range(NB) for cc in range(CPT)]
        tile_steps = key_steps + mid_steps + end_steps

        fills = [step for step in tile_steps if step[0] in ("sums", "keys", "keys back", "values") or step[0] == "product" and step[2] == 0]
        assert len(fills) % 2 == 0

        def tile_bank(*step):
            return bank[fills.index(step) % 2]

        def emptied(q, step):
            kind, *i = step
            if kind == "product":
                return s["pj_sb"], q * NP + i[0] + 1
            if kind == "sums":
                return s["ss_sb"], 2 * q + i[0] + 1
            if kind == "values":
                return s["v_sb"], q * UPT + i[0] * CPT + i[1] + 1
            return s["ktok_sb" if kind == "keys" else "kt_sb"], q * CPT + i[0] + 1

        def bank_for(pe, q, *step):
            n = q * len(fills) + fills.index(step) - 2
            if n >= 0:
                pe.wait_ge(*emptied(n // len(fills), fills[n % len(fills)]))
            return tile_bank(*step)

        def feature(par, kind, h):
            if kind == "k":
                return kraw[:, h, :]
            return qt[:, par, h, :] if kind == "q" else vraw[:, h, :]

        def pe_product(pe, q, par, i, k):
            kind, h = prods[i]
            n = q * NP + i
            if k == 0:
                if i == 0:
                    pe.wait_ge(s[f"x_in{par}"], 16 * (q // 2 + 1))
                bank_for(pe, q, "product", i, 0)
            b_p = tile_bank("product", i, 0)
            st = dict(start=(k == 0), stop=(k == KT - 1))
            if kind in "kqv":
                c = {"q": h * ROWS_K, "k": h * ROWS_K + P, "v": h // REP * ROWS_K + 2 * P + h % REP * P}[kind]
                j = pe.matmul(b_p[:, 0:WIN], wt[:, k, c:c + P], xtile[:, par, k, :], **st)
            elif kind == "z":
                cc, m = divmod(h, NB)
                w = wt[:, k, :].rearrange("p (h c) -> p h c", h=GK)[:, m * KPB:(m + 1) * KPB, 2 * P + REP * P:ROWS_K]
                j = pe.matmul(b_p[:], xtile[:, par, k, HALO + cc * P:HALO + (cc + 1) * P], w, **st)
            else:
                j = pe.matmul(b_p[:, 0:4 * GK], xtile[:, par, k, HALO + h * P:HALO + (h + 1) * P], wba[:, k, :], **st)
            if k == KT - 1:
                j.then_inc(s["pj_ps"], 1)

        def act_product(act, q, par, i):
            kind, h = prods[i]
            n, b_p = q * NP + i, tile_bank("product", i, 0)
            act.wait_ge(s["pj_ps"], n + 1)
            if kind in "kqv":
                f = feat_of[i]
                if q * NF + f >= 2:
                    act.wait_ge(s["cv"], q * NF + f - 1)
                act.activation(raw[:, f % 2, :], b_p[:, 0:WIN], ACT.Copy).then_inc(s["pj_sb"], 1)
            elif kind == "z":
                cc, m = divmod(h, NB)
                if q:
                    act.wait_ge(s["xf_sb"], q * UPT)
                act.activation(zs[:, par, cc, m * HEADS:(m + 1) * HEADS, :], b_p[:].rearrange("p (h c) -> p h c", h=HEADS), ACT.Silu).then_inc(s["pj_sb"], 1)
            else:
                act.activation(ba[:, h].rearrange("p k s r -> p (k s r)"), b_p[:, 0:4 * GK], ACT.Copy).then_inc(s["pj_sb"], 1)

        def dve_conv(dve, q, par, i, tap):
            kind, h = feats[i]
            n = q * NF + i
            acc, src = feature(par, kind, h), raw[:, i % 2, tap:tap + TILE]
            done = ("cv1", "cv2", "cv3", "cv")
            if tap:
                dve.wait_ge(s[done[tap - 1]], n + 1)
                dve.scalar_tensor_tensor(out=acc, in0=src, scalar=taps[:, i, tap:tap + 1], in1=acc, op0=ALU.mult, op1=ALU.add).then_inc(s[done[tap]], 1)
                return
            if q and h == 0:
                if kind == "k":
                    dve.wait_ge(s["sq_sb"], 2 * q - 1)
                    dve.wait_ge(s["tr_ps"], (q - 1) * N_TR + 2 * CPT)
                elif kind == "q":
                    dve.wait_ge(s["qs_ps"], q * UPT)
                    dve.wait_ge(s["kq_ps"], q * UPT)
                else:
                    dve.wait_ge(s["tr_ps"], q * N_TR)
            dve.wait_ge(s["pj_sb"], q * NP + prod_of[i] + 1)
            dve.tensor_scalar(acc, src, taps[:, i, 0:1], None, ALU.mult).then_inc(s["cv1"], 1)

        def act_silu(act, q, par, j):
            a, upto = ((kraw[:], GK), (qt[:, par], 2 * GK), (vraw[:, 0:HEADS], 2 * GK + HEADS), (vraw[:, HEADS:GV], NF))[j]
            act.wait_ge(s["cv"], q * NF + upto)
            act.activation(a, a, ACT.Silu).then_inc(s["silu"], 1)

        def pool_squares(pool, q, par, j):
            pool.wait_ge(s["silu"], q * N_SILU + j + 1)
            if q or j:
                pool.wait_ge(s["ss_ps"], 2 * q + j)
            a = qt[:, par] if j else kraw[:]
            pool.tensor_tensor(sq[:], a, a, ALU.mult).then_inc(s["sq_sb"], 1)

        def pe_squares(pe, q, j):
            pe.wait_ge(s["sq_sb"], 2 * q + j + 1)
            b_tr = bank_for(pe, q, "sums", j)
            for cc in range(CPT):
                for h in range(GK):
                    m = pe.matmul(b_tr[:, cc * GK + h:cc * GK + h + 1], sq[:, h, cc * P:(cc + 1) * P], ones[:, 0:1], start=True, stop=True)
            m.then_inc(s["ss_ps"], 1)

        def dve_squares(dve, q, par, j):
            b_tr = tile_bank("sums", j)
            dve.wait_ge(s["ss_ps"], 2 * q + j + 1)
            dve.tensor_scalar(rn[:, par, :, j * GK:(j + 1) * GK], b_tr[:, 0:CPT * GK].rearrange("p (c h) -> p c h", c=CPT), L2_EPS, None, ALU.add).then_inc(s["ss_sb"], 1)

        def pool_norms(pool, q, par, j):
            pool.wait_ge(s["ss_sb"], 2 * q + j + 1)
            r = rn[:, par, :, j * GK:(j + 1) * GK]
            pool.tensor_tensor(r, r, mhalf[:, 0:CPT * GK].rearrange("p (c h) -> p c h", c=CPT), ALU.pow).then_inc(s["rn_sb"], 1)

        def dve_qscale(dve, q, par):
            dve.wait_ge(s["rn_sb"], 3 * q + 2)
            r = rn[:, par, :, GK:2 * GK]
            dve.tensor_scalar(r, r, SCALE, None, ALU.mult).then_inc(s["rn_sb"], 1)

        def pe_keys(pe, q, par, cc):
            pe.wait_ge(s["silu"], q * N_SILU + 1)
            b_tr = bank_for(pe, q, "keys", cc)
            for h in range(GK):
                t = pe.transpose(b_tr[:, h * P:(h + 1) * P], kraw[:, h, cc * P:(cc + 1) * P], ident)
            t.then_inc(s["tr_ps"], 1)

        def pe_keys_back(pe, q, par, cc):
            pe.wait_ge(s["ktok_sb"], q * CPT + cc + 1)
            b_tr = bank_for(pe, q, "keys back", cc)
            for h in range(GK):
                t = pe.transpose(b_tr[:, h * P:(h + 1) * P], ktok[:, par, cc, h, :], ident)
            t.then_inc(s["tr_ps"], 1)

        def dve_keys(dve, q, par, cc):
            b_tr = tile_bank("keys", cc)
            dve.wait_ge(s["tr_ps"], q * N_TR + 2 * cc + 1)
            dve.wait_ge(s["rn_sb"], 3 * q + 1)
            if q:
                dve.wait_ge(s["kend_sb"], q * UPT)
            dve.tensor_tensor(ktok[:, par, cc], b_tr[:].rearrange("p (h c) -> p h c", h=GK),
                              rn[:, par, cc, 0:GK].unsqueeze(2).broadcast_to([P, GK, P]), ALU.mult).then_inc(s["ktok_sb"], 1)

        def act_keys(act, q, par, cc):
            b_tr = tile_bank("keys back", cc)
            act.wait_ge(s["tr_ps"], q * N_TR + 2 * cc + 2)
            if q:
                act.wait_ge(s["qs_ps"], q * UPT)
            act.activation(kt[:, par, :, cc * P:(cc + 1) * P], b_tr[:].rearrange("p (h c) -> p h c", h=GK), ACT.Copy).then_inc(s["kt_sb"], 1)

        def pe_values(pe, q, m, cc):
            pe.wait_ge(s["silu"], q * N_SILU + 3 + m)
            b_tr = bank_for(pe, q, "values", m, cc)
            for h in range(HEADS):
                t = pe.transpose(b_tr[:, h * P:(h + 1) * P], vraw[:, m * HEADS + h, cc * P:(cc + 1) * P], ident)
            t.then_inc(s["tr_ps"], 1)

        def act_values(act, q, par, m, cc):
            b_tr = tile_bank("values", m, cc)
            act.wait_ge(s["tr_ps"], q * N_TR + 2 * CPT + m * CPT + cc + 1)
            if q:
                act.wait_ge(s["r_sb"], q * UPT)
            act.activation(vtok[:, par, cc, m * HEADS:(m + 1) * HEADS, :], b_tr[:].rearrange("p (h c) -> p h c", h=HEADS), ACT.Copy).then_inc(s["v_sb"], 1)

        def act_gates(act, q):
            act.wait_ge(s["gt_sb"], q * N_GATE + 3)
            act.activation(bneg[:], bneg[:], ACT.Exp).then_inc(s["gt_exp"], 1)
            act.activation(yneg[:], yneg[:], ACT.Exp).then_inc(s["gt_exp"], 1)

        def dve_gates(dve, q, par, part):
            done = [q * N_GATE + (3 if part else 0)]

            def link(ins):
                ins.then_inc(s["gt_sb"], 1)
                done[0] += 1
                dve.wait_ge(s["gt_sb"], done[0])

            by_key = lambda a: a.rearrange("p c (k r) -> p c k r", r=REP)
            per_head = lambda a: a.unsqueeze(1).broadcast_to([P, CPT, GV])
            if part == 0:
                dve.wait_ge(s["pj_sb"], q * NP + BA_DONE)
                link(dve.tensor_scalar(by_key(bneg[:]), ba[:, :, :, 0, :], -1.0, 85.0, ALU.mult, ALU.min))
                for r in range(CPT):
                    ins = dve.tensor_tensor(ypos[:, r, :].rearrange("p (k r) -> p k r", r=REP), ba[:, r, :, 1, :], dtb[:].rearrange("p (k r) -> p k r", r=REP), ALU.add)
                link(ins)
                link(dve.scalar_tensor_tensor(out=yneg[:], in0=ypos[:], scalar=-1.0, in1=ypos[:], op0=ALU.mult, op1=ALU.min))
                return
            bt, gd = beta[:, par], gdec[:, par]
            if q:
                dve.wait_ge(s["gm_sb"], q * UPT)
                dve.wait_ge(s["gc_ps"], q * CPT)
            dve.wait_ge(s["gt_exp"], 2 * q + 2)
            link(dve.tensor_scalar(bneg[:], bneg[:], 1.0, None, ALU.add))
            link(dve.reciprocal(bt, bneg[:]))
            link(dve.tensor_scalar(ratio[:], yneg[:], 2.0, None, ALU.add))
            link(dve.reciprocal(ratio[:], ratio[:]))
            link(dve.tensor_tensor(ratio[:], ratio[:], yneg[:], ALU.mult))
            link(dve.tensor_tensor(ratio2[:], ratio[:], ratio[:], ALU.mult))
            link(dve.tensor_scalar(gd, ratio2[:], 1.0 / (2 * SERIES - 1), None, ALU.mult))
            for i in range(SERIES - 2, 0, -1):
                link(dve.scalar_tensor_tensor(out=gd, in0=gd, scalar=1.0 / (2 * i + 1), in1=ratio2[:], op0=ALU.add, op1=ALU.mult))
            link(dve.scalar_tensor_tensor(out=gd, in0=gd, scalar=1.0, in1=ratio[:], op0=ALU.add, op1=ALU.mult))
            link(dve.tensor_scalar(ypos[:], ypos[:], 0.0, None, ALU.max))
            link(dve.scalar_tensor_tensor(out=gd, in0=gd, scalar=2.0, in1=ypos[:], op0=ALU.mult, op1=ALU.add))
            link(dve.tensor_tensor(gd, gd, per_head(neg_a[:]), ALU.mult))
            assert done[0] == (q + 1) * N_GATE

        def pe_tile(pe, q, par, step):
            kind, *i = step
            if kind == "product":
                pe_product(pe, q, par, *i)
            elif kind == "sums":
                pe_squares(pe, q, *i)
            elif kind == "keys":
                pe_keys(pe, q, par, *i)
            elif kind == "keys back":
                pe_keys_back(pe, q, par, *i)
            elif kind == "values":
                pe_values(pe, q, *i)

        def act_tile(act, q, par, step):
            kind, *i = step
            if kind == "product":
                if i[1] == KT - 1:
                    act_product(act, q, par, i[0])
            elif kind == "silu":
                act_silu(act, q, par, *i)
            elif kind == "gates" and i[0] == 0:
                act_gates(act, q)
            elif kind == "keys back":
                act_keys(act, q, par, *i)
            elif kind == "values":
                act_values(act, q, par, *i)

        def dve_tile(dve, q, par, step):
            kind, *i = step
            if kind == "conv":
                dve_conv(dve, q, par, *i)
            elif kind == "sums":
                dve_squares(dve, q, par, *i)
                if i[0]:
                    dve_qscale(dve, q, par)
            elif kind == "gates":
                dve_gates(dve, q, par, *i)
            elif kind == "keys":
                dve_keys(dve, q, par, *i)

        def pool_tile(pool, q, par, step):
            kind, *i = step
            if kind == "squares":
                pool_squares(pool, q, par, *i)
            elif kind == "sums":
                pool_norms(pool, q, par, *i)

        def load_tile(sp, q, par, column):
            if q >= 2:
                sp.wait_ge(s["pj_ps"], (q - 1) * NP)
                sp.wait_ge(s[f"x_in{par}"], 16 * (q // 2))
            sp.dma_start(xtile[:, par], xt_d[:, :, bass.ds(column, WIN)]).then_inc(s[f"x_in{par}"], 16)

        def where(n):
            c, m = divmod(n, NB)
            return c, m, c // CPT, c % CPT

        def unit_heads(m):
            return slice(m * HEADS, (m + 1) * HEADS)

        quad = lambda b: b[:].rearrange("p (h c) -> p h c", h=HEADS)
        ident16 = mask[:, M_ID, :]

        def pe_gate(pe, c):
            tile, cc = divmod(c, CPT)
            if c:
                pe.wait_ge(s["gam_sb"], NB * c)
            if tile:
                pe.wait_ge(s["gt_sb"], tile * N_GATE)
            for i, a in enumerate((le, gt, ones)):
                j = pe.matmul(b_a[:, i * GV:(i + 1) * GV], a, gdec[:, tile % 2, cc, :], start=True, stop=True)
            j.then_inc(s["gc_ps"], 1)

        def act_gate(act, c):
            act.wait_ge(s["gc_ps"], c + 1)
            if c >= 2:
                act.wait_ge(s["s_sb"], NB * (c - 1))
                act.wait_ge(s["gs_sb"], 3 * (c - 1))
            act.activation(gex[:, c % 2].rearrange("p a h -> p (a h)"), b_a[:, 0:3 * GV], ACT.Exp).then_inc(s["gc_sb"], 1)

        def dve_gate(dve, c):
            tile, cc = divmod(c, CPT)
            dve.wait_ge(s["gc_sb"], c + 1)
            if tile:
                dve.wait_ge(s["rn_sb"], 3 * tile)
            if c >= 2:
                dve.wait_ge(s["t_sb"], NB * (c - 1))
                dve.wait_ge(s["kend_sb"], NB * (c - 1))
                dve.wait_ge(s["r_sb"], NB * (c - 1))
            p = c % 2
            dve.tensor_scalar(ngam[:, p], gex[:, p, 0], -1.0, None, ALU.mult).then_inc(s["gs_sb"], 1)
            dve.tensor_tensor(gamq[:, p].rearrange("p (k r) -> p k r", r=REP), gex[:, p, 0].rearrange("p (k r) -> p k r", r=REP),
                              rn[:, tile % 2, cc, GK:2 * GK].unsqueeze(2).broadcast_to([P, GK, REP]), ALU.mult).then_inc(s["gs_sb"], 1)
            dve.tensor_tensor(bend[:, p], gex[:, p, 1], beta[:, tile % 2, cc], ALU.mult).then_inc(s["gs_sb"], 1)

        def pool_decay(pool, n):
            c, m, tile, cc = where(n)
            if n:
                pool.wait_ge(s["gam_ps"], n)
            if tile:
                pool.wait_ge(s["gt_sb"], tile * N_GATE)
            pool.tensor_tensor(gm[:], le.unsqueeze(1).broadcast_to([P, HEADS, P]),
                               gdec[:, tile % 2, cc, unit_heads(m)].unsqueeze(2).broadcast_to([P, HEADS, P]), ALU.mult).then_inc(s["gm_sb"], 1)

        def pe_scores(pe, n):
            c, m, tile, cc = where(n)
            if m == 0:
                pe.wait_ge(s["gc_sb"], c + 1)
            else:
                pe.wait_ge(s["gam_sb"], n)
            if tile:
                pe.wait_ge(s["kt_sb"], tile * CPT)
                pe.wait_ge(s["silu"], (tile - 1) * N_SILU + 2)
            t = slice(cc * P, (cc + 1) * P)
            for j in range(KPB):
                h = m * KPB + j
                pe.matmul(b_a[:, j * P:(j + 1) * P], kt[:, tile % 2, h, t], kt[:, tile % 2, h, t], start=True, stop=True)
                i = pe.matmul(b_a[:, (KPB + j) * P:(KPB + j + 1) * P], kt[:, tile % 2, h, t], qt[:, tile % 2, h, t], start=True, stop=True)
            i.then_inc(s["kq_ps"], 1)

        def dve_scores(dve, n):
            dve.wait_ge(s["kq_ps"], n + 1)
            if n:
                dve.wait_ge(s["lt_sb"], n)
                dve.wait_ge(s["pt_sb"], n)
            dve.tensor_tensor(kqm[:], b_a[:].rearrange("p (h c) -> p h c", h=2 * KPB), mask[:, M_LT:M_LT + 2 * KPB, :], ALU.mult).then_inc(s["kq_sb"], 1)

        def pe_decay(pe, n):
            pe.wait_ge(s["kq_sb"], n + 1)
            pe.wait_ge(s["gm_sb"], n + 1)
            pe.matmul(b_a[:], gt, gm[:].rearrange("p h c -> p (h c)"), start=True, stop=True).then_inc(s["gam_ps"], 1)

        def act_decay(act, n):
            act.wait_ge(s["gam_ps"], n + 1)
            if n:
                act.wait_ge(s["pt_sb"], n)
                act.wait_ge(s["lt_sb"], n)
            act.activation(gam[:], quad(b_a), ACT.Exp).then_inc(s["gam_sb"], 1)

        def dve_matrices(dve, n):
            c, m, tile, cc = where(n)
            dve.wait_ge(s["gam_sb"], n + 1)
            dve.wait_ge(s["kq_sb"], n + 1)
            if n:
                dve.wait_ge(s["ltl_sb"], n)
            for h in range(HEADS):
                b = beta[:, tile % 2, cc, m * HEADS + h:m * HEADS + h + 1]
                i = dve.scalar_tensor_tensor(out=ltm[:, h], in0=gam[:, h], scalar=b, in1=kqm[:, h // REP], op0=ALU.mult, op1=ALU.mult)
            i.then_inc(s["lt_sb"], 1)
            if n >= PIPE:
                dve.wait_ge(s["o_ps"], n - PIPE + 1)
            for h in range(HEADS):
                b = beta[:, tile % 2, cc, m * HEADS + h:m * HEADS + h + 1]
                i = dve.scalar_tensor_tensor(out=pt[:, n % PIPE, h], in0=gam[:, h], scalar=b, in1=kqm[:, KPB + h // REP], op0=ALU.mult, op1=ALU.mult)
            i.then_inc(s["pt_sb"], 1)

        def pool_matrices(pool, n):
            pool.wait_ge(s["lt_sb"], n + 1)
            pool.tensor_tensor(ltm[:], ltm[:], mask[:, M_NEG, :].unsqueeze(1).broadcast_to([P, HEADS, P]), ALU.subtract).then_inc(s["lti_sb"], 1)
            pool.wait_ge(s["lth_sb"], n + 1)
            if n >= 2:
                for j in range(HALVES):
                    pool.wait_ge(s[f"er_ps{j}"], n - 1)
            pool.tensor_tensor(ltl[:, n % 2], ltm[:], lth[:, n % 2], ALU.subtract).then_inc(s["ltl_sb"], 1)

        def act_matrices(act, n):
            act.wait_ge(s["lti_sb"], n + 1)
            if n >= 2:
                for j in range(HALVES):
                    act.wait_ge(s[f"er_ps{j}"], n - 1)
                    act.wait_ge(s[f"y1_sb{j}"], n - 1)
                act.wait_ge(s["ltl_sb"], n - 1)
            act.activation(lth[:, n % 2], ltm[:], ACT.Copy).then_inc(s["lth_sb"], 1)

        def pool_kend(pool, n):
            c, m, tile, cc = where(n)
            pool.wait_ge(s["gs_sb"], 3 * (c + 1))
            if n >= 2:
                pool.wait_ge(s["su_ps"], n - 1)
            if tile:
                pool.wait_ge(s["ktok_sb"], tile * CPT)
            for r in range(KPB):
                h = m * HEADS + r * REP
                i = pool.tensor_tensor(kend[:, n % 2, r * REP:(r + 1) * REP], ktok[:, tile % 2, cc, m * KPB + r].unsqueeze(1).broadcast_to([P, REP, P]),
                                       bend[:, c % 2, h:h + REP].unsqueeze(2).broadcast_to([P, REP, P]), ALU.mult)
            i.then_inc(s["kend_sb"], 1)

        b_inv = (b_i0, b_i1)
        left = lambda j: b_inv[j][:, 0:HALF * P]
        right = lambda j: b_inv[j][:, HALF * P:2 * HALF * P]
        pair = lambda a: a.rearrange("p (h c) -> p h c", h=HALF)
        both = lambda i: mask[:, i, :].unsqueeze(1).broadcast_to([P, HALF, P])
        half_heads = lambda j: slice(j * HALF, (j + 1) * HALF)

        def at_level(n, lv):
            return LEVELS * n + lv + 1

        def at_merge(n, lv):
            return (LEVELS - 1) * n + lv

        def each_head(pe, dst, lhsT, rhs, done=None, start=True, stop=True):
            for h in range(HALF):
                i = pe.matmul(dst[:, h * P:(h + 1) * P], lhsT(h), rhs(h), start=start and h == 0, stop=stop, skip_group_check=True)
            if done:
                i.then_inc(s[done], 1)

        def pe_level(pe, n, j, lv):
            if lv == 0:
                pe.wait_ge(s["lth_sb"], n + 1)
                if n:
                    pe.wait_ge(s[f"yf_sb{j}"], n)
            elif lv == 1:
                pe.wait_ge(s[f"w_sb{j}"], at_level(n, 0))
            else:
                pe.wait_ge(s[f"xy_sb{j}"], at_merge(n, lv - 1))
            each_head(pe, left(j), lambda h: lth[:, n % 2, j * HALF + h], lambda h: xyinv[:, j, 0, h] if lv else ident16, f"w_ps{j}")

        def pe_merge(pe, n, j, lv):
            pe.wait_ge(s[f"w_sb{j}"], at_level(n, lv))
            if lv == 1:
                pe.wait_ge(s[f"y1_sb{j}"], n + 1)
            each_head(pe, left(j), lambda h: xyinv[:, j, 1, h], lambda h: winv[:, j, h], start=True, stop=True)
            each_head(pe, right(j), lambda h: winv[:, j, h], lambda h: xyinv[:, j, 1, h], f"xy_ps{j}", start=True, stop=True)

        def dve_level(dve, n, j, lv):
            if lv == 0:
                dve.wait_ge(s["lth_sb"], n + 1)
                if n:
                    dve.wait_ge(s[f"c3_ps{j}"], n)
                dve.tensor_tensor(xyinv[:, j, 1], lth[:, n % 2, half_heads(j)], both(M_L0T), ALU.mult).then_inc(s[f"y1_sb{j}"], 1)
            dve.wait_ge(s[f"w_ps{j}"], at_level(n, lv))
            dve.tensor_tensor(winv[:, j] if lv else xyinv[:, j, 0], pair(left(j)), both(M_L + lv), ALU.mult).then_inc(s[f"w_sb{j}"], 1)

        def act_merge(act, n, j, lv):
            act.wait_ge(s[f"xy_ps{j}"], at_merge(n, lv))
            act.activation(xyinv[:, j].rearrange("p a h c -> p (a h c)"), b_inv[j][:], ACT.Copy).then_inc(s[f"xy_sb{j}"], 1)

        def pe_error(pe, n, j):
            pe.wait_ge(s[f"xy_sb{j}"], at_merge(n, LEVELS - 1))
            pe.wait_ge(s["ltl_sb"], n + 1)
            each_head(pe, left(j), lambda h: ident16, lambda h: mask[:, M_NEG, :], start=True, stop=False)
            each_head(pe, left(j), lambda h: lth[:, n % 2, j * HALF + h], lambda h: xyinv[:, j, 0, h], start=False, stop=False)
            each_head(pe, left(j), lambda h: ltl[:, n % 2, j * HALF + h], lambda h: xyinv[:, j, 0, h], f"er_ps{j}", start=False, stop=True)

        def act_error(act, n, j):
            act.wait_ge(s[f"er_ps{j}"], n + 1)
            if n:
                act.wait_ge(s[f"c3_ps{j}"], n)
                act.wait_ge(s[f"el_sb{j}"], n)
            act.activation(errh[:, half_heads(j)], pair(left(j)), ACT.Copy).then_inc(s[f"eh_sb{j}"], 1)

        def dve_error(dve, n, j):
            dve.wait_ge(s[f"eh_sb{j}"], n + 1)
            if n:
                dve.wait_ge(s[f"c1_ps{j}"], n)
            dve.tensor_tensor(errl[:, j], pair(left(j)), errh[:, half_heads(j)], ALU.subtract).then_inc(s[f"el_sb{j}"], 1)

        def pe_first(pe, n, j):
            pe.wait_ge(s[f"el_sb{j}"], n + 1)
            each_head(pe, right(j), lambda h: errh[:, j * HALF + h], lambda h: xyinv[:, j, 1, h], start=True, stop=False)
            each_head(pe, right(j), lambda h: errl[:, j, h], lambda h: xyinv[:, j, 1, h], f"c1_ps{j}", start=False, stop=True)

        def act_first(act, n, j):
            act.wait_ge(s[f"c1_ps{j}"], n + 1)
            if n:
                act.wait_ge(s[f"c2_ps{j}"], n)
                act.wait_ge(s[f"c2_sb{j}"], n)
            act.activation(cor1[:, j], pair(right(j)), ACT.Copy, scale=-1.0 / SCALED).then_inc(s[f"c1_sb{j}"], 1)

        def pe_second(pe, n, j):
            pe.wait_ge(s[f"c1_sb{j}"], n + 1)
            each_head(pe, left(j), lambda h: errh[:, j * HALF + h], lambda h: cor1[:, j, h], f"c2_ps{j}", start=True, stop=True)

        def dve_second(dve, n, j):
            dve.wait_ge(s[f"c2_ps{j}"], n + 1)
            if n:
                dve.wait_ge(s[f"c3_ps{j}"], n)
            dve.scalar_tensor_tensor(out=cor2[:, half_heads(j)], in0=pair(left(j)), scalar=-1.0 / SCALED, in1=cor1[:, j],
                                     op0=ALU.mult, op1=ALU.add).then_inc(s[f"c2_sb{j}"], 1)

        def pe_third(pe, n, j):
            pe.wait_ge(s[f"c2_sb{j}"], n + 1)
            each_head(pe, right(j), lambda h: mask[:, M_NEG, :], lambda h: xyinv[:, j, 1, h], stop=False)
            each_head(pe, right(j), lambda h: errh[:, j * HALF + h], lambda h: xyinv[:, j, 1, h], start=False, stop=False)
            each_head(pe, right(j), lambda h: errl[:, j, h], lambda h: xyinv[:, j, 1, h], start=False, stop=False)
            each_head(pe, right(j), lambda h: errh[:, j * HALF + h], lambda h: cor2[:, j * HALF + h], f"c3_ps{j}", start=False)

        def act_third(act, n, j):
            act.wait_ge(s[f"c3_ps{j}"], n + 1)
            if n >= 2:
                act.wait_ge(s["e_ps"], n - 1)
            act.activation(yfin[:, n % 2, half_heads(j)], pair(right(j)), ACT.Copy, scale=-1.0 / SCALED).then_inc(s[f"yf_sb{j}"], 1)

        def pe_recall(pe, n):
            c, m, tile, cc = where(n)
            if n == 0:
                pe.wait_ge(s["s_set"], 1)
            else:
                pe.wait_ge(s["s_sb"], n)
            for j in range(KPB):
                h = m * KPB + j
                i = pe.matmul(b_s0[:, j * REP * P:(j + 1) * REP * P], kt[:, tile % 2, h, cc * P:(cc + 1) * P], state[:, h * REP:(h + 1) * REP, :], start=True, stop=True)
            i.then_inc(s["ks_ps"], 1)

        def dve_recall(dve, n):
            c, m, tile, cc = where(n)
            dve.wait_ge(s["ks_ps"], n + 1)
            dve.wait_ge(s["gs_sb"], 3 * (c + 1))
            if n:
                dve.wait_ge(s["o_ps"], n)
            if tile:
                dve.wait_ge(s["v_sb"], tile * UPT)
            for h in range(HEADS):
                v = m * HEADS + h
                i = dve.scalar_tensor_tensor(out=reps[:, h], in0=b_s0[:, h * P:(h + 1) * P], scalar=ngam[:, c % 2, v:v + 1],
                                             in1=vtok[:, tile % 2, cc, v], op0=ALU.mult, op1=ALU.add)
            i.then_inc(s["r_sb"], 1)

        def pe_query(pe, n):
            c, m, tile, cc = where(n)
            if n:
                pe.wait_ge(s["s_sb"], n)
                pe.wait_ge(s["o_sb"], n)
            for j in range(KPB):
                h = m * KPB + j
                i = pe.matmul(b_s1[:, j * REP * P:(j + 1) * REP * P], qt[:, tile % 2, h, cc * P:(cc + 1) * P], state[:, h * REP:(h + 1) * REP, :], start=True, stop=True)
            i.then_inc(s["qs_ps"], 1)

        def act_query(act, n):
            c, m, tile, cc = where(n)
            act.wait_ge(s["qs_ps"], n + 1)
            act.wait_ge(s["gs_sb"], 3 * (c + 1))
            if n >= 2:
                act.wait_ge(s["xt_ps"], n - 1)
            for h in range(HEADS):
                v = m * HEADS + h
                i = act.activation(tq[:, n % 2, h], b_s1[:, h * P:(h + 1) * P], ACT.Identity, scale=gamq[:, c % 2, v:v + 1])
            i.then_inc(s["t_sb"], 1)

        def pe_eps(pe, n):
            pe.wait_ge(s["r_sb"], n + 1)
            for j in range(HALVES):
                pe.wait_ge(s[f"yf_sb{j}"], n + 1)
            for h in range(HEADS):
                i = pe.matmul(b_s0[:, h * P:(h + 1) * P], yfin[:, n % 2, h], reps[:, h], start=True, stop=True)
            i.then_inc(s["e_ps"], 1)

        def act_eps(act, n):
            act.wait_ge(s["e_ps"], n + 1)
            act.activation(reps[:], quad(b_s0), ACT.Copy).then_inc(s["e_sb"], 1)

        def pe_learn(pe, n):
            pe.wait_ge(s["e_sb"], n + 1)
            pe.wait_ge(s["kend_sb"], n + 1)
            for h in range(HEADS):
                i = pe.matmul(b_s0[:, h * P:(h + 1) * P], kend[:, n % 2, h], reps[:, h], start=True, stop=True)
            i.then_inc(s["su_ps"], 1)

        def dve_learn(dve, n):
            c, m, tile, cc = where(n)
            dve.wait_ge(s["su_ps"], n + 1)
            dve.wait_ge(s["qs_ps"], n + 1)
            for h in range(HEADS):
                v = m * HEADS + h
                i = dve.scalar_tensor_tensor(out=state[:, v], in0=state[:, v], scalar=gex[:, c % 2, 2, v:v + 1], in1=b_s0[:, h * P:(h + 1) * P],
                                             op0=ALU.mult, op1=ALU.add)
            i.then_inc(s["s_sb"], 1)

        def pe_answer(pe, n):
            pe.wait_ge(s["e_sb"], n + 1)
            pe.wait_ge(s["t_sb"], n + 1)
            pe.wait_ge(s["pt_sb"], n + 1)
            for h in range(HEADS):
                i = pe.matmul(b_s1[:, h * P:(h + 1) * P], pt[:, n % PIPE, h], reps[:, h], start=True, stop=True)
            i.then_inc(s["o_ps"], 1)

        def dve_answer(dve, n):
            c, m, tile, cc = where(n)
            dve.wait_ge(s["o_ps"], n + 1)
            dve.wait_ge(s["t_sb"], n + 1)
            for j in range(KPB):
                h = slice(j * REP, (j + 1) * REP)
                i = dve.scalar_tensor_tensor(out=tq[:, n % 2, h], in0=quad(b_s1)[:, h], scalar=rn[:, tile % 2, cc, GK + m * KPB + j:GK + m * KPB + j + 1], in1=tq[:, n % 2, h],
                                             op0=ALU.mult, op1=ALU.add)
            i.then_inc(s["o_sb"], 1)

        def pool_gate_out(pool, n):
            c, m, tile, cc = where(n)
            pool.wait_ge(s["o_sb"], n + 1)
            if tile:
                pool.wait_ge(s["pj_sb"], tile * NP)
            pool.tensor_tensor(tq[:, n % 2], tq[:, n % 2], zs[:, tile % 2, cc, unit_heads(m)], ALU.mult).then_inc(s["xf_sb"], 1)

        def act_squares(act, n):
            act.wait_ge(s["xf_sb"], n + 1)
            if n:
                act.wait_ge(s["rm1_sb"], n)
                act.wait_ge(s["sn_sb"], n)
            for h in range(HEADS):
                i = act.activation(osq[:, h], tq[:, n % 2, h], ACT.Square, accum_out=ssq[:, h:h + 1])
            i.then_inc(s["sn_sb"], 1)

        def pool_rms(pool, n):
            pool.wait_ge(s["sn_sb"], n + 1)
            if n:
                pool.wait_ge(s["xn_sb"], n)
            pool.tensor_scalar(rms[:], ssq[:], 1.0 / P, RMS_EPS, ALU.mult, ALU.add).then_inc(s["rm1_sb"], 1)
            pool.wait_ge(s["rm1_sb"], n + 1)
            pool.tensor_tensor(rms[:], rms[:], mhalf[:, 0:HEADS], ALU.pow).then_inc(s["rm_sb"], 1)
            pool.wait_ge(s["rm_sb"], n + 1)
            pool.tensor_tensor(tq[:, n % 2], tq[:, n % 2], rms[:].unsqueeze(2).broadcast_to([P, HEADS, P]), ALU.mult).then_inc(s["xn_sb"], 1)

        def pe_turn(pe, n):
            pe.wait_ge(s["xn_sb"], n + 1)
            if n:
                pe.wait_ge(s["xt_sb"], n)
            if n >= NB and n % NB == 0:
                pe.wait_ge(s["po_sb"], n // NB)
            for h in range(HEADS):
                i = pe.transpose(b_o[:, h * P:(h + 1) * P], tq[:, n % 2, h], ident)
            i.then_inc(s["xt_ps"], 1)

        def act_turn(act, n):
            c, m, tile, cc = where(n)
            act.wait_ge(s["xt_ps"], n + 1)
            if c:
                act.wait_ge(s["out_ps"], c)
            act.activation(xnt[:, unit_heads(m)], quad(b_o), ACT.Identity, scale=nw[:, 0:1]).then_inc(s["xt_sb"], 1)

        def pe_out(pe, c, h):
            if h == 0:
                pe.wait_ge(s["xt_sb"], NB * (c + 1))
            i = pe.matmul(b_o[:], xnt[:, h], wot[:, h], start=(h == 0), stop=(h == GV - 1))
            if h == GV - 1:
                i.then_inc(s["out_ps"], 1)

        def dve_out(dve, c):
            dve.wait_ge(s["out_ps"], c + 1)
            dve.wait_ge(s["rows_in"], 48 * (c + 1))
            if c:
                dve.wait_ge(s["stored"], 32 * c)
                dve.wait_ge(s["yo_sb"], c)
            dve.tensor_tensor(pout[:], b_o[:], prow[:], ALU.add).then_inc(s["po_sb"], 1)

        def pool_out(pool, c):
            pool.wait_ge(s["po_sb"], c + 1)
            if c:
                pool.wait_ge(s["stored"], 32 * c)
            pool.tensor_tensor(yout[:], pout[:], grow[:], ALU.mult).then_inc(s["yg_sb"], 1)
            pool.wait_ge(s["yg_sb"], c + 1)
            pool.tensor_tensor(yout[:], yout[:], xrow[:], ALU.add).then_inc(s["yo_sb"], 1)

        def store(sp, c, row):
            sp.dma_start(part_d[bass.ds(row + c * P, P), :], pout[:]).then_inc(s["stored"], 16)
            sp.dma_start(out[bass.ds(row + c * P, P), :], yout[:]).then_inc(s["stored"], 16)

        def build_steps(n):
            c, m = divmod(n, NB)
            return ([("gate", c)] if m == 0 else []) + [("scores", n), ("decay", n), ("matrices", n)]

        def invert_steps(n, j):
            steps = [("level", n, j, 0)]
            for lv in range(1, LEVELS):
                steps += [("level", n, j, lv), ("merge", n, j, lv)]
            return steps + [(kind, n, j) for kind in ("error", "first", "second", "third")]

        def core_steps(n):
            return [("kend", n), ("recall", n), ("query", n), ("eps", n), ("learn", n), ("answer", n)]

        def out_steps(n):
            c, m = divmod(n, NB)
            return [("gated", n), ("norm", n), ("turn", n)] + ([("out", c, h) for h in range(GV)] if m == NB - 1 else [])

        lengths = {
            "gate": [("pe", 0.10), ("act", 0.31), ("dve", 0.46)], "scores": [("pe", 0.85), ("dve", 0.66)], "decay": [("pool", 1.53), ("pe", 0.92), ("act", 0.75)],
            "matrices": [("dve", 1.86), ("pool", 1.23), ("act", 0.49), ("pool", 1.28)], "kend": [("pool", 2.58)],
            "level": [("pe", 0.11), ("dve", 0.34)], "merge": [("pe", 0.19), ("act", 0.59)], "error": [("pe", 0.36), ("act", 0.41), ("dve", 0.39)],
            "first": [("pe", 0.21), ("act", 0.28)], "second": [("pe", 0.09), ("dve", 0.36)], "third": [("pe", 0.20), ("act", 0.34)],
            "recall": [("pe", 0.81), ("dve", 1.16)], "query": [("pe", 0.89), ("act", 1.11)], "eps": [("pe", 0.96), ("act", 0.71)],
            "learn": [("pe", 0.83), ("dve", 1.20)], "answer": [("pe", 0.95), ("dve", 0.83)], "gated": [("pool", 1.24)], "norm": [("act", 1.32), ("pool", 2.81)], "turn": [("pe", 0.43), ("act", 0.73)],
        }

        def length(step):
            kind, *i = step
            if kind == "out":
                return [("pe", 0.85)] + ([("dve", 0.59), ("pool", 2.84)] if i[1] == GV - 1 else [])
            if kind != "tile":
                return lengths[kind]
            kind, *i = i[1]
            if kind == "product":
                what = prods[i[0]][0]
                pe = [("pe", {"z": .9, "ba": .1}.get(what, .45))]
                return pe + ({"z": [("act", 0.74)], "ba": [("act", 0.23)]}.get(what, [("act", 0.42)]) if i[1] == KT - 1 else [])
            return {"conv": [("dve", 0.38)], "silu": [("act", 2.96)], "squares": [("pool", 2.40)], "sums": [("pe", 0.82), ("dve", 0.17), ("pool", 1.54)],
                    "keys": [("pe", 0.36), ("dve", 0.63)], "keys back": [("pe", 0.43), ("act", 0.59)],
                    "values": [("pe", 0.42), ("act", 0.62)], "gates": [("dve", 0.30), ("act", 0.64)] if i[0] == 0 else [("dve", 2.54)]}[kind]

        def needs(step):
            kind, *i = step
            n = i[0]
            units = lambda *pairs: [(kind, u) for kind, u in pairs if u >= 0]
            if kind == "gate":
                return units(("answer", NB * (n - 1) - 1), ("learn", NB * (n - 1) - 1)) + ([("tile", n // CPT - 1, mid_steps[-1])] if n and n % CPT == 0 else [])
            if kind == "matrices":
                return units(("answer", n - PIPE)) + ([("error", n - 2, j) for j in range(HALVES)] if n >= 2 else [])
            if kind == "level" and i[2] == 0:
                return [("matrices", n)]
            if kind == "third":
                return units(("eps", n - 2))
            if kind == "kend":
                return units(("matrices", n), ("learn", n - 2))
            if kind == "recall":
                return units(("learn", n - 1), ("answer", n - 1)) + ([("tile", n // UPT - 1, tile_steps[-1])] if n and n % UPT == 0 else [])
            if kind == "query":
                return units(("learn", n - NB), ("answer", n - 1), ("turn", n - 2))
            if kind == "eps":
                return [("recall", n)] + [("third", n, j) for j in range(HALVES)]
            if kind == "learn":
                return [("eps", n), ("kend", n), ("query", n)]
            if kind == "answer":
                return [("eps", n), ("query", n)]
            if kind == "gated":
                return [("answer", n)] + ([("tile", n // UPT - 1, tile_steps[-1])] if n and n % UPT == 0 else [])
            if kind == "out":
                return units(("turn", NB * n + NB - 1))
            if kind != "tile":
                return []
            q, (kind, *i) = i
            before = []
            if kind == "product" and i[1] == 0 and i[0] >= 2:
                before = [("product", i[0] - 2, KT - 1)]
            elif kind == "conv":
                before = [("product", prod_of[i[0]], KT - 1)]
            elif kind == "silu":
                before = [("conv", (GK, 2 * GK, 2 * GK + HEADS, NF)[i[0]] - 1, TAPS - 1)]
            elif kind == "squares":
                before = [("silu", i[0])]
            elif kind == "sums":
                before = [("squares", i[0])]
            elif kind == "keys":
                before = [("sums", 1)] + ([("keys back", i[0] - 1)] if i[0] else [])
            elif kind == "keys back":
                before = [("keys", i[0])]
            elif kind == "gates":
                before = [("gates", 0)] if i[0] else [("product", BA_DONE - 1, KT - 1)]
            elif kind == "values":
                before = [("silu", 2 + i[0])]
            taken = {("product", 0, 0): ("recall", q * UPT - 2), ("product", GK, 0): ("answer", q * UPT - 1), ("product", BA_DONE, 0): ("gated", q * UPT - 1)}
            return [("tile", q, b) for b in before] + ([taken[(kind, *i)]] if q and (kind, *i) in taken else [])

        units = range(UNITS)
        streams = {
            "core": [step for n in units for step in core_steps(n)], "out": [step for n in units for step in out_steps(n)],
            "halves": [[step for n in units for step in invert_steps(n, j)] for j in range(HALVES)],
            "build": [step for n in units for step in build_steps(n)], "tiles": [("tile", q, step) for q in range(BODY_TILES) for step in tile_steps],
        }
        order = scheduled([*streams["halves"], streams["tiles"], streams["build"], streams["core"], streams["out"]], length, needs,
                          loose=("tile", "out", "kend", "recall", "query", "eps", "learn", "answer"))

        with nc.Fori(0, GROUPS) as g:
            load_weights(g)

            with nc.Block() as block:
                @block.sync
                def _(sp):
                    load_tile(sp, 0, 0, 0)

                @block.tensor
                def _(pe):
                    for step in tile_steps:
                        pe_tile(pe, 0, 0, step)

                @block.scalar
                def _(act):
                    for step in tile_steps:
                        act_tile(act, 0, 0, step)

                @block.vector
                def _(dve):
                    for step in tile_steps:
                        dve_tile(dve, 0, 0, step)

                @block.gpsimd
                def _(pool):
                    for step in tile_steps:
                        pool_tile(pool, 0, 0, step)
            next_round()

            with nc.Fori(0, BATCH) as b:
                row = b * T
                with nc.Block() as block:
                    @block.sync
                    def _(sp):
                        def load(q):
                            load_tile(sp, q, (q + 1) % 2, b * PADT + ((q + 1) * TILE if q + 1 < BODY_TILES else PADT))

                        load(0)
                        load(1)
                        for c in range(BODY_CHUNKS):
                            if c:
                                sp.wait_ge(s["yo_sb"], c)
                                store(sp, c - 1, row)
                                sp.wait_ge(s["stored"], 32 * c)
                            for dst, src in ((prow, part_d), (grow, g_d), (xrow, x)):
                                sp.dma_start(dst[:], src[bass.ds(row + c * P, P), :]).then_inc(s["rows_in"], 16)
                            q, r = divmod(c, CPT)
                            if 1 <= q < BODY_TILES - 1 and r == 0:
                                load(q + 1)
                        sp.wait_ge(s["yo_sb"], BODY_CHUNKS)
                        store(sp, BODY_CHUNKS - 1, row)
                        sp.wait_ge(s["stored"], 32 * BODY_CHUNKS)

                    @block.tensor
                    def _(pe):
                        for kind, *i in order:
                            if kind == "tile":
                                pe_tile(pe, i[0], (i[0] + 1) % 2, i[1])
                            elif kind == "gate":
                                pe_gate(pe, *i)
                            elif kind == "scores":
                                pe_scores(pe, *i)
                            elif kind == "decay":
                                pe_decay(pe, *i)
                            elif kind == "level":
                                pe_level(pe, *i)
                            elif kind == "merge":
                                pe_merge(pe, *i)
                            elif kind == "error":
                                pe_error(pe, *i)
                            elif kind == "first":
                                pe_first(pe, *i)
                            elif kind == "second":
                                pe_second(pe, *i)
                            elif kind == "third":
                                pe_third(pe, *i)
                            elif kind == "recall":
                                pe_recall(pe, *i)
                            elif kind == "query":
                                pe_query(pe, *i)
                            elif kind == "eps":
                                pe_eps(pe, *i)
                            elif kind == "learn":
                                pe_learn(pe, *i)
                            elif kind == "answer":
                                pe_answer(pe, *i)
                            elif kind == "turn":
                                pe_turn(pe, *i)
                            elif kind == "out":
                                pe_out(pe, *i)

                    @block.scalar
                    def _(act):
                        for kind, *i in order:
                            if kind == "tile":
                                act_tile(act, i[0], (i[0] + 1) % 2, i[1])
                            elif kind == "gate":
                                act_gate(act, *i)
                            elif kind == "decay":
                                act_decay(act, *i)
                            elif kind == "matrices":
                                act_matrices(act, *i)
                            elif kind == "merge":
                                act_merge(act, *i)
                            elif kind == "error":
                                act_error(act, *i)
                            elif kind == "first":
                                act_first(act, *i)
                            elif kind == "third":
                                act_third(act, *i)
                            elif kind == "query":
                                act_query(act, *i)
                            elif kind == "eps":
                                act_eps(act, *i)
                            elif kind == "norm":
                                act_squares(act, *i)
                            elif kind == "turn":
                                act_turn(act, *i)

                    @block.vector
                    def _(dve):
                        dve.memset(state[:], 0.0).then_inc(s["s_set"], 1)
                        for kind, *i in order:
                            if kind == "tile":
                                dve_tile(dve, i[0], (i[0] + 1) % 2, i[1])
                            elif kind == "gate":
                                dve_gate(dve, *i)
                            elif kind == "scores":
                                dve_scores(dve, *i)
                            elif kind == "matrices":
                                dve_matrices(dve, *i)
                            elif kind == "level":
                                dve_level(dve, *i)
                            elif kind == "error":
                                dve_error(dve, *i)
                            elif kind == "second":
                                dve_second(dve, *i)
                            elif kind == "recall":
                                dve_recall(dve, *i)
                            elif kind == "learn":
                                dve_learn(dve, *i)
                            elif kind == "answer":
                                dve_answer(dve, *i)
                            elif kind == "out":
                                if i[1] == GV - 1:
                                    dve_out(dve, i[0])

                    @block.gpsimd
                    def _(pool):
                        for kind, *i in order:
                            if kind == "tile":
                                pool_tile(pool, i[0], (i[0] + 1) % 2, i[1])
                            elif kind == "decay":
                                pool_decay(pool, *i)
                            elif kind == "matrices":
                                pool_matrices(pool, *i)
                            elif kind == "kend":
                                pool_kend(pool, *i)
                            elif kind == "gated":
                                pool_gate_out(pool, *i)
                            elif kind == "norm":
                                pool_rms(pool, *i)
                            elif kind == "out":
                                if i[1] == GV - 1:
                                    pool_out(pool, i[0])
                next_round()


def program(nc, x, cst, masks, w_qkvz, w_ba, conv_w, dt_bias, a_log, norm_weight, w_out,
            w_router, b_router, norm1_w, wv, bv, wo, norm2_w, w_gate, w_up, w_down, out):
    xt_d = nc.dram_tensor("xt_scratch", (P, KT, BATCH * PADT + WIN), F32, kind="Internal").ap()
    g_d = nc.dram_tensor("g_scratch", (BATCH * T, D), F32, kind="Internal").ap()
    part_d = nc.dram_tensor("part_scratch", (BATCH * T, D), F32, kind="Internal").ap()
    with ExitStack() as ctx:
        bank = [ctx.enter_context(nc.psum_tensor(f"bank{i}", [P, 512], F32)) for i in range(8)]
        feed_forward(nc, bank, x, cst, w_router, b_router, norm1_w, wv, bv, wo, norm2_w, w_gate, w_up, w_down, xt_d, g_d, part_d)
        attention(nc, bank, x, cst, masks, w_qkvz, w_ba, conv_w, dt_bias, a_log, norm_weight, w_out, xt_d, g_d, part_d, out)


_INS = ["w_qkvz", "w_ba", "conv_w", "dt_bias", "A_log", "norm_weight", "w_out"]
_FFN = ["w_router", "b_router", "norm1_w", "wv", "bv", "wo", "norm2_w", "w_gate", "w_up", "w_down"]


def kernel(**inputs):
    import concourse.bacc as bacc
    from concourse.bass_utils import run_bass_kernel_spmd

    nc = bacc.Bacc("TRN2", target_bir_lowering=False, num_devices=1)
    arrays, args = {}, []

    def give(name, a):
        a = np.ascontiguousarray(a)
        arrays[name] = a
        args.append(nc.dram_tensor(name, a.shape, mybir.dt.from_np(a.dtype), kind="ExternalInput").ap())

    give("x", np.asarray(inputs["L0_attn_hidden_states"]).reshape(BATCH * T, D))
    for name, a in zip(("cst", "masks"), constants()):
        give(name, a)
    for name in _INS:
        give(name, np.asarray(inputs["L0_attn_" + name]))
    for name in _FFN:
        a = np.asarray(inputs["L0_ffn_" + name])
        if name == "b_router":
            a = a.reshape(1)
        elif name in ("norm1_w", "norm2_w", "bv"):
            a = a.reshape(KT, P).T
        give(name, a)
    args.append(nc.dram_tensor("out", (BATCH * T, D), F32, kind="ExternalOutput").ap())
    program(nc, *args)
    r = run_bass_kernel_spmd(nc, [arrays], core_ids=[0])
    return r.results[0]["out"].reshape(BATCH, T, D)
```
